# Optimizing a Trainium2 kernel written in Bass

```python
import numpy as np
import jax
import jax.numpy as jnp

def _softmax(x, axis=-1):
    return jax.nn.softmax(x, axis=axis)

def _gelu(x):
    return jax.nn.gelu(x, approximate=True)

def _silu(x):
    return jax.nn.silu(x)

def _sigmoid(x):
    return jax.nn.sigmoid(x)

def _layernorm(x, axis=-1, eps=1e-05):
    m = jnp.mean(x, axis=axis, keepdims=True)
    v = jnp.var(x, axis=axis, keepdims=True)
    return (x - m) / jnp.sqrt(v + eps)

def _scatter_add(tgt, idx, src, axis=0):
    return tgt.at[idx].add(src)

def _segment_sum(src, seg, n):
    return jax.ops.segment_sum(src, seg, n)
kernel_name = 'mk_decoder_preln_d1_seqx_r8_2789e7'

def setup_inputs(seed: int=0):
    np.random.seed(seed)
    _w = jnp.asarray

    def _rec_inputs():
        import jax
        import jax.numpy as jnp
        _rk = jax.random.key(seed)
        x = -0.0002928 + 1 * jax.random.normal(jax.random.fold_in(_rk, 1), (32, 56, 128), jnp.float32)
        _lenS = 56 - jax.random.randint(jax.random.fold_in(_rk, 7), (32,), 0, max(1, 56 // 4) + 1, jnp.int32)
        _lenS2 = 1500 - jax.random.randint(jax.random.fold_in(_rk, 8), (32,), 0, max(1, 1500 // 4) + 1, jnp.int32)
        _ctx_1024P = jax.random.normal(jax.random.fold_in(_rk, 11), (32, 16, 128), jnp.float32)
        _ctx_1024c = jax.random.dirichlet(jax.random.fold_in(_rk, 511), 0.3 * jnp.ones((16,), jnp.float32), (32, 1500))
        _ctx_1024t = jnp.einsum('bsk,bkd->bsd', _ctx_1024c, _ctx_1024P)
        _ctx_1024t = _ctx_1024t * jax.lax.rsqrt(jnp.mean(jnp.square(_ctx_1024t)) + 1e-12) * 0.953939
        ctx_1024 = -1.39393e-06 + 0.999914 * (_ctx_1024t + 0.3 * jax.random.normal(jax.random.fold_in(_rk, 611), (32, 1500, 128), jnp.float32))
        return (x, ctx_1024)
    x, ctx_1024 = _rec_inputs()

    def _L0_attn_setup():
        import jax, jax.numpy as jnp
        import numpy as np
        import math
        NUM_HEADS = 16
        D_MODEL = 128
        B, T = (1, 512)
        key = jax.random.key(seed)
        kx, kq, kk, kv, ko = jax.random.split(key, 5)
        s = 1.0 / math.sqrt(D_MODEL)
        return {'x': jax.random.normal(kx, (B, T, D_MODEL), dtype=jnp.float32), 'Wq': jax.random.normal(kq, (D_MODEL, D_MODEL), dtype=jnp.float32) * s, 'Wk': jax.random.normal(kk, (D_MODEL, D_MODEL), dtype=jnp.float32) * s, 'Wv': jax.random.normal(kv, (D_MODEL, D_MODEL), dtype=jnp.float32) * s, 'Wo': jax.random.normal(ko, (D_MODEL, D_MODEL), dtype=jnp.float32) * s}
    _L0_attn_all = _L0_attn_setup()
    _L0_attn_in = {k: v for k, v in _L0_attn_all.items() if k in ('Wq', 'Wk', 'Wv', 'Wo')}
    del _L0_attn_all

    def _L0_xattn_setup():
        import jax, jax.numpy as jnp
        import numpy as np
        EMBED_DIM = 128
        NUM_HEADS = 16
        HEAD_DIM = EMBED_DIM // NUM_HEADS
        SCALE_BASE = EMBED_DIM

        def _xpos_tables(length, offset):
            base = (jnp.arange(0, HEAD_DIM, 2, dtype=jnp.float32) + 0.4 * HEAD_DIM) / (1.4 * HEAD_DIM)
            min_pos = -(length + offset) // 2
            max_pos = length + offset + min_pos
            power = jnp.arange(min_pos, max_pos, dtype=jnp.float32) / SCALE_BASE
            scale = base[None, :] ** power[:, None]
            dim = HEAD_DIM // 2
            inv_freq = 1.0 / 10000.0 ** (jnp.arange(dim, dtype=jnp.float32) / dim)
            pos = jnp.arange(scale.shape[0], dtype=jnp.float32)
            ang = pos[:, None] * inv_freq[None, :]
            sin, cos = (jnp.sin(ang), jnp.cos(ang))
            if scale.shape[0] > length:
                scale, sin, cos = (scale[-length:], sin[-length:], cos[-length:])
            return (sin, cos, scale)

        def _rotate_every_two(x):
            x1, x2 = (x[..., ::2], x[..., 1::2])
            return jnp.stack((-x2, x1), axis=-1).reshape(x.shape)

        def _apply_xpos(x, offset, downscale):
            L = x.shape[2]
            sin, cos, scale = _xpos_tables(L, offset)
            if downscale:
                scale = 1.0 / scale
            sin_s = jnp.repeat(sin * scale, 2, axis=-1)
            cos_s = jnp.repeat(cos * scale, 2, axis=-1)
            return x * cos_s + _rotate_every_two(x) * sin_s
        key = jax.random.key(seed)
        ks = jax.random.split(key, 11)
        B, T, E = (2, 256, EMBED_DIM)
        s = 1.0 / np.sqrt(E)
        inp = {'query': jax.random.normal(ks[0], (B, T, E), jnp.float32), 'key': jax.random.normal(ks[1], (B, T, E), jnp.float32), 'value': jax.random.normal(ks[2], (B, T, E), jnp.float32), 'wq': jax.random.uniform(ks[3], (E, E), jnp.float32, -s, s), 'bq': jax.random.uniform(ks[4], (E,), jnp.float32, -s, s), 'wk': jax.random.uniform(ks[5], (E, E), jnp.float32, -s, s), 'bk': jax.random.uniform(ks[6], (E,), jnp.float32, -s, s), 'wv': jax.random.uniform(ks[7], (E, E), jnp.float32, -s, s), 'bv': jax.random.uniform(ks[8], (E,), jnp.float32, -s, s), 'wo': jax.random.uniform(ks[9], (E, E), jnp.float32, -s, s), 'bo': jax.random.uniform(ks[10], (E,), jnp.float32, -s, s)}
        return inp
    _L0_xattn_all = _L0_xattn_setup()
    _L0_xattn_in = {k: v for k, v in _L0_xattn_all.items() if k in ('wq', 'bq', 'wk', 'bk', 'wv', 'bv', 'wo', 'bo')}
    del _L0_xattn_all

    def _L0_ffn_setup():
        import math
        import jax, jax.numpy as jnp
        import numpy as np
        D_MODEL = 128
        D_HIDDEN = 256
        N_EXPERTS = 8
        TOP_K = 2
        CAPACITY_FACTOR = 1.25

        def _moe_forward(x, w_router, w_gate, w_down):
            B, T, D = x.shape
            N = B * T
            xf = x.reshape(N, D)
            logits = xf.astype(jnp.float32) @ w_router.T
            gates = jax.nn.softmax(logits, axis=-1)
            topk_gates, topk_idx = jax.lax.top_k(gates, TOP_K)
            expert_mask = jax.nn.one_hot(topk_idx, N_EXPERTS, dtype=jnp.int32).sum(axis=1)
            capacity = math.ceil(N / N_EXPERTS * CAPACITY_FACTOR)
            position_in_expert = jnp.cumsum(expert_mask, axis=0) - 1
            expert_mask = expert_mask * (position_in_expert < capacity)
            keep = jnp.take_along_axis(expert_mask, topk_idx, axis=1) > 0
            topk_gates = topk_gates * keep
            topk_gates = topk_gates / (topk_gates.sum(axis=-1, keepdims=True) + 1e-06)
            hidden = jax.nn.silu(xf @ w_gate.T)
            combine = (topk_gates[:, :, None] * jax.nn.one_hot(topk_idx, N_EXPERTS, dtype=topk_gates.dtype)).sum(axis=1)
            y = jnp.zeros((N, D), dtype=x.dtype)
            for e in range(N_EXPERTS):
                y = y + combine[:, e:e + 1] * (hidden @ w_down[e].T)
            return y.reshape(B, T, D)
        key = jax.random.key(seed)
        k0, k1, k2, k3 = jax.random.split(key, 4)
        B, T = (2, 256)
        x = jax.random.normal(k0, (B, T, D_MODEL), dtype=jnp.float32)
        w_router = jax.random.normal(k1, (N_EXPERTS, D_MODEL), dtype=jnp.float32) * 0.02
        w_gate = jax.random.normal(k2, (D_HIDDEN, D_MODEL), dtype=jnp.float32) * 0.02
        w_down = jax.random.normal(k3, (N_EXPERTS, D_MODEL, D_HIDDEN), dtype=jnp.float32) * 0.02
        return {'x': x, 'w_router': w_router, 'w_gate': w_gate, 'w_down': w_down}
    _L0_ffn_all = _L0_ffn_setup()
    _L0_ffn_in = {k: v for k, v in _L0_ffn_all.items() if k in ('w_router', 'w_gate', 'w_down')}
    del _L0_ffn_all
    return {'x': x, 'ctx_1024': ctx_1024, 'L0_attn_Wq': _L0_attn_in['Wq'], 'L0_attn_Wk': _L0_attn_in['Wk'], 'L0_attn_Wv': _L0_attn_in['Wv'], 'L0_attn_Wo': _L0_attn_in['Wo'], 'L0_xattn_wq': _L0_xattn_in['wq'], 'L0_xattn_bq': _L0_xattn_in['bq'], 'L0_xattn_wk': _L0_xattn_in['wk'], 'L0_xattn_bk': _L0_xattn_in['bk'], 'L0_xattn_wv': _L0_xattn_in['wv'], 'L0_xattn_bv': _L0_xattn_in['bv'], 'L0_xattn_wo': _L0_xattn_in['wo'], 'L0_xattn_bo': _L0_xattn_in['bo'], 'L0_ffn_w_router': _L0_ffn_in['w_router'], 'L0_ffn_w_gate': _L0_ffn_in['w_gate'], 'L0_ffn_w_down': _L0_ffn_in['w_down']}

def reference(x, ctx_1024, L0_attn_Wq, L0_attn_Wk, L0_attn_Wv, L0_attn_Wo, L0_xattn_wq, L0_xattn_bq, L0_xattn_wk, L0_xattn_bk, L0_xattn_wv, L0_xattn_bv, L0_xattn_wo, L0_xattn_bo, L0_ffn_w_router, L0_ffn_w_gate, L0_ffn_w_down):
    import jax
    import jax.numpy as jnp

    def _L0_attn_ref(x, Wq, Wk, Wv, Wo):
        import jax, jax.numpy as jnp
        import numpy as np
        import math
        NUM_HEADS = 16
        D_MODEL = 128
        B, T = (1, 512)
        Bx, Tx, D = x.shape
        H = NUM_HEADS
        dk = D // H
        q = (x @ Wq.T).reshape(Bx, Tx, H, dk)
        k = (x @ Wk.T).reshape(Bx, Tx, H, dk)
        v = (x @ Wv.T).reshape(Bx, Tx, H, dk)
        scores = jnp.einsum('bthd,bshd->bhts', q, k) / math.sqrt(dk)
        causal_mask = jnp.triu(jnp.ones((Tx, Tx), dtype=bool), k=1)
        scores = jnp.where(causal_mask, jnp.float32(-jnp.inf), scores).astype(jnp.float32)
        attn = jax.nn.softmax(scores, axis=-1)
        out = jnp.einsum('bhts,bshd->bthd', attn, v).reshape(Bx, Tx, D)
        return out @ Wo.T

    def _L0_xattn_ref(query, key, value, wq, bq, wk, bk, wv, bv, wo, bo):
        import jax, jax.numpy as jnp
        import numpy as np
        EMBED_DIM = 128
        NUM_HEADS = 16
        HEAD_DIM = EMBED_DIM // NUM_HEADS
        SCALE_BASE = EMBED_DIM

        def _xpos_tables(length, offset):
            base = (jnp.arange(0, HEAD_DIM, 2, dtype=jnp.float32) + 0.4 * HEAD_DIM) / (1.4 * HEAD_DIM)
            min_pos = -(length + offset) // 2
            max_pos = length + offset + min_pos
            power = jnp.arange(min_pos, max_pos, dtype=jnp.float32) / SCALE_BASE
            scale = base[None, :] ** power[:, None]
            dim = HEAD_DIM // 2
            inv_freq = 1.0 / 10000.0 ** (jnp.arange(dim, dtype=jnp.float32) / dim)
            pos = jnp.arange(scale.shape[0], dtype=jnp.float32)
            ang = pos[:, None] * inv_freq[None, :]
            sin, cos = (jnp.sin(ang), jnp.cos(ang))
            if scale.shape[0] > length:
                scale, sin, cos = (scale[-length:], sin[-length:], cos[-length:])
            return (sin, cos, scale)

        def _rotate_every_two(x):
            x1, x2 = (x[..., ::2], x[..., 1::2])
            return jnp.stack((-x2, x1), axis=-1).reshape(x.shape)

        def _apply_xpos(x, offset, downscale):
            L = x.shape[2]
            sin, cos, scale = _xpos_tables(L, offset)
            if downscale:
                scale = 1.0 / scale
            sin_s = jnp.repeat(sin * scale, 2, axis=-1)
            cos_s = jnp.repeat(cos * scale, 2, axis=-1)
            return x * cos_s + _rotate_every_two(x) * sin_s
        B, T, E = query.shape
        S = key.shape[1]
        scaling = HEAD_DIM ** (-0.5)

        def split_heads(x):
            return x.reshape(B, -1, NUM_HEADS, HEAD_DIM).transpose(0, 2, 1, 3)
        q = split_heads((query @ wq.T + bq) * scaling)
        k = split_heads(key @ wk.T + bk)
        v = split_heads(value @ wv.T + bv)
        k = _apply_xpos(k, 0, downscale=True)
        q = _apply_xpos(q, 0, downscale=False)
        scores = jnp.einsum('bhtd,bhsd->bhts', q, k)
        attn = jax.nn.softmax(scores.astype(jnp.float32), axis=-1).astype(scores.dtype)
        out = jnp.einsum('bhts,bhsd->bhtd', attn, v)
        out = out.transpose(0, 2, 1, 3).reshape(B, T, E)
        return out @ wo.T + bo

    def _L0_ffn_ref(x, w_router, w_gate, w_down):
        import math
        import jax, jax.numpy as jnp
        import numpy as np
        D_MODEL = 128
        D_HIDDEN = 256
        N_EXPERTS = 8
        TOP_K = 2
        CAPACITY_FACTOR = 1.25

        def _moe_forward(x, w_router, w_gate, w_down):
            B, T, D = x.shape
            N = B * T
            xf = x.reshape(N, D)
            logits = xf.astype(jnp.float32) @ w_router.T
            gates = jax.nn.softmax(logits, axis=-1)
            topk_gates, topk_idx = jax.lax.top_k(gates, TOP_K)
            expert_mask = jax.nn.one_hot(topk_idx, N_EXPERTS, dtype=jnp.int32).sum(axis=1)
            capacity = math.ceil(N / N_EXPERTS * CAPACITY_FACTOR)
            position_in_expert = jnp.cumsum(expert_mask, axis=0) - 1
            expert_mask = expert_mask * (position_in_expert < capacity)
            keep = jnp.take_along_axis(expert_mask, topk_idx, axis=1) > 0
            topk_gates = topk_gates * keep
            topk_gates = topk_gates / (topk_gates.sum(axis=-1, keepdims=True) + 1e-06)
            hidden = jax.nn.silu(xf @ w_gate.T)
            combine = (topk_gates[:, :, None] * jax.nn.one_hot(topk_idx, N_EXPERTS, dtype=topk_gates.dtype)).sum(axis=1)
            y = jnp.zeros((N, D), dtype=x.dtype)
            for e in range(N_EXPERTS):
                y = y + combine[:, e:e + 1] * (hidden @ w_down[e].T)
            return y.reshape(B, T, D)
        return _moe_forward(x, w_router, w_gate, w_down)
    x = x + _L0_attn_ref(_layernorm(x, axis=-1), L0_attn_Wq, L0_attn_Wk, L0_attn_Wv, L0_attn_Wo)
    x = x + _L0_xattn_ref(_layernorm(x, axis=-1), ctx_1024, ctx_1024, L0_xattn_wq, L0_xattn_bq, L0_xattn_wk, L0_xattn_bk, L0_xattn_wv, L0_xattn_bv, L0_xattn_wo, L0_xattn_bo)
    x = x + _L0_ffn_ref(_layernorm(x, axis=-1), L0_ffn_w_router, L0_ffn_w_gate, L0_ffn_w_down)
    return x

_drawn_inputs = setup_inputs


def setup_inputs(seed=0):
    import zlib

    import numpy as np

    out = dict(_drawn_inputs(seed))
    spreads = {}
    factors = {'L0_ffn_w_router': 3.177, 'L0_ffn_w_gate': 2.813, 'L0_ffn_w_down': 2.798}
    for name, (base, spread) in spreads.items():
        noise = np.random.default_rng([zlib.crc32(name.encode()), seed]).standard_normal(out[name].shape)
        drawn = base * np.exp(spread * noise) if base else spread * noise
        out[name] = jnp.asarray(drawn.astype(out[name].dtype))
    for name, factor in factors.items():
        out[name] = (out[name] * factor).astype(out[name].dtype)
    return out
```

```python
from contextlib import ExitStack

import concourse.bass as bass
from concourse import mybir

F32 = mybir.dt.float32
F32R = mybir.dt.float32r
U32 = mybir.dt.uint32
ALU = mybir.AluOpType
ACT = mybir.ActivationFunctionType
AX = mybir.AxisListType

B, T, D, H, S = 32, 56, 128, 16, 1500
DH = D // H
NT = B // 2
HALF = 64
HT = H * T
KT, NK = 125, 12
NE, FH = 8, 256
CAPACITY = -(-B * T * 5 // (NE * 4))
KC, NKC = 500, 3
NG = HT // 128
HG = 4
VW = DH + 1
EPS = 1e-5

PACK = [("ident", 128), ("causal", T), ("mask_nat", H), ("mask_split", H), ("mask_stack", HG), ("mask_m", NG),
        ("tri", 128), ("valid", 1), ("iota", NE), ("cosq", T), ("sinq", T),
        ("Wq", D), ("Wk", D), ("Wv", D), ("Wo", D), ("xwq", D), ("xwk", D), ("xwv", D), ("xwo", D),
        ("bq", 1), ("bk", 1), ("bv", 1), ("bo", D), ("wr", NE), ("wg", FH)]
PACK_AT = {}
PACK_N = 0
for _name, _width in PACK:
    PACK_AT[_name] = (PACK_N, PACK_N + _width)
    PACK_N += _width


def wait(eng, sem, value):
    if isinstance(value, int) and value <= 0:
        return
    eng.wait_ge(sem, value)


def mid(ap, n):
    return ap.unsqueeze(1).broadcast_to([ap.shape[0], n, ap.shape[1]])


def last(ap, n):
    return ap.unsqueeze(len(ap.shape)).broadcast_to([*ap.shape, n])


def layer_norm(nc, dve, x, work, stats, s, base):
    n = [base]

    def step(ins):
        n[0] += 1
        ins.then_inc(s["ln"], 1)
        dve.wait_ge(s["ln"], n[0])

    step(nc.vector.tensor_reduce(stats[:, 0, :], x, AX.X, ALU.add))
    step(nc.vector.tensor_scalar(stats[:, 1, :], stats[:, 0, :], -1.0 / D, None, ALU.mult))
    step(nc.vector.tensor_tensor(work, x, last(stats[:, 1, :], D), ALU.add))
    return n, step


def build_self_attention(nc, x_dram, pack, xres, qh, q3, fresh):
    with ExitStack() as ctx:
        sb = lambda name, shape, dt=F32: ctx.enter_context(nc.sbuf_tensor(name, shape, dt))
        sem = lambda name: ctx.enter_context(nc.semaphore("a_" + name))
        bank = [ctx.enter_context(nc.psum_tensor(f"a_bank{i}", [128, 512], F32)) for i in range(8)]
        w = lambda name: pack[:, PACK_AT[name][0]:PACK_AT[name][1]]
        ident = w("ident")

        xc = sb("a_xc", [128, NT, D])
        sq = sb("a_sq", [128, NT, D])
        stats = sb("a_stats", [128, 6, NT])
        ytile = sb("a_ytile", [128, 2, D])
        yT = sb("a_yT", [128, 2, 128])
        prj = sb("a_prj", [128, 2, 256])
        vblk = sb("a_vblk", [128, 2, 2, H // 2, 2, DH])
        kblk = sb("a_kblk", [128, 2, 2, H, T])
        att = sb("a_att", [128, 2, H, HALF])
        small = sb("a_small", [128, 4, H])
        pT = sb("a_pT", [128, H // 2, 128])
        on = sb("a_on", [128, D])
        oT = sb("a_oT", [128, 128])
        y2T = sb("a_y2T", [128, NT, 128])
        qa = sb("a_qa", [128, B, T])
        qb = sb("a_qb", [128, B, T])
        ql = sb("a_ql", [128, B, T])

        names = ("x_in pads ln var_ready std_ready rstd ytile_ready yT_mm yT_copied prj_mm prj_copied kblk_ready s_mm "
                 "masked max_ready shifted exp_done pT_mm pT_copied pv_mm den_ready inv_ready on_ready oT_mm oT_copied "
                 "out_mm x_added y2_ready y2T_mm y2T_copied q_mm q_biased q_rot q_sum q_high q_low q3_in").split()
        s = {name: sem(name) for name in names}
        s["pack_in"] = fresh["pack_in"]
        block = ctx.enter_context(nc.Block())

        def periods(eng, period):
            for p in range(-2, 2):
                period(p, p % 2)
            with eng.Fori(1, NT // 2 - 1) as it:
                for u in range(2):
                    period(2 * it + u, u)
            for p in range(NT - 2, NT):
                period(p, p % 2)

        def has(p):
            return not isinstance(p, int) or 0 <= p < NT

        @block.sync
        def _(sp):
            xv = x_dram.rearrange("(i two) t d -> two t i d", two=2)
            sp.wait_ge(s["pads"], 1)
            sp.dma_start(xres[0:T, :, :], xv[0]).then_inc(s["x_in"], 16)
            sp.dma_start(xres[HALF:HALF + T, :, :], xv[1]).then_inc(s["x_in"], 16)
            sp.wait_ge(s["q_high"], 1)
            for half in range(2):
                for g in range(4):
                    src = slice(64 * half + 16 * g, 64 * half + 16 * g + 16)
                    for quad in range(2):
                        dst = slice(32 * quad + 16 * half, 32 * quad + 16 * half + 16)
                        sp.dma_start(q3[dst, g, :, :], qh[src, :, :]).then_inc(s["q3_in"], 16)
            sp.wait_ge(s["q_low"], 1)
            for half in range(2):
                for g in range(4):
                    src = slice(64 * half + 16 * g, 64 * half + 16 * g + 16)
                    dst = slice(64 + 16 * half, 80 + 16 * half)
                    sp.dma_start(q3[dst, g, :, :], ql[src, :, :]).then_inc(s["q3_in"], 16)
            sp.wait_ge(s["q3_in"], 16 * 24)

        @block.gpsimd
        def _(pool):
            pool.wait_ge(s["pack_in"], 16)

            def period(p, u):
                q, b = p + 2, u % 2
                if has(q):
                    pool.wait_ge(s["prj_copied"], 3 * q + 1)
                    wait(pool, s["s_mm"], q - 1)
                    for a in range(2):
                        kT = prj[:, u, 128 + HALF * a:128 + HALF * a + T]
                        nc.gpsimd.tensor_tensor(kblk[:, b, a, :, :], mid(kT, H), last(w("mask_nat"), T),
                                                ALU.mult).then_inc(s["kblk_ready"], 1)

            periods(pool, period)

        @block.scalar
        def _(act):
            act.wait_ge(s["var_ready"], 1)
            nc.scalar.activation(stats[:, 3, :], stats[:, 2, :], ACT.Sqrt).then_inc(s["std_ready"], 1)

            def period(p, u):
                q, r = p + 2, p + 1
                if has(p):
                    act.wait_ge(s["pT_mm"], p + 1)
                    wait(act, s["pv_mm"], p)
                    for c in range(2):
                        ins = nc.scalar.activation(pT[:, 4 * c:4 * c + 4, :].rearrange("p h t -> p (h t)"),
                                                   bank[4 + c][:, :], ACT.Copy)
                    ins.then_inc(s["pT_copied"], 1)
                if has(q):
                    act.wait_ge(s["yT_mm"], q + 1)
                    wait(act, s["prj_mm"], q - 1)
                    nc.scalar.activation(yT[:, u % 2, :], bank[0][:, 0:128], ACT.Copy).then_inc(s["yT_copied"], 1)
                    act.wait_ge(s["prj_mm"], q + 1)
                    nc.scalar.activation(prj[:, u, :], bank[1][:, 0:256], ACT.Copy).then_inc(s["prj_copied"], 1)
                if has(r):
                    act.wait_ge(s["shifted"], r + 1)
                    a = att[:, (u + 1) % 2, :, 0:T]
                    nc.scalar.activation(a, a, ACT.Exp, scale=float(DH) ** -0.5).then_inc(s["exp_done"], 1)
                if has(p):
                    act.wait_ge(s["oT_mm"], p + 1)
                    wait(act, s["out_mm"], p)
                    nc.scalar.activation(oT[:, :], bank[6][:, 128:256], ACT.Copy).then_inc(s["oT_copied"], 1)
                if has(q):
                    wait(act, s["pv_mm"], q - 1)
                    for odd in range(2):
                        rows = slice(HALF * odd, HALF * odd + T)
                        nc.scalar.activation(
                            vblk[rows, u, :, :, odd, :].rearrange("p a j d -> p (a j) d"),
                            bank[1][rows, 256:512].rearrange("p (aj two d) -> p aj two d", two=2, d=DH)[:, :, odd, :],
                            ACT.Copy).then_inc(s["prj_copied"], 1)

            periods(act, period)
            act.wait_ge(s["var_ready"], 2)
            nc.scalar.activation(stats[:, 3, :], stats[:, 2, :], ACT.Sqrt).then_inc(s["std_ready"], 1)
            for c in range(4):
                act.wait_ge(s["y2T_mm"], c + 1)
                nc.scalar.activation(y2T[:, 4 * c:4 * c + 4, :].rearrange("p i t -> p (i t)"), bank[c][:, :],
                                     ACT.Copy).then_inc(s["y2T_copied"], 1)
            for c in range(4):
                act.wait_ge(s["q_mm"], c + 1)
                nc.scalar.activation(qa[:, 8 * c:8 * c + 8, :],
                                     bank[4 + c][:, :].rearrange("p (b t) -> p b t", t=HALF)[:, :, 0:T],
                                     ACT.Identity, bias=w("bq")).then_inc(s["q_biased"], 1)
            act.wait_ge(s["q_sum"], 1)
            nc.scalar.activation(qh[:, :, :].bitcast(F32R), qb[:, :, :], ACT.Copy).then_inc(s["q_high"], 1)

        @block.tensor
        def _(pe):
            pe.wait_ge(s["pack_in"], 16)

            def period(p, u):
                q, r, b = p + 2, p + 1, u % 2
                if has(p):
                    pe.wait_ge(s["exp_done"], p + 1)

                if has(p):
                    wait(pe, s["pT_copied"], p)
                    for h in range(H // 2):
                        ins = nc.tensor.transpose(bank[4 + h // 4][:, 128 * (h % 4):128 * (h % 4) + 128],
                                                  att[:, b, 2 * h:2 * h + 2, :].rearrange("p h t -> p (h t)"), ident)
                    ins.then_inc(s["pT_mm"], 1)
                if has(q):
                    pe.wait_ge(s["ytile_ready"], q + 1)
                    wait(pe, s["yT_copied"], q)
                    nc.tensor.transpose(bank[0][:, 0:128], ytile[:, b, :], ident).then_inc(s["yT_mm"], 1)
                if has(r):
                    pe.wait_ge(s["kblk_ready"], 2 * (r + 1))
                    wait(pe, s["masked"], r)
                    for hh in range(2):
                        for a in range(2):
                            ins = nc.tensor.matmul(
                                bank[2 + hh][HALF * a:HALF * a + T, 0:HT // 2],
                                prj[:, 1 - u, HALF * a:HALF * a + T],
                                kblk[:, (u + 1) % 2, a, 8 * hh:8 * hh + 8, :].rearrange("p h t -> p (h t)"),
                                start=True, stop=True)
                    ins.then_inc(s["s_mm"], 1)
                if has(q):
                    pe.wait_ge(s["yT_copied"], q + 1)
                    wait(pe, s["prj_copied"], 3 * q)
                    nc.tensor.matmul(bank[1][:, 0:128], w("Wq"), yT[:, b, :], start=True, stop=True)
                    nc.tensor.matmul(bank[1][:, 128:256], w("Wk"), yT[:, b, :], start=True, stop=True)
                    for a in range(2):
                        for half in (0, HALF):
                            ins = nc.tensor.matmul(bank[1][half:half + T, 256 + 128 * a:384 + 128 * a],
                                                   yT[:, b, HALF * a:HALF * a + T], w("Wv"), start=True, stop=True)
                    ins.then_inc(s["prj_mm"], 1)
                if has(p):
                    pe.wait_ge(s["pT_copied"], p + 1)
                    pe.wait_ge(s["prj_copied"], 3 * (p + 1))
                    wait(pe, s["oT_copied"], p)
                    for a in range(2):
                        for j in range(H // 2):
                            ins = nc.tensor.matmul(bank[6][HALF * a:HALF * a + T, 2 * DH * j:2 * DH * (j + 1)],
                                                   pT[:, j, HALF * a:HALF * a + T],
                                                   vblk[:, u, a, j, :, :].rearrange("p o d -> p (o d)"),
                                                   start=True, stop=True)
                    ins.then_inc(s["pv_mm"], 1)
                    pe.wait_ge(s["on_ready"], p + 1)
                    nc.tensor.transpose(bank[6][:, 128:256], on[:, :], ident).then_inc(s["oT_mm"], 1)
                    pe.wait_ge(s["oT_copied"], p + 1)
                    wait(pe, s["x_added"], p)
                    nc.tensor.matmul(bank[7][:, 0:128], oT[:, :], w("Wo"), start=True, stop=True)\
                        .then_inc(s["out_mm"], 1)

            pe.wait_ge(s["pads"], 2)
            periods(pe, period)
            pe.wait_ge(s["y2_ready"], 1)
            for c in range(4):
                for j in range(4):
                    ins = nc.tensor.transpose(bank[c][:, 128 * j:128 * j + 128], xc[:, 4 * c + j, :], ident)
                ins.then_inc(s["y2T_mm"], 1)
            for c in range(4):
                pe.wait_ge(s["y2T_copied"], c + 1)
                nc.tensor.matmul(bank[4 + c][:, :], w("xwq"),
                                 y2T[:, 4 * c:4 * c + 4, :].rearrange("p i t -> p (i t)"),
                                 start=True, stop=True).then_inc(s["q_mm"], 1)

        @block.vector
        def _(dve):
            nc.vector.memset(xres[:, :, :], 0.0).then_inc(s["pads"], 1)
            nc.vector.memset(att[:, :, :, :], 0.0)
            nc.vector.memset(vblk[:, :, :, :, :, :], 0.0)
            for i in range(8):
                ins = nc.vector.memset(bank[i][:, :], 0.0)
            ins.then_inc(s["pads"], 1)
            dve.wait_ge(s["x_in"], 32)

            def norm(base, second):
                n, step = layer_norm(nc, dve, xres[:, :, :], xc[:, :, :], stats, s, base)
                step(nc.vector.tensor_tensor(sq[:, :, :], xc[:, :, :], xc[:, :, :], ALU.mult))
                step(nc.vector.tensor_reduce(stats[:, 4, :], sq[:, :, :], AX.X, ALU.add))
                nc.vector.tensor_scalar(stats[:, 2, :], stats[:, 4, :], 1.0 / D, EPS, ALU.mult, ALU.add)\
                    .then_inc(s["var_ready"], 1)
                dve.wait_ge(s["std_ready"], 2 if second else 1)
                nc.vector.reciprocal(stats[:, 5, :], stats[:, 3, :]).then_inc(s["rstd"], 1)
                dve.wait_ge(s["rstd"], 2 if second else 1)
                return n[0]

            done = norm(0, False)
            dve.wait_ge(s["pack_in"], 16)

            def period(p, u):
                q, r, b = p + 2, p + 1, u % 2
                if has(q):
                    wait(dve, s["yT_mm"], q - 1)
                    at = bass.ds(q, 1) if not isinstance(q, int) else slice(q, q + 1)
                    nc.vector.tensor_tensor(ytile[:, b, :].unsqueeze(1), xc[:, at, :],
                                            last(stats[:, 5, at], D), ALU.mult).then_inc(s["ytile_ready"], 1)
                if has(p):
                    dve.wait_ge(s["exp_done"], p + 1)
                    nc.vector.tensor_reduce(small[:, 2, :], att[:, b, :, 0:T], AX.X, ALU.add).then_inc(s["den_ready"], 1)
                    dve.wait_ge(s["den_ready"], p + 1)
                    nc.vector.reciprocal(small[:, 3, :], small[:, 2, :]).then_inc(s["inv_ready"], 1)
                if has(r):
                    dve.wait_ge(s["s_mm"], r + 1)
                    wait(dve, s["pT_mm"], r - 1)
                    a = att[:, (u + 1) % 2, :, 0:T]
                    for hh in range(2):
                        ins = nc.vector.tensor_tensor(
                            a[:, 8 * hh:8 * hh + 8, :], bank[2 + hh][:, 0:HT // 2].rearrange("p (h t) -> p h t", t=T),
                            mid(w("causal"), 8), ALU.add)
                    ins.then_inc(s["masked"], 1)
                    dve.wait_ge(s["masked"], r + 1)
                    nc.vector.tensor_reduce(small[:, 0, :], a, AX.X, ALU.max).then_inc(s["max_ready"], 1)
                    dve.wait_ge(s["max_ready"], r + 1)
                    nc.vector.tensor_tensor(a, a, last(small[:, 0, :], T), ALU.subtract).then_inc(s["shifted"], 1)
                if has(p):
                    dve.wait_ge(s["pv_mm"], p + 1)
                    dve.wait_ge(s["inv_ready"], p + 1)
                    wait(dve, s["oT_mm"], p)
                    nc.vector.tensor_tensor(on[:, :].rearrange("p (h d) -> p h d", d=DH),
                                            bank[6][:, 0:128].rearrange("p (h d) -> p h d", d=DH),
                                            last(small[:, 3, :], DH), ALU.mult).then_inc(s["on_ready"], 1)
                    dve.wait_ge(s["out_mm"], p + 1)
                    at = bass.ds(p, 1) if not isinstance(p, int) else slice(p, p + 1)
                    nc.vector.tensor_tensor(xres[:, at, :], xres[:, at, :], bank[7][:, 0:128].unsqueeze(1),
                                            ALU.add).then_inc(s["x_added"], 1)

            periods(dve, period)
            dve.wait_ge(s["x_added"], NT)
            norm(done, True)
            nc.vector.tensor_tensor(xc[:, :, :], xc[:, :, :], last(stats[:, 5, :], D), ALU.mult)\
                .then_inc(s["y2_ready"], 1)
            dve.wait_ge(s["q_biased"], 4)
            sinq, lo, hi = w("sinq"), slice(0, 64), slice(64, 128)
            nc.vector.tensor_tensor(ql[lo, :, :], qa[hi, :, :], mid(sinq[hi], B), ALU.mult)
            nc.vector.tensor_tensor(ql[hi, :, :], qa[lo, :, :], mid(sinq[lo], B), ALU.mult)
            nc.vector.tensor_tensor(qb[:, :, :], qa[:, :, :], mid(w("cosq"), B), ALU.mult).then_inc(s["q_rot"], 1)
            dve.wait_ge(s["q_rot"], 1)
            nc.vector.tensor_tensor(qb[:, :, :], qb[:, :, :], ql[:, :, :], ALU.add).then_inc(s["q_sum"], 1)
            dve.wait_ge(s["q_high"], 1)
            nc.vector.tensor_tensor(ql[:, :, :], qb[:, :, :], qh[:, :, :], ALU.subtract).then_inc(s["q_low"], 1)


def build_cross_attention(nc, ctxT, rot, pack, qh, q3, oall):
    with ExitStack() as ctx:
        sb = lambda name, shape, dt=F32: ctx.enter_context(nc.sbuf_tensor(name, shape, dt))
        sem = lambda name: ctx.enter_context(nc.semaphore("b_" + name))
        psum = lambda name, shape: ctx.enter_context(nc.psum_tensor("b_" + name, shape, F32))
        w = lambda name: pack[:, PACK_AT[name][0]:PACK_AT[name][1]]
        ident = w("ident")

        max_bank = psum("max_bank", [128, 2, 512])
        exp_bank = psum("exp_bank", [128, 3, 512])
        o_bank = psum("o_bank", [128, 2, 2 * T])
        v_bank = psum("v_bank", [128, 512])
        k_bank = psum("k_bank", [128, 512])

        cosk = sb("b_cosk", [128, S])
        sink = sb("b_sink", [128, S])
        cx = sb("b_cx", [128, 2, S])
        kb = sb("b_kb", [128, S])
        kr = sb("b_kr", [128, S])
        ks = sb("b_ks", [128, S])
        kh = sb("b_kh", [128, 2, S], F32R)
        kl = sb("b_kl", [128, S], F32R)
        kst = sb("b_kst", [128, 2, 4, S], F32R)
        v = sb("b_v", [KT, 2, NK, H, VW])
        prob = sb("b_prob", [KT, 3, HT])
        qblk = sb("b_qblk", [128, 2, HT], F32R)
        qst = sb("b_qst", [128, 2, HT], F32R)
        part = sb("b_part", [128, NG, NKC])
        mx = sb("b_mx", [128, NG])
        osb = sb("b_osb", [128, 2, 2, HALF])
        inv = sb("b_inv", [128, 2, 4, 1])

        names = ("ctx_in0 ctx_in1 rot_in kst_in0 kst_in1 ones_ready k_mm k_copied v_mm v_copied cos_done sin_done k_sum "
                 "kh_done kl_done qblk_ready qst_ready maxs_mm chunk_max max_ready mT_mm row_ready s_mm exp_done pv_mm "
                 "o_copied oT_mm inv_ready o_ready").split()
        s = {name: sem(name) for name in names}
        kst_in, ctx_in = [s["kst_in0"], s["kst_in1"]], [s["ctx_in0"], s["ctx_in1"]]
        KDMA = 16 * 24
        NS, NM = 2 * NK, NG * NKC
        block = ctx.enter_context(nc.Block())

        def periods(eng, period):
            for n in range(-2, 2):
                period(n, n % 2, n // 2)
            with eng.Fori(1, B // 2 - 1) as it:
                for u in range(2):
                    period(2 * it + u, u, it)
            for n in range(B - 2, B + 1):
                period(n, n % 2, n // 2)

        def has(n):
            return not isinstance(n, int) or 0 <= n < B

        def row(n):
            return bass.ds(n, 1) if not isinstance(n, int) else slice(n, n + 1)

        @block.sync
        def _(sp):
            sp.dma_start(cx[:, 0, :], ctxT[0]).then_inc(ctx_in[0], 16)
            sp.dma_start(cx[:, 1, :], ctxT[1]).then_inc(ctx_in[1], 16)
            sp.dma_start(cosk[:, :], rot[0]).then_inc(s["rot_in"], 16)
            sp.dma_start(sink[:, :], rot[1]).then_inc(s["rot_in"], 16)

            def period(n, u, it):
                m, o = n + 1, 1 - u
                if has(n + 3):
                    nxt = ctxT[n + 3] if isinstance(n, int) else \
                        ctxT[bass.ds(sp.snap(n + 3), 1)].rearrange("o p s -> (o p) s")
                made, used = 4 * (m + 1), 3 * (m + 1)
                if not isinstance(n, int):
                    made, used = sp.snap(made), sp.snap(used)
                if has(m):
                    sp.wait_ge(s["qst_ready"], made)
                    for part_, dsts in (("h", (0, 64)), ("l", (32,))):
                        src = kh[:, o, :] if part_ == "h" else kl
                        for half in range(2):
                            for g in range(4):
                                at = slice(64 * half + 16 * g, 64 * half + 16 * g + 16)
                                for d in dsts:
                                    sp.dma_start(kst[d + 16 * half:d + 16 * half + 16, o, g, :].bitcast(F32),
                                                 src[at, :].bitcast(F32)).then_inc(kst_in[o], 16)
                if has(n + 3) and (not isinstance(n, int) or n >= -1):
                    sp.wait_ge(s["v_mm"], used)
                    sp.wait_ge(s["k_mm"], used)
                    sp.dma_start(cx[:, o, :], nxt).then_inc(ctx_in[o], 16)

            for n in range(-2, 2):
                period(n, n % 2, n // 2)
            with sp.Fori(1, B // 2 - 2) as it:
                for u in range(2):
                    period(2 * it + u, u, it)
            for n in range(B - 4, B):
                period(n, n % 2, n // 2)

        @block.gpsimd
        def _(pool):
            nc.gpsimd.memset(kst[96:128, :, :, :].bitcast(F32), 1.0).then_inc(s["ones_ready"], 1)
            pool.wait_ge(s["ones_ready"], 2)
            pool.wait_ge(s["rot_in"], 32)

            def block_queries(n, b):
                wait(pool, s["maxs_mm"], NM * (n - 1))
                nc.gpsimd.tensor_tensor(qblk[:, b, :].rearrange("p (h t) -> p h t", t=T),
                                        qh[:, row(n), :].broadcast_to([128, H, T]),
                                        last(w("mask_split"), T), ALU.mult).then_inc(s["qblk_ready"], 1)

            def period(n, u, it):
                m, k, o = n + 1, n + 2, 1 - u
                if has(m):
                    wait(pool, s["s_mm"], NS * (m - 1))
                    for g in range(4):
                        nc.gpsimd.tensor_tensor(
                            qst[0:96, o, HG * T * g:HG * T * (g + 1)].rearrange("p (h t) -> p h t", t=T),
                            q3[:, g, row(m), :].broadcast_to([96, HG, T]),
                            last(w("mask_stack")[0:96], T), ALU.mult).then_inc(s["qst_ready"], 1)
                if has(k):
                    wait(pool, s["kl_done"], k)
                    wait(pool, s["kh_done"], NKC * k)
                    for q in range(NKC):
                        at = slice(KC * q, KC * (q + 1))
                        pool.wait_ge(s["k_copied"], NKC * k + q + 1)
                        nc.gpsimd.tensor_tensor(kr[:, at], kb[:, at], cosk[:, at], ALU.mult)\
                            .then_inc(s["cos_done"], 1)
                        pool.wait_ge(s["cos_done"], NKC * k + q + 1)
                        pool.wait_ge(s["sin_done"], NKC * k + q + 1)
                        nc.gpsimd.tensor_tensor(kr[:, at], kr[:, at], ks[:, at], ALU.add).then_inc(s["k_sum"], 1)
                    block_queries(k, u)
                    pool.wait_ge(s["kh_done"], NKC * (k + 1))
                    wait(pool, kst_in[1 - u], KDMA * (it + u + 1))
                    nc.gpsimd.tensor_tensor(kl[:, :], kr[:, :], kh[:, u, :].bitcast(F32), ALU.subtract)\
                        .then_inc(s["kl_done"], 1)

            periods(pool, period)

        V_SLOT = {0: 0, 2: 1, 4: 2}
        K_SLOT = {1: 0, 3: 1, 5: 2}
        M_COUNT = [3, 3, 2, 3, 2, 3, 1, 2, 2]
        M_SLOT = [range(sum(M_COUNT[:i]), sum(M_COUNT[:i + 1])) for i in range(len(M_COUNT))]
        SIN_SLOT = {2: 0, 4: 1, 6: 2}
        HIGH_SLOT = {4: 0, 6: 1, 8: 2}
        ROW_SLOT = 9

        @block.scalar
        def _(act):
            def period(n, u, it):
                m, k, o = n + 1, n + 2, 1 - u
                for kt in range(NK):
                    if has(n):
                        wait(act, s["pv_mm"], NK * n + kt - 2)
                        for hh in range(2):
                            c = NS * n + 2 * kt + hh
                            act.wait_ge(s["s_mm"], c + 1)
                            nc.scalar.activation(prob[:, kt % 3, HT // 2 * hh:HT // 2 * (hh + 1)],
                                                 exp_bank[0:KT, (2 * kt + hh) % 3, 0:HT // 2],
                                                 ACT.Exp).then_inc(s["exp_done"], 1)
                    if kt == 0 and has(n - 1):
                        act.wait_ge(s["pv_mm"], NK * n)
                        wait(act, s["oT_mm"], n - 1)
                        nc.scalar.activation(osb[:, :, :, 0:T].rearrange("p j a t -> p (j a) t"),
                                             o_bank[:, :, :].rearrange("p j (a t) -> p (j a) t", t=T), ACT.Copy).then_inc(s["o_copied"], 1)
                    if kt in V_SLOT and has(m):
                        q = V_SLOT[kt]
                        act.wait_ge(s["v_mm"], 3 * m + q + 1)
                        wait(act, s["pv_mm"], NK * n)
                        if q == 0 and isinstance(n, int) and n <= 0:
                            act.wait_ge(s["ones_ready"], 2)
                        nc.scalar.activation(
                            v[:, o, 4 * q:4 * q + 4, :, 0:DH].rearrange("p k h d -> p (k h) d"),
                            v_bank[0:KT, :].rearrange("p (kh d) -> p kh d", d=DH), ACT.Copy).then_inc(s["v_copied"], 1)
                    if kt in K_SLOT and has(k):
                        q = K_SLOT[kt]
                        act.wait_ge(s["k_mm"], 3 * k + q + 1)
                        wait(act, s["cos_done"], NKC * (k - 1) + q + 1)
                        wait(act, s["sin_done"], NKC * (k - 1) + q + 1)
                        nc.scalar.activation(kb[:, KC * q:KC * (q + 1)], k_bank[:, 0:KC], ACT.Identity,
                                             bias=w("bk")).then_inc(s["k_copied"], 1)
                    if kt in HIGH_SLOT and has(k):
                        q = HIGH_SLOT[kt]
                        act.wait_ge(s["k_sum"], NKC * k + q + 1)
                        wait(act, s["maxs_mm"], NM * (k - 1))
                        wait(act, kst_in[u], KDMA * (it + 1))
                        nc.scalar.activation(kh[:, u, KC * q:KC * (q + 1)], kr[:, KC * q:KC * (q + 1)],
                                             ACT.Copy).then_inc(s["kh_done"], 1)

            periods(act, period)

        @block.tensor
        def _(pe):
            pe.wait_ge(s["ones_ready"], 2)

            def products(n, u, kt):
                pe.wait_ge(s["exp_done"], NS * n + 2 * kt + 2)
                if kt == 0:
                    pe.wait_ge(s["v_copied"], 3 * (n + 1))
                    wait(pe, s["o_copied"], n)
                for j in range(H // 2):
                    ins = nc.tensor.matmul(
                        o_bank[32 * (j % 4):32 * (j % 4) + 2 * VW, j // 4, 0:2 * T],
                        v[:, u, kt, 2 * j:2 * j + 2, :].rearrange("p h d -> p (h d)"),
                        prob[:, kt % 3, 2 * T * j:2 * T * (j + 1)],
                        start=(kt == 0 and j < 4), stop=(kt == NK - 1), skip_group_check=True)
                ins.then_inc(s["pv_mm"], 1)

            def period(n, u, it):
                m, k, o = n + 1, n + 2, 1 - u

                def maxima(c):
                    q, g = divmod(c, NG)
                    if c == 0:
                        pe.wait_ge(s["kh_done"], NKC * (m + 1))
                        pe.wait_ge(s["qblk_ready"], m + 1)
                    wait(pe, s["chunk_max"], NM * m + c - 1)
                    nc.tensor.matmul(max_bank[:, (o + c) % 2, 0:KC], qblk[:, o, 128 * g:128 * g + 128],
                                     kh[:, o, KC * q:KC * (q + 1)], start=True, stop=True)\
                        .then_inc(s["maxs_mm"], 1)

                for kt in range(NK):
                    chunks = list(M_SLOT[kt]) if kt < len(M_SLOT) and has(m) else []
                    if has(n):
                        if kt == 0:
                            pe.wait_ge(s["qst_ready"], 4 * (n + 1))
                            pe.wait_ge(s["row_ready"], n + 1)
                            pe.wait_ge(kst_in[u], KDMA * (it + 1))
                        for hh in range(2):
                            wait(pe, s["exp_done"], NS * n + 2 * kt + hh - 2)
                            for g in range(2 * hh, 2 * hh + 2):
                                ins = nc.tensor.matmul(
                                    exp_bank[0:KT, (2 * kt + hh) % 3, HG * T * (g % 2):HG * T * (g % 2 + 1)],
                                    kst[:, u, g, KT * kt:KT * (kt + 1)], qst[:, u, HG * T * g:HG * T * (g + 1)],
                                    start=True, stop=True)
                            ins.then_inc(s["s_mm"], 1)
                            if chunks:
                                maxima(chunks.pop(0))
                        if kt > 0:
                            products(n, u, kt - 1)
                    if kt == 0 and has(n - 1):
                        products(n - 1, o, NK - 1)
                    for c in chunks:
                        maxima(c)
                    if kt in V_SLOT and has(m):
                        q = V_SLOT[kt]
                        if q == 0:
                            pe.wait_ge(ctx_in[o], 16 * ((it + u) + 1))
                            wait(pe, s["row_ready"], m)
                        wait(pe, s["v_copied"], 3 * m + q)
                        for j in range(4):
                            ins = nc.tensor.matmul(v_bank[0:KT, 128 * j:128 * j + 128],
                                                   cx[:, o, KT * (4 * q + j):KT * (4 * q + j + 1)], w("xwv"),
                                                   start=True, stop=True)
                        ins.then_inc(s["v_mm"], 1)
                    if kt in K_SLOT and has(k):
                        q = K_SLOT[kt]
                        if q == 0:
                            pe.wait_ge(ctx_in[u], 16 * (it + 2))
                            wait(pe, s["o_ready"], n - 1)
                        wait(pe, s["k_copied"], 3 * k + q)
                        nc.tensor.matmul(k_bank[:, 0:KC], w("xwk"), cx[:, u, KC * q:KC * (q + 1)],
                                         start=True, stop=True).then_inc(s["k_mm"], 1)
                    if kt == 6 and has(n - 1):
                        pe.wait_ge(s["o_copied"], n)
                        wait(pe, s["k_copied"], min_rows(n))
                        wait(pe, s["o_ready"], n - 1)
                        for j in range(2):
                            ins = nc.tensor.transpose(k_bank[:, 128 * j:128 * j + 128],
                                                      osb[:, j, :, :].rearrange("p a t -> p (a t)"), ident)
                        ins.then_inc(s["oT_mm"], 1)
                    if kt == ROW_SLOT and has(m):
                        pe.wait_ge(s["max_ready"], m + 1)
                        pe.wait_ge(s["v_copied"], 3 * (m + 1))
                        nc.tensor.transpose(v_bank[0:NG, 0:128], mx[:, :], ident).then_inc(s["mT_mm"], 1)

            def min_rows(n):
                return min(3 * (n + 3), 3 * B) if isinstance(n, int) else 3 * (n + 3)

            periods(pe, period)

        @block.vector
        def _(dve):
            nc.vector.memset(v[:, :, :, :, DH:VW], 1.0)
            nc.vector.memset(qst[96:128, :, :].bitcast(F32), 0.0)
            nc.vector.memset(osb[:, :, :, :], 0.0)
            nc.vector.memset(o_bank[:, :, :], 0.0).then_inc(s["ones_ready"], 1)
            dve.wait_ge(s["rot_in"], 32)
            lo, hi = slice(0, 64), slice(64, 128)

            def period(n, u, it):
                m, k, o = n + 1, n + 2, 1 - u
                for kt in range(NK):
                    if kt < len(M_SLOT) and has(m):
                        if kt == 0:
                            wait(dve, s["max_ready"], m)
                        for c in M_SLOT[kt]:
                            dve.wait_ge(s["maxs_mm"], NM * m + c + 1)
                            nc.vector.tensor_reduce(part[:, c % NG, c // NG:c // NG + 1],
                                                    max_bank[:, (o + c) % 2, 0:KC], AX.X, ALU.max)\
                                .then_inc(s["chunk_max"], 1)
                    if kt in SIN_SLOT and has(k):
                        q = SIN_SLOT[kt]
                        at = slice(KC * q, KC * (q + 1))
                        dve.wait_ge(s["k_copied"], NKC * k + q + 1)
                        wait(dve, s["k_sum"], NKC * (k - 1) + q + 1)
                        nc.vector.tensor_tensor(ks[lo, at], kb[hi, at], sink[hi, at], ALU.mult)
                        nc.vector.tensor_tensor(ks[hi, at], kb[lo, at], sink[lo, at], ALU.mult)\
                            .then_inc(s["sin_done"], 1)
                    if kt == ROW_SLOT and has(m):
                        dve.wait_ge(s["chunk_max"], NM * (m + 1))
                        wait(dve, s["mT_mm"], m)
                        nc.vector.tensor_reduce(mx[:, :], part[:, :, :], AX.X, ALU.max, negate=True)\
                            .then_inc(s["max_ready"], 1)
                    if kt == ROW_SLOT and has(n - 1):
                        dve.wait_ge(s["oT_mm"], n)
                        for a in range(2):
                            ov = k_bank[HALF * a:HALF * a + T, 0:256].rearrange("p (j q r) -> p j q r", j=2, r=32)
                            nc.vector.reciprocal(inv[HALF * a:HALF * a + T, :, :, :],
                                                 ov[:, :, :, VW * a + DH:VW * a + VW]).then_inc(s["inv_ready"], 1)
                        dve.wait_ge(s["inv_ready"], 2 * n)
                        dst = oall[HALF * o:HALF * o + T, row_tile(n - 1, it, u), :]\
                            .rearrange("p i (j q a d) -> p (i j) q a d", j=2, a=2, d=DH)
                        for a in range(2):
                            ov = k_bank[HALF * a:HALF * a + T, 0:256].rearrange("p (j q r) -> p j q r", j=2, r=32)
                            ins = nc.vector.tensor_tensor(dst[:, :, :, a, :], ov[:, :, :, VW * a:VW * a + DH],
                                                          inv[HALF * a:HALF * a + T, :, :, :]
                                                          .broadcast_to([T, 2, 4, DH]), ALU.mult)
                        ins.then_inc(s["o_ready"], 1)
                    if kt == ROW_SLOT and has(m):
                        dve.wait_ge(s["mT_mm"], m + 1)
                        dve.wait_ge(s["ones_ready"], 2)
                        wait(dve, s["s_mm"], NS * (m - 1))
                        nc.vector.tensor_tensor(qst[96:96 + NG, o, :].rearrange("p (g r) -> p g r", r=128),
                                                mid(v_bank[0:NG, 0:128], NG), last(w("mask_m")[0:NG], 128),
                                                ALU.mult).then_inc(s["row_ready"], 1)

            def row_tile(n, it, u):
                t = it if u == 1 else it - 1
                return bass.ds(t, 1) if not isinstance(t, int) else slice(t, t + 1)

            periods(dve, period)


def build_experts(nc, pack, wd_dram, xres, oall, out_dram):
    with ExitStack() as ctx:
        sb = lambda name, shape, dt=F32: ctx.enter_context(nc.sbuf_tensor(name, shape, dt))
        sem = lambda name: ctx.enter_context(nc.semaphore("c_" + name))
        bank = [ctx.enter_context(nc.psum_tensor(f"c_bank{i}", [128, 512], F32)) for i in range(8)]
        w = lambda name: pack[:, PACK_AT[name][0]:PACK_AT[name][1]]
        ident = w("ident")

        oT = sb("c_oT", [128, NT, 128])
        xc = sb("c_xc", [128, NT, D])
        sq = sb("c_sq", [128, NT, D])
        yT = sb("c_yT", [128, NT, 128])
        stats = sb("c_stats", [128, 6, NT])
        brow = sb("c_brow", [1, D])
        ones = sb("c_ones", [128, 128])
        logit = sb("c_logit", [128, NT, NE])
        top = sb("c_top", [128, NT, 8])
        topi = sb("c_topi", [128, NT, 8], U32)
        topf = sb("c_topf", [128, NT, 8])
        hot = sb("c_hot", [128, 3, NT, NE])
        ex = sb("c_ex", [128, NT, NE])
        cum = sb("c_cum", [128, NT, NE])
        off = sb("c_off", [128, NT, NE])
        g = sb("c_g", [128, 10, NT])
        comb = sb("c_comb", [128, NT, NE])
        wd = sb("c_wd", [128, 2, NE * D])
        hid = sb("c_hid", [128, 2, 2, 128])
        acc = sb("c_acc", [128, NT, D])

        names = ("ready brow_mm brow_ready oT_mm oT_copied o_mm x_added ln var_ready std_ready rstd y_ready yT_mm "
                 "yT_copied lg_mm r wd_in ex_ready gap_ready exp2_done cum_mm comb_ready h_mm h_done e_mm e_done out_in").split()
        s = {name: sem(name) for name in names}
        block = ctx.enter_context(nc.Block())

        @block.tensor
        def _(pe):
            pe.wait_ge(s["ready"], 2)
            nc.tensor.matmul(bank[7][0:1, 0:D], w("bv"), w("xwo"), start=True, stop=True).then_inc(s["brow_mm"], 1)
            for c in range(4):
                for j in range(4):
                    ins = nc.tensor.transpose(bank[c][:, 128 * j:128 * j + 128], oall[:, 4 * c + j, :], ident)
                ins.then_inc(s["oT_mm"], 1)
            pe.wait_ge(s["brow_ready"], 1)
            for c in range(4):
                pe.wait_ge(s["oT_copied"], c + 1)
                if c == 3:
                    pe.wait_ge(s["x_added"], 0 + 1)
                for j in range(4):
                    o = bank[4 + c % 3][:, 128 * j:128 * j + 128]
                    nc.tensor.matmul(o, oT[:, 4 * c + j, :], w("xwo"), start=True, stop=False)
                    ins = nc.tensor.matmul(o, ones[0:1, :], brow[0:1, :], start=False, stop=True)
                ins.then_inc(s["o_mm"], 1)
            pe.wait_ge(s["y_ready"], 1)
            for c in range(4):
                for j in range(4):
                    ins = nc.tensor.transpose(bank[c][:, 128 * j:128 * j + 128], xc[:, 4 * c + j, :], ident)
                ins.then_inc(s["yT_mm"], 1)
            for i in range(NT):
                if i % 4 == 0:
                    pe.wait_ge(s["yT_copied"], i // 4 + 1)
                ins = nc.tensor.matmul(bank[7][:, NE * i:NE * i + NE], yT[:, i, :], w("wr"), start=True, stop=True)
            ins.then_inc(s["lg_mm"], 1)
            pe.wait_ge(s["r"], 4)
            hots = hot[:, 2, :, :].rearrange("p i e -> p (i e)")
            nc.tensor.matmul(bank[0][:, 0:NT * NE], w("tri"), hots, start=True, stop=True)
            nc.tensor.matmul(bank[1][:, 0:NT * NE], ones[:, :], hots, start=True, stop=True).then_inc(s["cum_mm"], 1)

            def tile(i, u):
                wait(pe, s["h_done"], 2 * i)
                at = bass.ds(i, 1) if not isinstance(i, int) else slice(i, i + 1)
                for f in range(2):
                    nc.tensor.matmul(bank[6 + f][:, 0:128], w("wg")[:, 128 * f:128 * f + 128],
                                     yT[:, at, :].rearrange("p i t -> p (i t)"), start=True, stop=True)\
                        .then_inc(s["h_mm"], 1)

            def experts(i, u):
                pe.wait_ge(s["h_done"], 2 * i + 2)
                wait(pe, s["e_done"], i - 1)
                for c in range(2):
                    for f in range(2):
                        ins = nc.tensor.matmul(bank[2 + 2 * u + c][:, :], hid[:, u, f, :],
                                               wd[:, f, 512 * c:512 * c + 512], start=(f == 0), stop=(f == 1))
                ins.then_inc(s["e_mm"], 1)

            tile(0, 0)
            pe.wait_ge(s["wd_in"], 16)
            for i in range(2):
                tile(i + 1, 1 - i)
                experts(i, i)
            with pe.Fori(1, NT // 2 - 1) as it:
                for u in range(2):
                    tile(2 * it + u + 1, 1 - u)
                    experts(2 * it + u, u)
            tile(NT - 1, 1)
            experts(NT - 2, 0)
            experts(NT - 1, 1)

        @block.scalar
        def _(act):
            for c in range(4):
                act.wait_ge(s["oT_mm"], c + 1)
                nc.scalar.activation(oT[:, 4 * c:4 * c + 4, :].rearrange("p i t -> p (i t)"), bank[c][:, :],
                                     ACT.Copy).then_inc(s["oT_copied"], 1)
            act.wait_ge(s["var_ready"], 1)
            nc.scalar.activation(stats[:, 3, :], stats[:, 2, :], ACT.Sqrt).then_inc(s["std_ready"], 1)
            for c in range(4):
                act.wait_ge(s["yT_mm"], c + 1)
                nc.scalar.activation(yT[:, 4 * c:4 * c + 4, :].rearrange("p i t -> p (i t)"), bank[c][:, :],
                                     ACT.Copy).then_inc(s["yT_copied"], 1)
            act.wait_ge(s["gap_ready"], 1)
            nc.scalar.activation(ex[:, :, :], ex[:, :, :], ACT.Exp).then_inc(s["ex_ready"], 1)
            nc.scalar.activation(g[:, 1, :], g[:, 0, :], ACT.Exp).then_inc(s["exp2_done"], 1)

            def tile(i, u):
                for f in range(2):
                    act.wait_ge(s["h_mm"], 2 * i + f + 1)
                    if f == 0:
                        wait(act, s["e_mm"], i - 1)
                    nc.scalar.activation(hid[:, u, f, :], bank[6 + f][:, 0:128], ACT.Silu).then_inc(s["h_done"], 1)

            tile(0, 0)
            tile(1, 1)
            with act.Fori(1, NT // 2) as it:
                for u in range(2):
                    tile(2 * it + u, u)

        @block.vector
        def _(dve):
            nc.vector.memset(ones[:, :], 1.0).then_inc(s["ready"], 1)
            nc.vector.memset(acc[:, :, :], 0.0).then_inc(s["ready"], 1)
            dve.wait_ge(s["brow_mm"], 1)
            nc.vector.tensor_tensor(brow[0:1, :], bank[7][0:1, 0:D], w("bo")[0:1, :], ALU.add).then_inc(s["brow_ready"], 1)
            for c in range(4):
                dve.wait_ge(s["o_mm"], c + 1)
                nc.vector.tensor_tensor(xres[:, 4 * c:4 * c + 4, :], xres[:, 4 * c:4 * c + 4, :],
                                        bank[4 + c % 3][:, :].rearrange("p (i d) -> p i d", d=D),
                                        ALU.add).then_inc(s["x_added"], 1)
            dve.wait_ge(s["x_added"], 4)
            n, step = layer_norm(nc, dve, xres[:, :, :], xc[:, :, :], stats, s, 0)
            step(nc.vector.tensor_tensor(sq[:, :, :], xc[:, :, :], xc[:, :, :], ALU.mult))
            step(nc.vector.tensor_reduce(stats[:, 4, :], sq[:, :, :], AX.X, ALU.add))
            nc.vector.tensor_scalar(stats[:, 2, :], stats[:, 4, :], 1.0 / D, EPS, ALU.mult, ALU.add)\
                .then_inc(s["var_ready"], 1)
            dve.wait_ge(s["std_ready"], 1)
            nc.vector.reciprocal(stats[:, 5, :], stats[:, 3, :]).then_inc(s["rstd"], 1)
            dve.wait_ge(s["rstd"], 1)
            nc.vector.tensor_tensor(xc[:, :, :], xc[:, :, :], last(stats[:, 5, :], D), ALU.mult)\
                .then_inc(s["y_ready"], 1)

            dve.wait_ge(s["lg_mm"], 1)
            nc.vector.tensor_copy(logit[:, :, :], bank[7][:, 0:NT * NE].rearrange("p (i e) -> p i e", e=NE))\
                .then_inc(s["r"], 1)
            dve.wait_ge(s["r"], 1)
            for i in range(NT):
                ins = nc.vector.max(top[:, i, :], logit[:, i, :])
            ins.then_inc(s["r"], 1)
            dve.wait_ge(s["r"], 2)
            for i in range(NT):
                ins = nc.vector.max_index(topi[:, i, :], top[:, i, :], logit[:, i, :])
            step(ins)
            step(nc.vector.tensor_copy(topf[:, :, :], topi[:, :, :]))
            for c in range(2):
                ins = nc.vector.tensor_tensor(hot[:, c, :, :], mid(w("iota"), NT),
                                              topf[:, :, c:c + 1].broadcast_to([128, NT, NE]), ALU.is_equal)
            ins.then_inc(s["r"], 1)
            dve.wait_ge(s["r"], 3)
            step(nc.vector.tensor_tensor(hot[:, 2, :, :], hot[:, 0, :, :], hot[:, 1, :, :], ALU.add))
            nc.vector.tensor_scalar(hot[:, 2, :, :], hot[:, 2, :, :], w("valid"), None, ALU.mult).then_inc(s["r"], 1)
            nc.vector.tensor_tensor(ex[:, :, :], logit[:, :, :], top[:, :, 0:1].broadcast_to([128, NT, NE]), ALU.subtract)
            nc.vector.tensor_tensor(g[:, 0, :].unsqueeze(2), top[:, :, 1:2], top[:, :, 0:1], ALU.subtract)\
                .then_inc(s["gap_ready"], 1)
            dve.wait_ge(s["cum_mm"], 1)
            step(nc.vector.memset(off[:, 0, :], 0.0))
            tot = bank[1][:, 0:NT * NE].rearrange("p (i e) -> p i e", e=NE)
            for i in range(1, NT):
                step(nc.vector.tensor_tensor(off[:, i, :], off[:, i - 1, :], tot[:, i - 1, :], ALU.add))
            step(nc.vector.tensor_tensor(cum[:, :, :], bank[0][:, 0:NT * NE].rearrange("p (i e) -> p i e", e=NE),
                                         off[:, :, :], ALU.add))
            step(nc.vector.tensor_scalar(cum[:, :, :], cum[:, :, :], float(CAPACITY), None, ALU.is_le))
            for c in range(2):
                step(nc.vector.tensor_tensor(sq[:, :, 0:NE], cum[:, :, :], hot[:, c, :, :], ALU.mult))
                step(nc.vector.tensor_reduce(g[:, 2 + c, :], sq[:, :, 0:NE], AX.X, ALU.add))
            dve.wait_ge(s["ex_ready"], 1)
            step(nc.vector.tensor_reduce(g[:, 4, :], ex[:, :, :], AX.X, ALU.add))
            step(nc.vector.reciprocal(g[:, 5, :], g[:, 4, :]))
            dve.wait_ge(s["exp2_done"], 1)
            step(nc.vector.tensor_tensor(g[:, 6, :], g[:, 5, :], g[:, 2, :], ALU.mult))
            step(nc.vector.tensor_tensor(g[:, 7, :], g[:, 5, :], g[:, 1, :], ALU.mult))
            step(nc.vector.tensor_tensor(g[:, 7, :], g[:, 7, :], g[:, 3, :], ALU.mult))
            step(nc.vector.tensor_tensor(g[:, 8, :], g[:, 6, :], g[:, 7, :], ALU.add))
            step(nc.vector.tensor_scalar(g[:, 8, :], g[:, 8, :], 1e-6, None, ALU.add))
            step(nc.vector.reciprocal(g[:, 9, :], g[:, 8, :]))
            step(nc.vector.tensor_tensor(g[:, 6, :], g[:, 6, :], g[:, 9, :], ALU.mult))
            step(nc.vector.tensor_tensor(g[:, 7, :], g[:, 7, :], g[:, 9, :], ALU.mult))
            step(nc.vector.tensor_tensor(comb[:, :, :], hot[:, 0, :, :], last(g[:, 6, :], NE), ALU.mult))
            step(nc.vector.tensor_tensor(sq[:, :, 0:NE], hot[:, 1, :, :], last(g[:, 7, :], NE), ALU.mult))
            nc.vector.tensor_tensor(comb[:, :, :], comb[:, :, :], sq[:, :, 0:NE], ALU.add).then_inc(s["comb_ready"], 1)
            dve.wait_ge(s["comb_ready"], 1)

            def tile(i, u):
                at = bass.ds(i, 1) if not isinstance(i, int) else slice(i, i + 1)
                dve.wait_ge(s["e_mm"], i + 1)
                for e in range(NE):
                    a = acc[:, at, :].rearrange("p i d -> p (i d)")
                    r = xres[:, at, :].rearrange("p i d -> p (i d)")
                    ins = nc.vector.scalar_tensor_tensor(
                        out=a, in0=bank[2 + 2 * u + e // 4][:, 128 * (e % 4):128 * (e % 4) + 128],
                        scalar=comb[:, at, e:e + 1].rearrange("p i e -> p (i e)"), in1=r if e == 0 else a,
                        op0=ALU.mult, op1=ALU.add)
                    if e < NE - 1:
                        ins.then_inc(s["r"], 1)
                        dve.wait_ge(s["r"], 4 + (NE - 1) * i + e + 1)
                    else:
                        ins.then_inc(s["e_done"], 1)

            with dve.Fori(0, NT // 2) as it:
                for u in range(2):
                    tile(2 * it + u, u)

        @block.sync
        def _(sp):
            sp.dma_start(wd[:, :, :], wd_dram).then_inc(s["wd_in"], 16)
            ov = out_dram.rearrange("(i two) t d -> two t i d", two=2)
            for c in range(4):
                sp.wait_ge(s["e_done"], 4 * (c + 1))
                at = slice(4 * c, 4 * c + 4)
                sp.dma_start(ov[0][:, at, :], acc[0:T, at, :]).then_inc(s["out_in"], 16)
                sp.dma_start(ov[1][:, at, :], acc[HALF:HALF + T, at, :]).then_inc(s["out_in"], 16)
            sp.wait_ge(s["out_in"], 16 * 8)


def build(nc, x, ctxT, rot, packed, wd, out):
    with ExitStack() as ctx:
        sb = lambda name, shape, dt=F32: ctx.enter_context(nc.sbuf_tensor(name, shape, dt))
        xres = sb("xres", [128, NT, D])
        qh = sb("qh", [128, B, T])
        oall = sb("oall", [128, NT, D])
        pack = sb("pack", [128, PACK_N])
        fresh = {"pack_in": ctx.enter_context(nc.semaphore("pack_in"))}
        q3 = sb("q3", [96, 4, B, T])
        with ExitStack() as load:
            block = load.enter_context(nc.Block())

            @block.sync
            def _(sp):
                sp.dma_start(pack[:, :], packed).then_inc(fresh["pack_in"], 16)

            @block.vector
            def _(dve):
                nc.vector.memset(oall[:, :, :], 0.0)

        build_self_attention(nc, x, pack, xres, qh, q3, fresh)
        build_cross_attention(nc, ctxT, rot, pack, qh, q3, oall)
        build_experts(nc, pack, wd, xres, oall, out)


def kernel(x, ctx_1024, L0_attn_Wq, L0_attn_Wk, L0_attn_Wv, L0_attn_Wo, L0_xattn_wq, L0_xattn_bq, L0_xattn_wk,
           L0_xattn_bk, L0_xattn_wv, L0_xattn_bv, L0_xattn_wo, L0_xattn_bo, L0_ffn_w_router, L0_ffn_w_gate,
           L0_ffn_w_down):
    import numpy as np
    import concourse.bacc as bacc
    from concourse.bass_utils import run_bass_kernel_spmd as run

    split = np.array([DH * h + 2 * f + odd for odd in range(2) for h in range(H) for f in range(DH // 2)])

    def tables(length, inverse, factor):
        f32 = np.float32
        base = (np.arange(0, DH, 2, dtype=f32) + f32(0.4 * DH)) / f32(1.4 * DH)
        low = -length // 2
        power = np.arange(low, length + low, dtype=f32) / f32(D)
        scale = base[None, :] ** power[:, None]
        freq = (1.0 / 10000.0 ** (np.arange(DH // 2, dtype=f32) / f32(DH // 2))).astype(f32)
        ang = np.arange(length, dtype=f32)[:, None] * freq[None, :]
        if inverse:
            scale = 1.0 / scale
        cos = (np.cos(ang) * scale * factor).T.astype(f32)
        sin = (np.sin(ang) * scale * factor).T.astype(f32)
        return np.tile(cos, (2 * H, 1)), np.concatenate([np.tile(sin, (H, 1)), -np.tile(sin, (H, 1))])

    cosk, sink = tables(S, True, np.float32(1.0))
    cosq, sinq = tables(T, False, np.float32(DH ** -0.5))
    p = np.arange(128)
    c = {
        "ident": np.eye(128),
        "causal": np.where((np.arange(T)[None, :] > (p % HALF)[:, None]) & ((p % HALF) < T)[:, None], -1e30, 0.0),
        "mask_nat": (p // DH)[:, None] == np.arange(H)[None, :],
        "mask_split": ((p % 64) // 4)[:, None] == np.arange(H)[None, :],
        "mask_stack": ((p % 16) // 4)[:, None] == np.arange(HG)[None, :],
        "mask_m": p[:, None] == np.arange(NG)[None, :],
        "tri": p[:, None] <= p[None, :],
        "valid": ((p % HALF) < T)[:, None],
        "iota": np.broadcast_to(np.arange(NE), (128, NE)),
        "cosq": cosq, "sinq": sinq,
    }
    c = {k: np.asarray(a).astype(np.float32) for k, a in c.items()}
    a = {k: np.asarray(v) for k, v in dict(
        Wq=L0_attn_Wq, Wk=L0_attn_Wk, Wv=L0_attn_Wv, Wo=L0_attn_Wo, xwv=L0_xattn_wv, xwo=L0_xattn_wo,
        wr=L0_ffn_w_router, wg=L0_ffn_w_gate).items()}
    c.update({k: v.T for k, v in a.items()})
    c["xwq"] = np.asarray(L0_xattn_wq).T[:, split]
    c["xwk"] = np.asarray(L0_xattn_wk).T[:, split]
    c["bq"] = np.asarray(L0_xattn_bq)[split][:, None]
    c["bk"] = np.asarray(L0_xattn_bk)[split][:, None]
    c["bv"] = np.asarray(L0_xattn_bv)[:, None]
    c["bo"] = np.broadcast_to(np.asarray(L0_xattn_bo)[None, :], (128, D))
    wd = np.asarray(L0_ffn_w_down).transpose(2, 0, 1).reshape(2, 128, NE * D).transpose(1, 0, 2)
    packed = np.ascontiguousarray(np.concatenate([c[name] for name, _ in PACK], axis=1))

    arrays = {
        "x": np.ascontiguousarray(np.asarray(x)),
        "ctxT": np.ascontiguousarray(np.asarray(ctx_1024).transpose(0, 2, 1)),
        "rot": np.ascontiguousarray(np.stack([cosk, sink])),
        "packed": packed,
        "wd": np.ascontiguousarray(wd),
    }
    nc = bacc.Bacc("TRN2", target_bir_lowering=False, num_devices=1)
    args = [nc.dram_tensor(k, v.shape, mybir.dt.from_np(v.dtype), kind="ExternalInput").ap()
            for k, v in arrays.items()]
    out = nc.dram_tensor("out", (B, T, D), F32, kind="ExternalOutput").ap()
    build(nc, *args, out)
    r = run(nc, [arrays], core_ids=[0])
    return r.results[0]["out"]
```

```python
from contextlib import ExitStack

import concourse.bass as bass
from concourse import mybir

F32 = mybir.dt.float32
F32R = mybir.dt.float32r
U32 = mybir.dt.uint32
ALU = mybir.AluOpType
ACT = mybir.ActivationFunctionType
AX = mybir.AxisListType

B, T, D, H, S = 32, 56, 128, 16, 1500
DH = D // H
NT = B // 2
HALF = 64
HT = H * T
KT, NK = 125, 12
NE, FH = 8, 256
CAPACITY = -(-B * T * 5 // (NE * 4))
KC, NKC = 500, 3
NG = HT // 128
HG = 4
VW = DH + 1
EPS = 1e-5

PACK = [("ident", 128), ("causal", T), ("mask_nat", H), ("mask_split", H), ("mask_stack", HG), ("mask_m", NG),
        ("tri", 128), ("valid", 1), ("iota", NE), ("cosq", T), ("sinq", T),
        ("Wq", D), ("Wk", D), ("Wv", D), ("Wo", D), ("xwq", D), ("xwk", D), ("xwv", D), ("xwo", D),
        ("bq", 1), ("bk", 1), ("bv", 1), ("bo", D), ("wr", NE), ("wg", FH)]
PACK_AT = {}
PACK_N = 0
for _name, _width in PACK:
    PACK_AT[_name] = (PACK_N, PACK_N + _width)
    PACK_N += _width


def wait(eng, sem, value):
    if isinstance(value, int) and value <= 0:
        return
    eng.wait_ge(sem, value)


def mid(ap, n):
    return ap.unsqueeze(1).broadcast_to([ap.shape[0], n, ap.shape[1]])


def last(ap, n):
    return ap.unsqueeze(len(ap.shape)).broadcast_to([*ap.shape, n])


def layer_norm(nc, dve, x, work, stats, s, base):
    n = [base]

    def step(ins):
        n[0] += 1
        ins.then_inc(s["ln"], 1)
        dve.wait_ge(s["ln"], n[0])

    step(nc.vector.tensor_reduce(stats[:, 0, :], x, AX.X, ALU.add))
    step(nc.vector.tensor_scalar(stats[:, 1, :], stats[:, 0, :], -1.0 / D, None, ALU.mult))
    step(nc.vector.tensor_tensor(work, x, last(stats[:, 1, :], D), ALU.add))
    return n, step


def build_self_attention(nc, x_dram, packed, ctxT, rot, pack, xres, oall, qh, cx, cosk, sink, kst, low, shared):
    with ExitStack() as ctx:
        sb = lambda name, shape, dt=F32: ctx.enter_context(nc.sbuf_tensor(name, shape, dt))
        sem = lambda name: ctx.enter_context(nc.semaphore("a_" + name))
        psum = lambda name, shape: ctx.enter_context(nc.psum_tensor("a_" + name, shape, F32))
        w = lambda name: pack[:, PACK_AT[name][0]:PACK_AT[name][1]]
        ident = w("ident")

        y_bank = psum("y_bank", [128, 512])
        prj_bank = psum("prj_bank", [128, 512])
        s_bank = psum("s_bank", [128, 2, 512])
        p_bank = psum("p_bank", [128, 2, 512])
        pv_bank = psum("pv_bank", [128, 512])
        out_bank = psum("out_bank", [128, 512])

        bn = sb("a_bn", [128, NT, 6])
        mv = sb("a_mv", [128, NT, 2])
        std = sb("a_std", [128, 3, NT])
        ytile = sb("a_ytile", [128, 2, D])
        yT = sb("a_yT", [128, 2, 128])
        prj = sb("a_prj", [128, 2, 256])
        vblk = sb("a_vblk", [128, 2, 2, H // 2, 2, VW])
        kblk = sb("a_kblk", [128, 2, 2, H, T])
        att = sb("a_att", [128, 2, H, HALF])
        top = sb("a_top", [128, H])
        inv = sb("a_inv", [128, H // 2, 2, 1])
        pT = sb("a_pT", [128, H // 2, 128])
        on = sb("a_on", [128, D])
        oT = sb("a_oT", [128, 128])
        y2 = sb("a_y2", [128, NT, D])
        y2T = sb("a_y2T", [128, NT, 128])
        qa = sb("a_qa", [128, B, T])
        qb = sb("a_qb", [128, B, T])
        ql = low[:, :].rearrange("p (b t) -> p b t", t=T)

        names = ("pack_in v_zeroed pool_set zeroed x_in pads bn_done mv_done var_ready std_ready rstd_ready ytile_ready yT_mm yT_copied "
                 "prj_mm prj_copied v_mm v_copied kblk_ready s_mm masked max_ready shifted exp_done pT_mm pT_copied pv_mm "
                 "inv_ready on_ready oT_mm oT_copied out_mm x_added y2_ready y2T_mm y2T_copied q_mm q_biased q_cos "
                 "q_sin q_sum q_high q_low").split()
        s = {name: sem(name) for name in names}
        block = ctx.enter_context(nc.Block())

        def periods(eng, period):
            for p in range(-3, 2):
                period(p, p % 2)
            with eng.Fori(1, NT // 2 - 2) as it:
                for u in range(2):
                    period(2 * it + u, u)
            for p in range(NT - 4, NT + 1):
                period(p, p % 2)

        def has(p):
            return not isinstance(p, int) or 0 <= p < NT

        def tile(p):
            return bass.ds(p, 1) if not isinstance(p, int) else slice(p, p + 1)

        def high(act, c):
            rows = slice(8 * c, 8 * c + 8)
            act.wait_ge(s["q_sum"], c + 1)
            nc.scalar.activation(qh[:, rows, :].bitcast(F32R), qb[:, rows, :], ACT.Copy).then_inc(s["q_high"], 1)

        tail_banks = [s_bank[:, 0, :], s_bank[:, 1, :], p_bank[:, 0, :], p_bank[:, 1, :]]

        @block.sync
        def _(sp):
            sp.dma_start(pack[:, :], packed).then_inc(s["pack_in"], 16)
            xv = x_dram.rearrange("(i two) t d -> two t i d", two=2)
            sp.wait_ge(s["zeroed"], 2)
            sp.dma_start(xres[0:T, :, :], xv[0]).then_inc(s["x_in"], 16)
            sp.dma_start(xres[HALF:HALF + T, :, :], xv[1]).then_inc(s["x_in"], 16)
            sp.dma_start(cosk[:, :], rot[0]).then_inc(shared["rot_in"], 16)
            sp.dma_start(sink[:, :], rot[1]).then_inc(shared["rot_in"], 16)
            sp.dma_start(cx[:, 0, :], ctxT[0]).then_inc(shared["ctx_in0"], 16)
            sp.dma_start(cx[:, 1, :], ctxT[1]).then_inc(shared["ctx_in1"], 16)

        @block.gpsimd
        def _(pool):
            nc.gpsimd.memset(xres[:, NT // 2:NT, :], 0.0).then_inc(s["zeroed"], 1)
            nc.gpsimd.memset(att[:, :, :, :], 0.0).then_inc(s["pads"], 1)
            nc.gpsimd.memset(oall[:, :, :], 0.0).then_inc(s["pool_set"], 1)
            pool.wait_ge(s["pool_set"], 1)
            nc.gpsimd.memset(kst[96:128, :, :, :].bitcast(F32), 1.0).then_inc(s["pool_set"], 1)
            pool.wait_ge(s["pool_set"], 2)
            pool.wait_ge(s["pack_in"], 16)

            def period(p, u):
                q, b = p + 2, u % 2
                if has(q):
                    pool.wait_ge(s["prj_copied"], q + 1)
                    wait(pool, s["s_mm"], 2 * (q - 1))
                    for a in range(2):
                        kT = prj[:, b, 128 + HALF * a:128 + HALF * a + T]
                        nc.gpsimd.tensor_tensor(kblk[:, b, a, :, :], mid(kT, H), last(w("mask_nat"), T),
                                                ALU.mult).then_inc(s["kblk_ready"], 1)

            periods(pool, period)
            for c in range(4):
                rows = slice(8 * c, 8 * c + 8)
                pool.wait_ge(s["q_biased"], c + 1)
                nc.gpsimd.tensor_tensor(qb[:, rows, :], qa[:, rows, :], mid(w("cosq"), 8), ALU.mult)\
                    .then_inc(s["q_cos"], 1)

        @block.scalar
        def _(act):
            act.wait_ge(s["var_ready"], 1)
            nc.scalar.activation(std[:, 1, :], std[:, 0, :], ACT.Sqrt).then_inc(s["std_ready"], 1)

            def period(p, u):
                z, q, r, o = p + 3, p + 2, p + 1, p - 1
                b, other = u % 2, (u + 1) % 2
                if has(q):
                    act.wait_ge(s["prj_mm"], q + 1)
                    wait(act, s["s_mm"], 2 * (q - 1))
                    wait(act, s["kblk_ready"], 2 * (q - 1))
                    nc.scalar.activation(prj[:, b, :], prj_bank[:, 0:256], ACT.Copy).then_inc(s["prj_copied"], 1)
                if has(o):
                    act.wait_ge(s["oT_mm"], o + 1)
                    wait(act, s["out_mm"], o)
                    nc.scalar.activation(oT[:, :], out_bank[:, 0:128], ACT.Copy).then_inc(s["oT_copied"], 1)
                if has(z):
                    act.wait_ge(s["yT_mm"], z + 1)
                    wait(act, s["v_mm"], z - 1)
                    nc.scalar.activation(yT[:, other, :], y_bank[:, 0:128], ACT.Copy).then_inc(s["yT_copied"], 1)
                if has(p):
                    wait(act, s["pv_mm"], p)
                    for c in range(2):
                        act.wait_ge(s["pT_mm"], 2 * p + c + 1)
                        nc.scalar.activation(pT[:, 4 * c:4 * c + 4, :].rearrange("p h t -> p (h t)"),
                                             p_bank[:, c, :], ACT.Copy).then_inc(s["pT_copied"], 1)
                if has(r):
                    act.wait_ge(s["shifted"], r + 1)
                    a = att[:, other, :, 0:T]
                    nc.scalar.activation(a, a, ACT.Exp, scale=float(DH) ** -0.5).then_inc(s["exp_done"], 1)
                if has(q):
                    act.wait_ge(s["v_mm"], q + 1)
                    wait(act, s["pv_mm"], q - 1)
                    for a in range(2):
                        for odd in range(2):
                            ins = nc.scalar.activation(
                                vblk[HALF * odd:HALF * odd + T, b, a, :, odd, 0:DH],
                                y_bank[HALF * a:HALF * a + T, 128:256]
                                .rearrange("p (j two d) -> p j two d", two=2, d=DH)[:, :, odd, :], ACT.Copy)
                    ins.then_inc(s["v_copied"], 1)

            periods(act, period)
            act.wait_ge(s["var_ready"], 2)
            nc.scalar.activation(std[:, 1, :], std[:, 0, :], ACT.Sqrt).then_inc(s["std_ready"], 1)
            for c in range(4):
                act.wait_ge(s["y2T_mm"], c + 1)
                nc.scalar.activation(y2T[:, 4 * c:4 * c + 4, :].rearrange("p i t -> p (i t)"), tail_banks[c % 2],
                                     ACT.Copy).then_inc(s["y2T_copied"], 1)
                act.wait_ge(s["q_mm"], c + 1)
                nc.scalar.activation(qa[:, 8 * c:8 * c + 8, :],
                                     tail_banks[2 + c % 2].rearrange("p (b t) -> p b t", t=HALF)[:, :, 0:T],
                                     ACT.Identity, bias=w("bq")).then_inc(s["q_biased"], 1)
                if c > 0:
                    high(act, c - 1)
            high(act, 3)

        @block.tensor
        def _(pe):
            pe.wait_ge(s["pack_in"], 16)

            def period(p, u):
                z, q, r, o = p + 3, p + 2, p + 1, p - 1
                b, other = u % 2, (u + 1) % 2
                if has(q):
                    pe.wait_ge(s["yT_copied"], q + 1)
                    wait(pe, s["prj_copied"], q)
                    nc.tensor.matmul(prj_bank[:, 0:128], w("Wq"), yT[:, b, :], start=True, stop=True)
                    nc.tensor.matmul(prj_bank[:, 128:256], w("Wk"), yT[:, b, :], start=True, stop=True)\
                        .then_inc(s["prj_mm"], 1)
                if has(r):
                    if isinstance(r, int) and r == 0:
                        pe.wait_ge(s["pads"], 2)
                    wait(pe, s["masked"], r)
                    for hh in range(2):
                        for a in range(2):
                            if hh == 0:
                                pe.wait_ge(s["kblk_ready"], 2 * r + a + 1)
                            ins = nc.tensor.matmul(
                                s_bank[HALF * a:HALF * a + T, hh, 0:HT // 2],
                                prj[:, other, HALF * a:HALF * a + T],
                                kblk[:, other, a, 8 * hh:8 * hh + 8, :].rearrange("p h t -> p (h t)"),
                                start=True, stop=True)
                        ins.then_inc(s["s_mm"], 1)
                if has(q):
                    wait(pe, s["v_copied"], q)
                    nc.tensor.matmul(y_bank[:, 128:256], yT[:, b, :], w("Wv"), start=True, stop=True)\
                        .then_inc(s["v_mm"], 1)
                if has(o):
                    pe.wait_ge(s["on_ready"], o + 1)
                    wait(pe, s["x_added"], o)
                    nc.tensor.transpose(out_bank[:, 0:128], on[:, :], ident).then_inc(s["oT_mm"], 1)
                if has(z):
                    pe.wait_ge(s["ytile_ready"], z + 1)
                    wait(pe, s["yT_copied"], z)
                    nc.tensor.transpose(y_bank[:, 0:128], ytile[:, other, :], ident).then_inc(s["yT_mm"], 1)
                if has(p):
                    pe.wait_ge(s["exp_done"], p + 1)
                    wait(pe, s["pT_copied"], 2 * p)
                    for h in range(H // 2):
                        ins = nc.tensor.transpose(p_bank[:, h // 4, 128 * (h % 4):128 * (h % 4) + 128],
                                                  att[:, b, 2 * h:2 * h + 2, :].rearrange("p h t -> p (h t)"), ident)
                        if h % 4 == 3:
                            ins.then_inc(s["pT_mm"], 1)
                if has(o):
                    pe.wait_ge(s["oT_copied"], o + 1)
                    nc.tensor.matmul(out_bank[:, 128:256], oT[:, :], w("Wo"), start=True, stop=True)\
                        .then_inc(s["out_mm"], 1)
                if has(p):
                    pe.wait_ge(s["v_copied"], p + 1)
                    wait(pe, s["on_ready"], p)
                    for j in range(H // 2):
                        if j % 4 == 0:
                            pe.wait_ge(s["pT_copied"], 2 * p + j // 4 + 1)
                        for a in range(2):
                            ins = nc.tensor.matmul(pv_bank[HALF * a:HALF * a + T, 2 * VW * j:2 * VW * (j + 1)],
                                                   pT[:, j, HALF * a:HALF * a + T],
                                                   vblk[:, b, a, j, :, :].rearrange("p o d -> p (o d)"),
                                                   start=True, stop=True)
                    ins.then_inc(s["pv_mm"], 1)

            periods(pe, period)
            for c in range(4):
                pe.wait_ge(s["y2_ready"], c + 1)
                if c >= 2:
                    pe.wait_ge(s["y2T_copied"], c - 1)
                for j in range(4):
                    ins = nc.tensor.transpose(tail_banks[c % 2][:, 128 * j:128 * j + 128], y2[:, 4 * c + j, :], ident)
                ins.then_inc(s["y2T_mm"], 1)
                pe.wait_ge(s["y2T_copied"], c + 1)
                if c >= 2:
                    pe.wait_ge(s["q_biased"], c - 1)
                nc.tensor.matmul(tail_banks[2 + c % 2], w("xwq"),
                                 y2T[:, 4 * c:4 * c + 4, :].rearrange("p i t -> p (i t)"),
                                 start=True, stop=True).then_inc(s["q_mm"], 1)

        @block.vector
        def _(dve):
            nc.vector.memset(xres[:, 0:NT // 2, :], 0.0).then_inc(s["zeroed"], 1)
            nc.vector.memset(vblk[:, :, :, :, :, :], 0.0).then_inc(s["v_zeroed"], 1)
            dve.wait_ge(s["v_zeroed"], 1)
            for odd in range(2):
                nc.vector.memset(vblk[HALF * odd:HALF * odd + T, :, :, :, odd, DH:VW], 1.0)
            nc.vector.memset(s_bank[:, :, :], 0.0)
            pv = pv_bank[:, 0:H * VW].rearrange("p (j o d) -> p j o d", o=2, d=VW)
            nc.vector.memset(pv[:, :, :, 0:DH], 0.0)
            nc.vector.memset(pv[:, :, :, DH:VW], 1.0).then_inc(s["pads"], 1)

            def inverse_std(nth):
                dve.wait_ge(s["bn_done"], NT * nth)
                for i in range(NT):
                    ins = nc.vector.bn_aggr(mv[:, i, :], bn[:, i, :])
                ins.then_inc(s["mv_done"], 1)
                dve.wait_ge(s["mv_done"], nth)
                nc.vector.tensor_scalar(std[:, 0, :], mv[:, :, 1], EPS, None, ALU.add).then_inc(s["var_ready"], 1)
                dve.wait_ge(s["std_ready"], nth)
                nc.vector.reciprocal(std[:, 2, :], std[:, 1, :]).then_inc(s["rstd_ready"], 1)
                dve.wait_ge(s["rstd_ready"], nth)

            dve.wait_ge(s["x_in"], 32)
            for i in range(NT):
                nc.vector.bn_stats(bn[:, i, :], xres[:, i, :]).then_inc(s["bn_done"], 1)
            inverse_std(1)
            dve.wait_ge(s["pack_in"], 16)

            def normalise(out, i):
                flat = lambda ap: ap.rearrange("p i d -> p (i d)")
                return nc.vector.tensor_scalar(out, flat(xres[:, tile(i), :]), flat(mv[:, tile(i), 0:1]),
                                               std[:, 2, tile(i)], ALU.subtract, ALU.mult)

            def period(p, u):
                z, r, o = p + 3, p + 1, p - 1
                b, other = u % 2, (u + 1) % 2
                if has(o):
                    dve.wait_ge(s["pv_mm"], o + 1)
                    nc.vector.reciprocal(inv[:, :, :, :], pv[:, :, :, DH:VW]).then_inc(s["inv_ready"], 1)
                    dve.wait_ge(s["inv_ready"], o + 1)
                    wait(dve, s["oT_mm"], o)
                    nc.vector.tensor_tensor(on[:, :].rearrange("p (j o d) -> p j o d", o=2, d=DH),
                                            pv[:, :, :, 0:DH], inv[:, :, :, :].broadcast_to([128, H // 2, 2, DH]),
                                            ALU.mult).then_inc(s["on_ready"], 1)
                if has(z):
                    wait(dve, s["yT_mm"], z - 1)
                    normalise(ytile[:, other, :], z).then_inc(s["ytile_ready"], 1)
                if has(r):
                    wait(dve, s["pT_mm"], 2 * (r - 1))
                    a = att[:, other, :, 0:T]
                    if isinstance(r, int) and r == 0:
                        dve.wait_ge(s["pads"], 2)
                    for hh in range(2):
                        dve.wait_ge(s["s_mm"], 2 * r + hh + 1)
                        ins = nc.vector.tensor_tensor(
                            a[:, 8 * hh:8 * hh + 8, :], s_bank[:, hh, 0:HT // 2].rearrange("p (h t) -> p h t", t=T),
                            mid(w("causal"), 8), ALU.add)
                    ins.then_inc(s["masked"], 1)
                    dve.wait_ge(s["masked"], r + 1)
                    nc.vector.tensor_reduce(top[:, :], a, AX.X, ALU.max).then_inc(s["max_ready"], 1)
                    dve.wait_ge(s["max_ready"], r + 1)
                    nc.vector.tensor_tensor(a, a, last(top[:, :], T), ALU.subtract).then_inc(s["shifted"], 1)
                if has(o):
                    dve.wait_ge(s["out_mm"], o + 1)
                    x = xres[:, tile(o), :]
                    nc.vector.tensor_tensor(x, x, out_bank[:, 128:256].unsqueeze(1), ALU.add)\
                        .then_inc(s["x_added"], 1)
                    dve.wait_ge(s["x_added"], o + 1)
                    nc.vector.bn_stats(bn[:, tile(o), :].rearrange("p i n -> p (i n)"),
                                       x.rearrange("p i d -> p (i d)")).then_inc(s["bn_done"], 1)

            periods(dve, period)
            inverse_std(2)
            for i in range(NT):
                ins = normalise(y2[:, i, :], i)
                if i % 4 == 3:
                    ins.then_inc(s["y2_ready"], 1)
            sinq, lo, hi = w("sinq"), slice(0, 64), slice(64, 128)

            def low(c):
                rows = slice(8 * c, 8 * c + 8)
                dve.wait_ge(s["q_high"], c + 1)
                nc.vector.tensor_tensor(ql[:, rows, :], qb[:, rows, :], qh[:, rows, :], ALU.subtract)\
                    .then_inc(s["q_low"], 1)

            for c in range(4):
                rows = slice(8 * c, 8 * c + 8)
                dve.wait_ge(s["q_biased"], c + 1)
                nc.vector.tensor_tensor(ql[lo, rows, :], qa[hi, rows, :], mid(sinq[hi], 8), ALU.mult)
                nc.vector.tensor_tensor(ql[hi, rows, :], qa[lo, rows, :], mid(sinq[lo], 8), ALU.mult)\
                    .then_inc(s["q_sin"], 1)
                dve.wait_ge(s["q_sin"], c + 1)
                dve.wait_ge(s["q_cos"], c + 1)
                nc.vector.tensor_tensor(qb[:, rows, :], qb[:, rows, :], ql[:, rows, :], ALU.add)\
                    .then_inc(s["q_sum"], 1)
                if c > 0:
                    low(c - 1)
            low(3)


def build_cross_attention(nc, ctxT, pack, qh, q3, oall, cx, cosk, sink, kst, low, shared):
    with ExitStack() as ctx:
        sb = lambda name, shape, dt=F32: ctx.enter_context(nc.sbuf_tensor(name, shape, dt))
        sem = lambda name: ctx.enter_context(nc.semaphore("b_" + name))
        psum = lambda name, shape: ctx.enter_context(nc.psum_tensor("b_" + name, shape, F32))
        w = lambda name: pack[:, PACK_AT[name][0]:PACK_AT[name][1]]
        ident = w("ident")

        max_bank = psum("max_bank", [128, 2, 512])
        exp_bank = psum("exp_bank", [128, 3, 512])
        o_bank = psum("o_bank", [128, 2, 2 * T])
        v_bank = psum("v_bank", [128, 512])
        k_bank = psum("k_bank", [128, 512])

        kb = sb("b_kb", [128, S])
        kr = sb("b_kr", [128, S])
        ks = sb("b_ks", [128, S])
        kh = sb("b_kh", [128, 2, S], F32R)
        kl = low[:, 0:S].bitcast(F32R)
        ql = low[:, :].rearrange("p (b t) -> p b t", t=T)
        v = sb("b_v", [KT, 2, NK, H, VW])
        prob = sb("b_prob", [KT, 3, HT])
        qblk = sb("b_qblk", [128, 2, HT], F32R)
        qst = sb("b_qst", [128, 2, HT], F32R)
        part = sb("b_part", [128, NG, NKC])
        mx = sb("b_mx", [128, NG])
        osb = sb("b_osb", [128, 2, 2, HALF])
        inv = sb("b_inv", [128, 2, 4, 1])

        names = ("q3_in kst_in0 kst_in1 ones_ready k_mm k_copied v_mm v_copied cos_done sin_done k_sum "
                 "kh_done kl_done qblk_ready qst_ready maxs_mm chunk_max max_ready mT_mm row_ready s_mm exp_done pv_mm "
                 "o_copied oT_mm inv_ready o_ready").split()
        s = {name: sem(name) for name in names}
        s.update(shared)
        kst_in, ctx_in = [s["kst_in0"], s["kst_in1"]], [s["ctx_in0"], s["ctx_in1"]]
        KDMA = 16 * 24
        NS, NM = 2 * NK, NG * NKC
        block = ctx.enter_context(nc.Block())

        def periods(eng, period):
            for n in range(-2, 2):
                period(n, n % 2, n // 2)
            with eng.Fori(1, B // 2 - 1) as it:
                for u in range(2):
                    period(2 * it + u, u, it)
            for n in range(B - 2, B + 1):
                period(n, n % 2, n // 2)

        def has(n):
            return not isinstance(n, int) or 0 <= n < B

        def row(n):
            return bass.ds(n, 1) if not isinstance(n, int) else slice(n, n + 1)

        @block.sync
        def _(sp):
            for quad, src in enumerate((qh, qh, ql)):
                for half in range(2):
                    for g in range(4):
                        at = slice(64 * half + 16 * g, 64 * half + 16 * g + 16)
                        dst = slice(32 * quad + 16 * half, 32 * quad + 16 * half + 16)
                        sp.dma_start(q3[dst, g, :, :], src[at, :, :]).then_inc(s["q3_in"], 16)

            def period(n, u, it):
                m, o = n + 1, 1 - u
                if has(n + 3):
                    nxt = ctxT[n + 3] if isinstance(n, int) else \
                        ctxT[bass.ds(sp.snap(n + 3), 1)].rearrange("o p s -> (o p) s")
                made, used = 4 * (m + 1), 3 * (m + 1)
                if not isinstance(n, int):
                    made, used = sp.snap(made), sp.snap(used)
                if has(m):
                    sp.wait_ge(s["qst_ready"], made)
                    for part_, dsts in (("h", (0, 64)), ("l", (32,))):
                        src = kh[:, o, :] if part_ == "h" else kl
                        for half in range(2):
                            for g in range(4):
                                at = slice(64 * half + 16 * g, 64 * half + 16 * g + 16)
                                for d in dsts:
                                    sp.dma_start(kst[d + 16 * half:d + 16 * half + 16, o, g, :].bitcast(F32),
                                                 src[at, :].bitcast(F32)).then_inc(kst_in[o], 16)
                if has(n + 3) and (not isinstance(n, int) or n >= -1):
                    sp.wait_ge(s["v_mm"], used)
                    sp.wait_ge(s["k_mm"], used)
                    sp.dma_start(cx[:, o, :], nxt).then_inc(ctx_in[o], 16)

            for n in range(-2, 2):
                period(n, n % 2, n // 2)
            with sp.Fori(1, B // 2 - 2) as it:
                for u in range(2):
                    period(2 * it + u, u, it)
            for n in range(B - 4, B):
                period(n, n % 2, n // 2)

        @block.gpsimd
        def _(pool):
            pool.wait_ge(s["rot_in"], 32)

            def block_queries(n, b):
                wait(pool, s["maxs_mm"], NM * (n - 1))
                nc.gpsimd.tensor_tensor(qblk[:, b, :].rearrange("p (h t) -> p h t", t=T),
                                        qh[:, row(n), :].broadcast_to([128, H, T]),
                                        last(w("mask_split"), T), ALU.mult).then_inc(s["qblk_ready"], 1)

            def period(n, u, it):
                m, k, o = n + 1, n + 2, 1 - u
                if has(m):
                    wait(pool, s["s_mm"], NS * (m - 1))
                    for g in range(4):
                        nc.gpsimd.tensor_tensor(
                            qst[0:96, o, HG * T * g:HG * T * (g + 1)].rearrange("p (h t) -> p h t", t=T),
                            q3[:, g, row(m), :].broadcast_to([96, HG, T]),
                            last(w("mask_stack")[0:96], T), ALU.mult).then_inc(s["qst_ready"], 1)
                if has(k):
                    wait(pool, s["kl_done"], k)
                    wait(pool, s["kh_done"], NKC * k)
                    for q in range(NKC):
                        at = slice(KC * q, KC * (q + 1))
                        pool.wait_ge(s["k_copied"], NKC * k + q + 1)
                        nc.gpsimd.tensor_tensor(kr[:, at], kb[:, at], cosk[:, at], ALU.mult)\
                            .then_inc(s["cos_done"], 1)
                        pool.wait_ge(s["cos_done"], NKC * k + q + 1)
                        pool.wait_ge(s["sin_done"], NKC * k + q + 1)
                        nc.gpsimd.tensor_tensor(kr[:, at], kr[:, at], ks[:, at], ALU.add).then_inc(s["k_sum"], 1)
                    block_queries(k, u)
                    pool.wait_ge(s["kh_done"], NKC * (k + 1))
                    wait(pool, kst_in[1 - u], KDMA * (it + u + 1))
                    if isinstance(k, int) and k == 0:
                        pool.wait_ge(s["q3_in"], 16 * 24)
                    nc.gpsimd.tensor_tensor(kl[:, :], kr[:, :], kh[:, u, :].bitcast(F32), ALU.subtract)\
                        .then_inc(s["kl_done"], 1)

            periods(pool, period)

        V_SLOT = {0: 0, 2: 1, 4: 2}
        K_SLOT = {1: 0, 3: 1, 5: 2}
        M_COUNT = [3, 3, 2, 3, 2, 3, 1, 2, 2]
        M_SLOT = [range(sum(M_COUNT[:i]), sum(M_COUNT[:i + 1])) for i in range(len(M_COUNT))]
        SIN_SLOT = {2: 0, 4: 1, 6: 2}
        HIGH_SLOT = {4: 0, 6: 1, 8: 2}
        ROW_SLOT = 9

        @block.scalar
        def _(act):
            def period(n, u, it):
                m, k, o = n + 1, n + 2, 1 - u
                for kt in range(NK):
                    if has(n):
                        wait(act, s["pv_mm"], NK * n + kt - 2)
                        for hh in range(2):
                            c = NS * n + 2 * kt + hh
                            act.wait_ge(s["s_mm"], c + 1)
                            nc.scalar.activation(prob[:, kt % 3, HT // 2 * hh:HT // 2 * (hh + 1)],
                                                 exp_bank[0:KT, (2 * kt + hh) % 3, 0:HT // 2],
                                                 ACT.Exp).then_inc(s["exp_done"], 1)
                    if kt == 0 and has(n - 1):
                        act.wait_ge(s["pv_mm"], NK * n)
                        wait(act, s["oT_mm"], n - 1)
                        nc.scalar.activation(osb[:, :, :, 0:T].rearrange("p j a t -> p (j a) t"),
                                             o_bank[:, :, :].rearrange("p j (a t) -> p (j a) t", t=T), ACT.Copy).then_inc(s["o_copied"], 1)
                    if kt in V_SLOT and has(m):
                        q = V_SLOT[kt]
                        act.wait_ge(s["v_mm"], 3 * m + q + 1)
                        wait(act, s["pv_mm"], NK * n)
                        if q == 0 and isinstance(n, int) and n <= 0:
                            act.wait_ge(s["ones_ready"], 1)
                        nc.scalar.activation(
                            v[:, o, 4 * q:4 * q + 4, :, 0:DH].rearrange("p k h d -> p (k h) d"),
                            v_bank[0:KT, :].rearrange("p (kh d) -> p kh d", d=DH), ACT.Copy).then_inc(s["v_copied"], 1)
                    if kt in K_SLOT and has(k):
                        q = K_SLOT[kt]
                        act.wait_ge(s["k_mm"], 3 * k + q + 1)
                        wait(act, s["cos_done"], NKC * (k - 1) + q + 1)
                        wait(act, s["sin_done"], NKC * (k - 1) + q + 1)
                        nc.scalar.activation(kb[:, KC * q:KC * (q + 1)], k_bank[:, 0:KC], ACT.Identity,
                                             bias=w("bk")).then_inc(s["k_copied"], 1)
                    if kt in HIGH_SLOT and has(k):
                        q = HIGH_SLOT[kt]
                        act.wait_ge(s["k_sum"], NKC * k + q + 1)
                        wait(act, s["maxs_mm"], NM * (k - 1))
                        wait(act, kst_in[u], KDMA * (it + 1))
                        nc.scalar.activation(kh[:, u, KC * q:KC * (q + 1)], kr[:, KC * q:KC * (q + 1)],
                                             ACT.Copy).then_inc(s["kh_done"], 1)

            periods(act, period)

        @block.tensor
        def _(pe):
            def products(n, u, kt):
                pe.wait_ge(s["exp_done"], NS * n + 2 * kt + 2)
                if kt == 0:
                    if isinstance(n, int) and n == 0:
                        pe.wait_ge(s["ones_ready"], 1)
                    pe.wait_ge(s["v_copied"], 3 * (n + 1))
                    wait(pe, s["o_copied"], n)
                for j in range(H // 2):
                    ins = nc.tensor.matmul(
                        o_bank[32 * (j % 4):32 * (j % 4) + 2 * VW, j // 4, 0:2 * T],
                        v[:, u, kt, 2 * j:2 * j + 2, :].rearrange("p h d -> p (h d)"),
                        prob[:, kt % 3, 2 * T * j:2 * T * (j + 1)],
                        start=(kt == 0 and j < 4), stop=(kt == NK - 1), skip_group_check=True)
                ins.then_inc(s["pv_mm"], 1)

            def period(n, u, it):
                m, k, o = n + 1, n + 2, 1 - u

                def maxima(c):
                    q, g = divmod(c, NG)
                    if c == 0:
                        pe.wait_ge(s["kh_done"], NKC * (m + 1))
                        pe.wait_ge(s["qblk_ready"], m + 1)
                    wait(pe, s["chunk_max"], NM * m + c - 1)
                    nc.tensor.matmul(max_bank[:, (o + c) % 2, 0:KC], qblk[:, o, 128 * g:128 * g + 128],
                                     kh[:, o, KC * q:KC * (q + 1)], start=True, stop=True)\
                        .then_inc(s["maxs_mm"], 1)

                for kt in range(NK):
                    chunks = list(M_SLOT[kt]) if kt < len(M_SLOT) and has(m) else []
                    if has(n):
                        if kt == 0:
                            pe.wait_ge(s["qst_ready"], 4 * (n + 1))
                            pe.wait_ge(s["row_ready"], n + 1)
                            pe.wait_ge(kst_in[u], KDMA * (it + 1))
                        for hh in range(2):
                            wait(pe, s["exp_done"], NS * n + 2 * kt + hh - 2)
                            for g in range(2 * hh, 2 * hh + 2):
                                ins = nc.tensor.matmul(
                                    exp_bank[0:KT, (2 * kt + hh) % 3, HG * T * (g % 2):HG * T * (g % 2 + 1)],
                                    kst[:, u, g, KT * kt:KT * (kt + 1)], qst[:, u, HG * T * g:HG * T * (g + 1)],
                                    start=True, stop=True)
                            ins.then_inc(s["s_mm"], 1)
                            if chunks:
                                maxima(chunks.pop(0))
                        if kt > 0:
                            products(n, u, kt - 1)
                    if kt == 0 and has(n - 1):
                        products(n - 1, o, NK - 1)
                    for c in chunks:
                        maxima(c)
                    if kt in V_SLOT and has(m):
                        q = V_SLOT[kt]
                        if q == 0:
                            pe.wait_ge(ctx_in[o], 16 * ((it + u) + 1))
                            wait(pe, s["row_ready"], m)
                        wait(pe, s["v_copied"], 3 * m + q)
                        for j in range(4):
                            ins = nc.tensor.matmul(v_bank[0:KT, 128 * j:128 * j + 128],
                                                   cx[:, o, KT * (4 * q + j):KT * (4 * q + j + 1)], w("xwv"),
                                                   start=True, stop=True)
                        ins.then_inc(s["v_mm"], 1)
                    if kt in K_SLOT and has(k):
                        q = K_SLOT[kt]
                        if q == 0:
                            pe.wait_ge(ctx_in[u], 16 * (it + 2))
                            wait(pe, s["o_ready"], n - 1)
                        wait(pe, s["k_copied"], 3 * k + q)
                        nc.tensor.matmul(k_bank[:, 0:KC], w("xwk"), cx[:, u, KC * q:KC * (q + 1)],
                                         start=True, stop=True).then_inc(s["k_mm"], 1)
                    if kt == 6 and has(n - 1):
                        pe.wait_ge(s["o_copied"], n)
                        wait(pe, s["k_copied"], min_rows(n))
                        wait(pe, s["o_ready"], n - 1)
                        for j in range(2):
                            ins = nc.tensor.transpose(k_bank[:, 128 * j:128 * j + 128],
                                                      osb[:, j, :, :].rearrange("p a t -> p (a t)"), ident)
                        ins.then_inc(s["oT_mm"], 1)
                    if kt == ROW_SLOT and has(m):
                        pe.wait_ge(s["max_ready"], m + 1)
                        pe.wait_ge(s["v_copied"], 3 * (m + 1))
                        nc.tensor.transpose(v_bank[0:NG, 0:128], mx[:, :], ident).then_inc(s["mT_mm"], 1)

            def min_rows(n):
                return min(3 * (n + 3), 3 * B) if isinstance(n, int) else 3 * (n + 3)

            periods(pe, period)

        @block.vector
        def _(dve):
            nc.vector.memset(v[:, :, :, :, DH:VW], 1.0)
            nc.vector.memset(qst[96:128, :, :].bitcast(F32), 0.0)
            nc.vector.memset(osb[:, :, :, :], 0.0)
            nc.vector.memset(o_bank[:, :, :], 0.0).then_inc(s["ones_ready"], 1)
            dve.wait_ge(s["rot_in"], 32)
            lo, hi = slice(0, 64), slice(64, 128)

            def period(n, u, it):
                m, k, o = n + 1, n + 2, 1 - u
                for kt in range(NK):
                    if kt < len(M_SLOT) and has(m):
                        if kt == 0:
                            wait(dve, s["max_ready"], m)
                        for c in M_SLOT[kt]:
                            dve.wait_ge(s["maxs_mm"], NM * m + c + 1)
                            nc.vector.tensor_reduce(part[:, c % NG, c // NG:c // NG + 1],
                                                    max_bank[:, (o + c) % 2, 0:KC], AX.X, ALU.max)\
                                .then_inc(s["chunk_max"], 1)
                    if kt in SIN_SLOT and has(k):
                        q = SIN_SLOT[kt]
                        at = slice(KC * q, KC * (q + 1))
                        dve.wait_ge(s["k_copied"], NKC * k + q + 1)
                        wait(dve, s["k_sum"], NKC * (k - 1) + q + 1)
                        nc.vector.tensor_tensor(ks[lo, at], kb[hi, at], sink[hi, at], ALU.mult)
                        nc.vector.tensor_tensor(ks[hi, at], kb[lo, at], sink[lo, at], ALU.mult)\
                            .then_inc(s["sin_done"], 1)
                    if kt == ROW_SLOT and has(m):
                        dve.wait_ge(s["chunk_max"], NM * (m + 1))
                        wait(dve, s["mT_mm"], m)
                        nc.vector.tensor_reduce(mx[:, :], part[:, :, :], AX.X, ALU.max, negate=True)\
                            .then_inc(s["max_ready"], 1)
                    if kt == ROW_SLOT and has(n - 1):
                        dve.wait_ge(s["oT_mm"], n)
                        for a in range(2):
                            ov = k_bank[HALF * a:HALF * a + T, 0:256].rearrange("p (j q r) -> p j q r", j=2, r=32)
                            nc.vector.reciprocal(inv[HALF * a:HALF * a + T, :, :, :],
                                                 ov[:, :, :, VW * a + DH:VW * a + VW]).then_inc(s["inv_ready"], 1)
                        dve.wait_ge(s["inv_ready"], 2 * n)
                        dst = oall[HALF * o:HALF * o + T, row_tile(n - 1, it, u), :]\
                            .rearrange("p i (j q a d) -> p (i j) q a d", j=2, a=2, d=DH)
                        for a in range(2):
                            ov = k_bank[HALF * a:HALF * a + T, 0:256].rearrange("p (j q r) -> p j q r", j=2, r=32)
                            ins = nc.vector.tensor_tensor(dst[:, :, :, a, :], ov[:, :, :, VW * a:VW * a + DH],
                                                          inv[HALF * a:HALF * a + T, :, :, :]
                                                          .broadcast_to([T, 2, 4, DH]), ALU.mult)
                        ins.then_inc(s["o_ready"], 1)
                    if kt == ROW_SLOT and has(m):
                        dve.wait_ge(s["mT_mm"], m + 1)
                        wait(dve, s["s_mm"], NS * (m - 1))
                        nc.vector.tensor_tensor(qst[96:96 + NG, o, :].rearrange("p (g r) -> p g r", r=128),
                                                mid(v_bank[0:NG, 0:128], NG), last(w("mask_m")[0:NG], 128),
                                                ALU.mult).then_inc(s["row_ready"], 1)

            def row_tile(n, it, u):
                t = it if u == 1 else it - 1
                return bass.ds(t, 1) if not isinstance(t, int) else slice(t, t + 1)

            periods(dve, period)


def build_experts(nc, pack, wd_dram, xres, oall, out_dram):
    with ExitStack() as ctx:
        sb = lambda name, shape, dt=F32: ctx.enter_context(nc.sbuf_tensor(name, shape, dt))
        sem = lambda name: ctx.enter_context(nc.semaphore("c_" + name))
        bank = [ctx.enter_context(nc.psum_tensor(f"c_bank{i}", [128, 512], F32)) for i in range(8)]
        w = lambda name: pack[:, PACK_AT[name][0]:PACK_AT[name][1]]
        ident = w("ident")

        oT = sb("c_oT", [128, NT, 128])
        xc = sb("c_xc", [128, NT, D])
        sq = sb("c_sq", [128, NT, D])
        yT = sb("c_yT", [128, NT, 128])
        stats = sb("c_stats", [128, 6, NT])
        brow = sb("c_brow", [1, D])
        ones = sb("c_ones", [128, 128])
        logit = sb("c_logit", [128, NT, NE])
        top = sb("c_top", [128, NT, 8])
        topi = sb("c_topi", [128, NT, 8], U32)
        topf = sb("c_topf", [128, NT, 8])
        hot = sb("c_hot", [128, 3, NT, NE])
        ex = sb("c_ex", [128, NT, NE])
        cum = sb("c_cum", [128, NT, NE])
        off = sb("c_off", [128, NT, NE])
        g = sb("c_g", [128, 10, NT])
        comb = sb("c_comb", [128, NT, NE])
        wd = sb("c_wd", [128, 2, NE * D])
        hid = sb("c_hid", [128, 2, 2, 128])
        acc = sb("c_acc", [128, NT, D])

        names = ("ready brow_mm brow_ready oT_mm oT_copied o_mm x_added ln var_ready std_ready rstd y_ready yT_mm "
                 "yT_copied lg_mm r wd_in ex_ready gap_ready exp2_done cum_mm comb_ready h_mm h_done e_mm e_done out_in").split()
        s = {name: sem(name) for name in names}
        block = ctx.enter_context(nc.Block())

        @block.tensor
        def _(pe):
            pe.wait_ge(s["ready"], 2)
            nc.tensor.matmul(bank[7][0:1, 0:D], w("bv"), w("xwo"), start=True, stop=True).then_inc(s["brow_mm"], 1)
            for c in range(4):
                for j in range(4):
                    ins = nc.tensor.transpose(bank[c][:, 128 * j:128 * j + 128], oall[:, 4 * c + j, :], ident)
                ins.then_inc(s["oT_mm"], 1)
            pe.wait_ge(s["brow_ready"], 1)
            for c in range(4):
                pe.wait_ge(s["oT_copied"], c + 1)
                if c == 3:
                    pe.wait_ge(s["x_added"], 0 + 1)
                for j in range(4):
                    o = bank[4 + c % 3][:, 128 * j:128 * j + 128]
                    nc.tensor.matmul(o, oT[:, 4 * c + j, :], w("xwo"), start=True, stop=False)
                    ins = nc.tensor.matmul(o, ones[0:1, :], brow[0:1, :], start=False, stop=True)
                ins.then_inc(s["o_mm"], 1)
            pe.wait_ge(s["y_ready"], 1)
            for c in range(4):
                for j in range(4):
                    ins = nc.tensor.transpose(bank[c][:, 128 * j:128 * j + 128], xc[:, 4 * c + j, :], ident)
                ins.then_inc(s["yT_mm"], 1)
            for i in range(NT):
                if i % 4 == 0:
                    pe.wait_ge(s["yT_copied"], i // 4 + 1)
                ins = nc.tensor.matmul(bank[7][:, NE * i:NE * i + NE], yT[:, i, :], w("wr"), start=True, stop=True)
            ins.then_inc(s["lg_mm"], 1)
            pe.wait_ge(s["r"], 4)
            hots = hot[:, 2, :, :].rearrange("p i e -> p (i e)")
            nc.tensor.matmul(bank[0][:, 0:NT * NE], w("tri"), hots, start=True, stop=True)
            nc.tensor.matmul(bank[1][:, 0:NT * NE], ones[:, :], hots, start=True, stop=True).then_inc(s["cum_mm"], 1)

            def tile(i, u):
                wait(pe, s["h_done"], 2 * i)
                at = bass.ds(i, 1) if not isinstance(i, int) else slice(i, i + 1)
                for f in range(2):
                    nc.tensor.matmul(bank[6 + f][:, 0:128], w("wg")[:, 128 * f:128 * f + 128],
                                     yT[:, at, :].rearrange("p i t -> p (i t)"), start=True, stop=True)\
                        .then_inc(s["h_mm"], 1)

            def experts(i, u):
                pe.wait_ge(s["h_done"], 2 * i + 2)
                wait(pe, s["e_done"], i - 1)
                for c in range(2):
                    for f in range(2):
                        ins = nc.tensor.matmul(bank[2 + 2 * u + c][:, :], hid[:, u, f, :],
                                               wd[:, f, 512 * c:512 * c + 512], start=(f == 0), stop=(f == 1))
                ins.then_inc(s["e_mm"], 1)

            tile(0, 0)
            pe.wait_ge(s["wd_in"], 16)
            for i in range(2):
                tile(i + 1, 1 - i)
                experts(i, i)
            with pe.Fori(1, NT // 2 - 1) as it:
                for u in range(2):
                    tile(2 * it + u + 1, 1 - u)
                    experts(2 * it + u, u)
            tile(NT - 1, 1)
            experts(NT - 2, 0)
            experts(NT - 1, 1)

        @block.scalar
        def _(act):
            for c in range(4):
                act.wait_ge(s["oT_mm"], c + 1)
                nc.scalar.activation(oT[:, 4 * c:4 * c + 4, :].rearrange("p i t -> p (i t)"), bank[c][:, :],
                                     ACT.Copy).then_inc(s["oT_copied"], 1)
            act.wait_ge(s["var_ready"], 1)
            nc.scalar.activation(stats[:, 3, :], stats[:, 2, :], ACT.Sqrt).then_inc(s["std_ready"], 1)
            for c in range(4):
                act.wait_ge(s["yT_mm"], c + 1)
                nc.scalar.activation(yT[:, 4 * c:4 * c + 4, :].rearrange("p i t -> p (i t)"), bank[c][:, :],
                                     ACT.Copy).then_inc(s["yT_copied"], 1)
            act.wait_ge(s["gap_ready"], 1)
            nc.scalar.activation(ex[:, :, :], ex[:, :, :], ACT.Exp).then_inc(s["ex_ready"], 1)
            nc.scalar.activation(g[:, 1, :], g[:, 0, :], ACT.Exp).then_inc(s["exp2_done"], 1)

            def tile(i, u):
                for f in range(2):
                    act.wait_ge(s["h_mm"], 2 * i + f + 1)
                    if f == 0:
                        wait(act, s["e_mm"], i - 1)
                    nc.scalar.activation(hid[:, u, f, :], bank[6 + f][:, 0:128], ACT.Silu).then_inc(s["h_done"], 1)

            tile(0, 0)
            tile(1, 1)
            with act.Fori(1, NT // 2) as it:
                for u in range(2):
                    tile(2 * it + u, u)

        @block.vector
        def _(dve):
            nc.vector.memset(ones[:, :], 1.0).then_inc(s["ready"], 1)
            nc.vector.memset(acc[:, :, :], 0.0).then_inc(s["ready"], 1)
            dve.wait_ge(s["brow_mm"], 1)
            nc.vector.tensor_tensor(brow[0:1, :], bank[7][0:1, 0:D], w("bo")[0:1, :], ALU.add).then_inc(s["brow_ready"], 1)
            for c in range(4):
                dve.wait_ge(s["o_mm"], c + 1)
                nc.vector.tensor_tensor(xres[:, 4 * c:4 * c + 4, :], xres[:, 4 * c:4 * c + 4, :],
                                        bank[4 + c % 3][:, :].rearrange("p (i d) -> p i d", d=D),
                                        ALU.add).then_inc(s["x_added"], 1)
            dve.wait_ge(s["x_added"], 4)
            n, step = layer_norm(nc, dve, xres[:, :, :], xc[:, :, :], stats, s, 0)
            step(nc.vector.tensor_tensor(sq[:, :, :], xc[:, :, :], xc[:, :, :], ALU.mult))
            step(nc.vector.tensor_reduce(stats[:, 4, :], sq[:, :, :], AX.X, ALU.add))
            nc.vector.tensor_scalar(stats[:, 2, :], stats[:, 4, :], 1.0 / D, EPS, ALU.mult, ALU.add)\
                .then_inc(s["var_ready"], 1)
            dve.wait_ge(s["std_ready"], 1)
            nc.vector.reciprocal(stats[:, 5, :], stats[:, 3, :]).then_inc(s["rstd"], 1)
            dve.wait_ge(s["rstd"], 1)
            nc.vector.tensor_tensor(xc[:, :, :], xc[:, :, :], last(stats[:, 5, :], D), ALU.mult)\
                .then_inc(s["y_ready"], 1)

            dve.wait_ge(s["lg_mm"], 1)
            nc.vector.tensor_copy(logit[:, :, :], bank[7][:, 0:NT * NE].rearrange("p (i e) -> p i e", e=NE))\
                .then_inc(s["r"], 1)
            dve.wait_ge(s["r"], 1)
            for i in range(NT):
                ins = nc.vector.max(top[:, i, :], logit[:, i, :])
            ins.then_inc(s["r"], 1)
            dve.wait_ge(s["r"], 2)
            for i in range(NT):
                ins = nc.vector.max_index(topi[:, i, :], top[:, i, :], logit[:, i, :])
            step(ins)
            step(nc.vector.tensor_copy(topf[:, :, :], topi[:, :, :]))
            for c in range(2):
                ins = nc.vector.tensor_tensor(hot[:, c, :, :], mid(w("iota"), NT),
                                              topf[:, :, c:c + 1].broadcast_to([128, NT, NE]), ALU.is_equal)
            ins.then_inc(s["r"], 1)
            dve.wait_ge(s["r"], 3)
            step(nc.vector.tensor_tensor(hot[:, 2, :, :], hot[:, 0, :, :], hot[:, 1, :, :], ALU.add))
            nc.vector.tensor_scalar(hot[:, 2, :, :], hot[:, 2, :, :], w("valid"), None, ALU.mult).then_inc(s["r"], 1)
            nc.vector.tensor_tensor(ex[:, :, :], logit[:, :, :], top[:, :, 0:1].broadcast_to([128, NT, NE]), ALU.subtract)
            nc.vector.tensor_tensor(g[:, 0, :].unsqueeze(2), top[:, :, 1:2], top[:, :, 0:1], ALU.subtract)\
                .then_inc(s["gap_ready"], 1)
            dve.wait_ge(s["cum_mm"], 1)
            step(nc.vector.memset(off[:, 0, :], 0.0))
            tot = bank[1][:, 0:NT * NE].rearrange("p (i e) -> p i e", e=NE)
            for i in range(1, NT):
                step(nc.vector.tensor_tensor(off[:, i, :], off[:, i - 1, :], tot[:, i - 1, :], ALU.add))
            step(nc.vector.tensor_tensor(cum[:, :, :], bank[0][:, 0:NT * NE].rearrange("p (i e) -> p i e", e=NE),
                                         off[:, :, :], ALU.add))
            step(nc.vector.tensor_scalar(cum[:, :, :], cum[:, :, :], float(CAPACITY), None, ALU.is_le))
            for c in range(2):
                step(nc.vector.tensor_tensor(sq[:, :, 0:NE], cum[:, :, :], hot[:, c, :, :], ALU.mult))
                step(nc.vector.tensor_reduce(g[:, 2 + c, :], sq[:, :, 0:NE], AX.X, ALU.add))
            dve.wait_ge(s["ex_ready"], 1)
            step(nc.vector.tensor_reduce(g[:, 4, :], ex[:, :, :], AX.X, ALU.add))
            step(nc.vector.reciprocal(g[:, 5, :], g[:, 4, :]))
            dve.wait_ge(s["exp2_done"], 1)
            step(nc.vector.tensor_tensor(g[:, 6, :], g[:, 5, :], g[:, 2, :], ALU.mult))
            step(nc.vector.tensor_tensor(g[:, 7, :], g[:, 5, :], g[:, 1, :], ALU.mult))
            step(nc.vector.tensor_tensor(g[:, 7, :], g[:, 7, :], g[:, 3, :], ALU.mult))
            step(nc.vector.tensor_tensor(g[:, 8, :], g[:, 6, :], g[:, 7, :], ALU.add))
            step(nc.vector.tensor_scalar(g[:, 8, :], g[:, 8, :], 1e-6, None, ALU.add))
            step(nc.vector.reciprocal(g[:, 9, :], g[:, 8, :]))
            step(nc.vector.tensor_tensor(g[:, 6, :], g[:, 6, :], g[:, 9, :], ALU.mult))
            step(nc.vector.tensor_tensor(g[:, 7, :], g[:, 7, :], g[:, 9, :], ALU.mult))
            step(nc.vector.tensor_tensor(comb[:, :, :], hot[:, 0, :, :], last(g[:, 6, :], NE), ALU.mult))
            step(nc.vector.tensor_tensor(sq[:, :, 0:NE], hot[:, 1, :, :], last(g[:, 7, :], NE), ALU.mult))
            nc.vector.tensor_tensor(comb[:, :, :], comb[:, :, :], sq[:, :, 0:NE], ALU.add).then_inc(s["comb_ready"], 1)
            dve.wait_ge(s["comb_ready"], 1)

            def tile(i, u):
                at = bass.ds(i, 1) if not isinstance(i, int) else slice(i, i + 1)
                dve.wait_ge(s["e_mm"], i + 1)
                for e in range(NE):
                    a = acc[:, at, :].rearrange("p i d -> p (i d)")
                    r = xres[:, at, :].rearrange("p i d -> p (i d)")
                    ins = nc.vector.scalar_tensor_tensor(
                        out=a, in0=bank[2 + 2 * u + e // 4][:, 128 * (e % 4):128 * (e % 4) + 128],
                        scalar=comb[:, at, e:e + 1].rearrange("p i e -> p (i e)"), in1=r if e == 0 else a,
                        op0=ALU.mult, op1=ALU.add)
                    if e < NE - 1:
                        ins.then_inc(s["r"], 1)
                        dve.wait_ge(s["r"], 4 + (NE - 1) * i + e + 1)
                    else:
                        ins.then_inc(s["e_done"], 1)

            with dve.Fori(0, NT // 2) as it:
                for u in range(2):
                    tile(2 * it + u, u)

        @block.sync
        def _(sp):
            sp.dma_start(wd[:, :, :], wd_dram).then_inc(s["wd_in"], 16)
            ov = out_dram.rearrange("(i two) t d -> two t i d", two=2)
            for c in range(4):
                sp.wait_ge(s["e_done"], 4 * (c + 1))
                at = slice(4 * c, 4 * c + 4)
                sp.dma_start(ov[0][:, at, :], acc[0:T, at, :]).then_inc(s["out_in"], 16)
                sp.dma_start(ov[1][:, at, :], acc[HALF:HALF + T, at, :]).then_inc(s["out_in"], 16)
            sp.wait_ge(s["out_in"], 16 * 8)


def build(nc, x, ctxT, rot, packed, wd, out):
    with ExitStack() as ctx:
        sb = lambda name, shape, dt=F32: ctx.enter_context(nc.sbuf_tensor(name, shape, dt))
        xres = sb("xres", [128, NT, D])
        qh = sb("qh", [128, B, T])
        oall = sb("oall", [128, NT, D])
        pack = sb("pack", [128, PACK_N])
        q3 = sb("q3", [96, 4, B, T])
        cosk = sb("cosk", [128, S])
        sink = sb("sink", [128, S])
        cx = sb("cx", [128, 2, S])
        kst = sb("kst", [128, 2, 4, S], F32R)
        low = sb("low", [128, B * T])
        shared = {name: ctx.enter_context(nc.semaphore(name)) for name in ("rot_in", "ctx_in0", "ctx_in1")}
        build_self_attention(nc, x, packed, ctxT, rot, pack, xres, oall, qh, cx, cosk, sink, kst, low, shared)
        build_cross_attention(nc, ctxT, pack, qh, q3, oall, cx, cosk, sink, kst, low, shared)
        build_experts(nc, pack, wd, xres, oall, out)


def kernel(x, ctx_1024, L0_attn_Wq, L0_attn_Wk, L0_attn_Wv, L0_attn_Wo, L0_xattn_wq, L0_xattn_bq, L0_xattn_wk,
           L0_xattn_bk, L0_xattn_wv, L0_xattn_bv, L0_xattn_wo, L0_xattn_bo, L0_ffn_w_router, L0_ffn_w_gate,
           L0_ffn_w_down):
    import numpy as np
    import concourse.bacc as bacc
    from concourse.bass_utils import run_bass_kernel_spmd as run

    split = np.array([DH * h + 2 * f + odd for odd in range(2) for h in range(H) for f in range(DH // 2)])

    def tables(length, inverse, factor):
        f32 = np.float32
        base = (np.arange(0, DH, 2, dtype=f32) + f32(0.4 * DH)) / f32(1.4 * DH)
        low = -length // 2
        power = np.arange(low, length + low, dtype=f32) / f32(D)
        scale = base[None, :] ** power[:, None]
        freq = (1.0 / 10000.0 ** (np.arange(DH // 2, dtype=f32) / f32(DH // 2))).astype(f32)
        ang = np.arange(length, dtype=f32)[:, None] * freq[None, :]
        if inverse:
            scale = 1.0 / scale
        cos = (np.cos(ang) * scale * factor).T.astype(f32)
        sin = (np.sin(ang) * scale * factor).T.astype(f32)
        return np.tile(cos, (2 * H, 1)), np.concatenate([np.tile(sin, (H, 1)), -np.tile(sin, (H, 1))])

    cosk, sink = tables(S, True, np.float32(1.0))
    cosq, sinq = tables(T, False, np.float32(DH ** -0.5))
    p = np.arange(128)
    c = {
        "ident": np.eye(128),
        "causal": np.where((np.arange(T)[None, :] > (p % HALF)[:, None]) & ((p % HALF) < T)[:, None], -1e30, 0.0),
        "mask_nat": (p // DH)[:, None] == np.arange(H)[None, :],
        "mask_split": ((p % 64) // 4)[:, None] == np.arange(H)[None, :],
        "mask_stack": ((p % 16) // 4)[:, None] == np.arange(HG)[None, :],
        "mask_m": p[:, None] == np.arange(NG)[None, :],
        "tri": p[:, None] <= p[None, :],
        "valid": ((p % HALF) < T)[:, None],
        "iota": np.broadcast_to(np.arange(NE), (128, NE)),
        "cosq": cosq, "sinq": sinq,
    }
    c = {k: np.asarray(a).astype(np.float32) for k, a in c.items()}
    a = {k: np.asarray(v) for k, v in dict(
        Wq=L0_attn_Wq, Wk=L0_attn_Wk, Wv=L0_attn_Wv, Wo=L0_attn_Wo, xwv=L0_xattn_wv, xwo=L0_xattn_wo,
        wr=L0_ffn_w_router, wg=L0_ffn_w_gate).items()}
    c.update({k: v.T for k, v in a.items()})
    c["xwq"] = np.asarray(L0_xattn_wq).T[:, split]
    c["xwk"] = np.asarray(L0_xattn_wk).T[:, split]
    c["bq"] = np.asarray(L0_xattn_bq)[split][:, None]
    c["bk"] = np.asarray(L0_xattn_bk)[split][:, None]
    c["bv"] = np.asarray(L0_xattn_bv)[:, None]
    c["bo"] = np.broadcast_to(np.asarray(L0_xattn_bo)[None, :], (128, D))
    wd = np.asarray(L0_ffn_w_down).transpose(2, 0, 1).reshape(2, 128, NE * D).transpose(1, 0, 2)
    packed = np.ascontiguousarray(np.concatenate([c[name] for name, _ in PACK], axis=1))

    arrays = {
        "x": np.ascontiguousarray(np.asarray(x)),
        "ctxT": np.ascontiguousarray(np.asarray(ctx_1024).transpose(0, 2, 1)),
        "rot": np.ascontiguousarray(np.stack([cosk, sink])),
        "packed": packed,
        "wd": np.ascontiguousarray(wd),
    }
    nc = bacc.Bacc("TRN2", target_bir_lowering=False, num_devices=1)
    args = [nc.dram_tensor(k, v.shape, mybir.dt.from_np(v.dtype), kind="ExternalInput").ap()
            for k, v in arrays.items()]
    out = nc.dram_tensor("out", (B, T, D), F32, kind="ExternalOutput").ap()
    build(nc, *args, out)
    r = run(nc, [arrays], core_ids=[0])
    return r.results[0]["out"]
```

```python
from contextlib import ExitStack

import concourse.bass as bass
from concourse import mybir

F32 = mybir.dt.float32
F32R = mybir.dt.float32r
U32 = mybir.dt.uint32
ALU = mybir.AluOpType
ACT = mybir.ActivationFunctionType
AX = mybir.AxisListType

B, T, D, H, S = 32, 56, 128, 16, 1500
DH = D // H
NT = B // 2
HALF = 64
HT = H * T
KT, NK = 125, 12
NE, FH = 8, 256
CAPACITY = -(-B * T * 5 // (NE * 4))
KC, NKC = 500, 3
NG = HT // 128
HG = 4
VW = DH + 1
EPS = 1e-5

PACK = [("ident", 128), ("causal", T), ("mask_nat", H), ("mask_split", H), ("mask_stack", HG), ("mask_m", NG),
        ("tri", 128), ("valid", 1), ("iota", NE), ("cosq", T), ("sinq", T),
        ("Wq", D), ("Wk", D), ("Wv", D), ("Wo", D), ("xwq", D), ("xwk", D), ("xwv", D), ("xwo", D),
        ("bq", 1), ("bk", 1), ("bv", 1), ("bo", D), ("wr", NE), ("wg", FH)]
PACK_AT = {}
PACK_N = 0
for _name, _width in PACK:
    PACK_AT[_name] = (PACK_N, PACK_N + _width)
    PACK_N += _width


def wait(eng, sem, value):
    if isinstance(value, int) and value <= 0:
        return
    eng.wait_ge(sem, value)


def mid(ap, n):
    return ap.unsqueeze(1).broadcast_to([ap.shape[0], n, ap.shape[1]])


def last(ap, n):
    return ap.unsqueeze(len(ap.shape)).broadcast_to([*ap.shape, n])


def build_self_attention(nc, x_dram, packed, ctxT, rot, pack, xres, oall, qh, cx, cosk, sink, kst, low, shared):
    with ExitStack() as ctx:
        sb = lambda name, shape, dt=F32: ctx.enter_context(nc.sbuf_tensor(name, shape, dt))
        sem = lambda name: ctx.enter_context(nc.semaphore("a_" + name))
        psum = lambda name, shape: ctx.enter_context(nc.psum_tensor("a_" + name, shape, F32))
        w = lambda name: pack[:, PACK_AT[name][0]:PACK_AT[name][1]]
        ident = w("ident")

        y_bank = psum("y_bank", [128, 512])
        prj_bank = psum("prj_bank", [128, 512])
        s_bank = psum("s_bank", [128, 2, 512])
        p_bank = psum("p_bank", [128, 2, 512])
        pv_bank = psum("pv_bank", [128, 512])
        out_bank = psum("out_bank", [128, 512])

        bn = sb("a_bn", [128, NT, 6])
        mv = sb("a_mv", [128, NT, 2])
        std = sb("a_std", [128, 3, NT])
        ytile = sb("a_ytile", [128, 2, D])
        yT = sb("a_yT", [128, 2, 128])
        prj = sb("a_prj", [128, 2, 256])
        vblk = sb("a_vblk", [128, 2, 2, H // 2, 2, VW])
        kblk = sb("a_kblk", [128, 2, 2, H, T])
        att = sb("a_att", [128, 2, H, HALF])
        top = sb("a_top", [128, H])
        inv = sb("a_inv", [128, H // 2, 2, 1])
        pT = sb("a_pT", [128, H // 2, 128])
        on = sb("a_on", [128, D])
        oT = sb("a_oT", [128, 128])
        y2 = sb("a_y2", [128, NT, D])
        y2T = sb("a_y2T", [128, NT, 128])
        qa = sb("a_qa", [128, B, T])
        qb = sb("a_qb", [128, B, T])
        ql = low[:, :].rearrange("p (b t) -> p b t", t=T)

        names = ("pack_in v_zeroed pool_set zeroed first_in x_in pads bn_done mv_done var_ready std_ready "
                 "rstd_ready ytile_ready yT_mm yT_copied prj_mm prj_copied v_mm v_copied kblk_ready s_mm "
                 "masked max_ready shifted exp_done pT_mm pT_copied pv_mm inv_ready on_ready oT_mm oT_copied "
                 "out_mm x_added y2_ready y2T_mm y2T_copied q_mm q_biased q_cos q_sin q_sum q_high q_low").split()
        s = {name: sem(name) for name in names}
        block = ctx.enter_context(nc.Block())

        def periods(eng, period):
            for p in range(-3, 2):
                period(p, p % 2)
            with eng.Fori(1, NT // 2 - 2) as it:
                for u in range(2):
                    period(2 * it + u, u)
            for p in range(NT - 4, NT + 1):
                period(p, p % 2)

        def has(p):
            return not isinstance(p, int) or 0 <= p < NT

        def tile(p):
            return bass.ds(p, 1) if not isinstance(p, int) else slice(p, p + 1)

        def high(act, c):
            rows = slice(8 * c, 8 * c + 8)
            act.wait_ge(s["q_sum"], c + 1)
            nc.scalar.activation(qh[:, rows, :].bitcast(F32R), qb[:, rows, :], ACT.Copy).then_inc(s["q_high"], 1)

        tail_banks = [s_bank[:, 0, :], s_bank[:, 1, :], prj_bank[:, :], y_bank[:, :]]
        EARLY = 12
        FIRST = 4

        @block.sync
        def _(sp):
            xv = x_dram.rearrange("(i two) t d -> two t i d", two=2)
            sp.wait_ge(s["zeroed"], 2)
            for at, loaded in ((slice(0, FIRST), "first_in"), (slice(FIRST, NT), "x_in")):
                if loaded == "x_in":
                    sp.dma_start(pack[:, :], packed).then_inc(s["pack_in"], 16)
                sp.dma_start(xres[0:T, at, :], xv[0][:, at, :]).then_inc(s[loaded], 16)
                sp.dma_start(xres[HALF:HALF + T, at, :], xv[1][:, at, :]).then_inc(s[loaded], 16)
            sp.dma_start(cosk[:, :], rot[0]).then_inc(shared["rot_in"], 16)
            sp.dma_start(sink[:, :], rot[1]).then_inc(shared["rot_in"], 16)
            sp.dma_start(cx[:, 0, :], ctxT[0]).then_inc(shared["ctx_in0"], 16)
            sp.dma_start(cx[:, 1, :], ctxT[1]).then_inc(shared["ctx_in1"], 16)

        @block.gpsimd
        def _(pool):
            nc.gpsimd.memset(xres[:, NT // 2:NT, :], 0.0).then_inc(s["zeroed"], 1)
            nc.gpsimd.memset(att[:, :, :, :], 0.0).then_inc(s["pads"], 1)
            nc.gpsimd.memset(oall[:, :, :], 0.0).then_inc(s["pool_set"], 1)
            pool.wait_ge(s["pool_set"], 1)
            nc.gpsimd.memset(kst[96:128, :, :, :].bitcast(F32), 1.0).then_inc(s["pool_set"], 1)
            pool.wait_ge(s["pool_set"], 2)
            pool.wait_ge(s["pack_in"], 16)

            def period(p, u):
                q, b = p + 2, u % 2
                if has(q):
                    pool.wait_ge(s["prj_copied"], q + 1)
                    wait(pool, s["s_mm"], 2 * (q - 1))
                    for a in range(2):
                        kT = prj[:, b, 128 + HALF * a:128 + HALF * a + T]
                        nc.gpsimd.tensor_tensor(kblk[:, b, a, :, :], mid(kT, H), last(w("mask_nat"), T),
                                                ALU.mult).then_inc(s["kblk_ready"], 1)

            def cosines(c):
                rows = slice(8 * c, 8 * c + 8)
                pool.wait_ge(s["q_biased"], c + 1)
                nc.gpsimd.tensor_tensor(qb[:, rows, :], qa[:, rows, :], mid(w("cosq"), 8), ALU.mult)\
                    .then_inc(s["q_cos"], 1)

            periods(pool, period)
            for c in range(4):
                cosines(c)

        @block.scalar
        def _(act):
            def root(nth, at):
                act.wait_ge(s["var_ready"], nth)
                nc.scalar.activation(std[:, 1, at], std[:, 0, at], ACT.Sqrt).then_inc(s["std_ready"], 1)

            root(1, slice(0, FIRST))

            def period(p, u):
                z, q, r, o = p + 3, p + 2, p + 1, p - 1
                b, other = u % 2, (u + 1) % 2
                if has(q):
                    act.wait_ge(s["prj_mm"], q + 1)
                    wait(act, s["s_mm"], 2 * (q - 1))
                    wait(act, s["kblk_ready"], 2 * (q - 1))
                    nc.scalar.activation(prj[:, b, :], prj_bank[:, 0:256], ACT.Copy).then_inc(s["prj_copied"], 1)
                if has(o):
                    act.wait_ge(s["oT_mm"], o + 1)
                    wait(act, s["out_mm"], o)
                    nc.scalar.activation(oT[:, :], out_bank[:, 0:128], ACT.Copy).then_inc(s["oT_copied"], 1)
                if isinstance(p, int) and p == NT:
                    root(3, slice(0, EARLY))
                    y2_copy(0)
                    y2_copy(1)
                if has(z):
                    act.wait_ge(s["yT_mm"], z + 1)
                    wait(act, s["v_mm"], z - 1)
                    nc.scalar.activation(yT[:, other, :], y_bank[:, 0:128], ACT.Copy).then_inc(s["yT_copied"], 1)
                    if isinstance(z, int) and z == 0:
                        root(2, slice(FIRST, NT))
                if has(p):
                    wait(act, s["pv_mm"], p)
                    for c in range(2):
                        act.wait_ge(s["pT_mm"], 2 * p + c + 1)
                        nc.scalar.activation(pT[:, 4 * c:4 * c + 4, :].rearrange("p h t -> p (h t)"),
                                             p_bank[:, c, :], ACT.Copy).then_inc(s["pT_copied"], 1)
                if has(r):
                    act.wait_ge(s["shifted"], r + 1)
                    a = att[:, other, :, 0:T]
                    nc.scalar.activation(a, a, ACT.Exp, scale=float(DH) ** -0.5).then_inc(s["exp_done"], 1)
                if has(q):
                    act.wait_ge(s["v_mm"], q + 1)
                    wait(act, s["pv_mm"], q - 1)
                    for a in range(2):
                        for odd in range(2):
                            ins = nc.scalar.activation(
                                vblk[HALF * odd:HALF * odd + T, b, a, :, odd, 0:DH],
                                y_bank[HALF * a:HALF * a + T, 128:256]
                                .rearrange("p (j two d) -> p j two d", two=2, d=DH)[:, :, odd, :], ACT.Copy)
                    ins.then_inc(s["v_copied"], 1)

            def y2_copy(c):
                act.wait_ge(s["y2T_mm"], c + 1)
                nc.scalar.activation(y2T[:, 4 * c:4 * c + 4, :].rearrange("p i t -> p (i t)"), tail_banks[c % 2],
                                     ACT.Copy).then_inc(s["y2T_copied"], 1)

            def queries(c):
                act.wait_ge(s["q_mm"], c + 1)
                nc.scalar.activation(qa[:, 8 * c:8 * c + 8, :],
                                     tail_banks[2 + c % 2].rearrange("p (b t) -> p b t", t=HALF)[:, :, 0:T],
                                     ACT.Identity, bias=w("bq")).then_inc(s["q_biased"], 1)

            periods(act, period)
            root(4, slice(EARLY, NT))
            queries(0)
            y2_copy(2)
            queries(1)
            high(act, 0)
            y2_copy(3)
            queries(2)
            high(act, 1)
            queries(3)
            high(act, 2)
            high(act, 3)

        @block.tensor
        def _(pe):
            pe.wait_ge(s["pack_in"], 16)

            def period(p, u):
                z, q, r, o = p + 3, p + 2, p + 1, p - 1
                b, other = u % 2, (u + 1) % 2
                if has(q):
                    pe.wait_ge(s["yT_copied"], q + 1)
                    wait(pe, s["prj_copied"], q)
                    nc.tensor.matmul(prj_bank[:, 0:128], w("Wq"), yT[:, b, :], start=True, stop=True)
                    nc.tensor.matmul(prj_bank[:, 128:256], w("Wk"), yT[:, b, :], start=True, stop=True)\
                        .then_inc(s["prj_mm"], 1)
                if has(r):
                    if isinstance(r, int) and r == 0:
                        pe.wait_ge(s["pads"], 2)
                    wait(pe, s["masked"], r)
                    for hh in range(2):
                        for a in range(2):
                            if hh == 0:
                                pe.wait_ge(s["kblk_ready"], 2 * r + a + 1)
                            ins = nc.tensor.matmul(
                                s_bank[HALF * a:HALF * a + T, hh, 0:HT // 2],
                                prj[:, other, HALF * a:HALF * a + T],
                                kblk[:, other, a, 8 * hh:8 * hh + 8, :].rearrange("p h t -> p (h t)"),
                                start=True, stop=True)
                        ins.then_inc(s["s_mm"], 1)
                if has(q):
                    wait(pe, s["v_copied"], q)
                    nc.tensor.matmul(y_bank[:, 128:256], yT[:, b, :], w("Wv"), start=True, stop=True)\
                        .then_inc(s["v_mm"], 1)
                if has(o):
                    pe.wait_ge(s["on_ready"], o + 1)
                    wait(pe, s["x_added"], o)
                    nc.tensor.transpose(out_bank[:, 0:128], on[:, :], ident).then_inc(s["oT_mm"], 1)
                if isinstance(p, int) and p == NT:
                    transposes(0)
                    transposes(1)
                if has(z):
                    pe.wait_ge(s["ytile_ready"], z + 1)
                    wait(pe, s["yT_copied"], z)
                    nc.tensor.transpose(y_bank[:, 0:128], ytile[:, other, :], ident).then_inc(s["yT_mm"], 1)
                if has(p):
                    pe.wait_ge(s["exp_done"], p + 1)
                    wait(pe, s["pT_copied"], 2 * p)
                    for h in range(H // 2):
                        ins = nc.tensor.transpose(p_bank[:, h // 4, 128 * (h % 4):128 * (h % 4) + 128],
                                                  att[:, b, 2 * h:2 * h + 2, :].rearrange("p h t -> p (h t)"), ident)
                        if h % 4 == 3:
                            ins.then_inc(s["pT_mm"], 1)
                if has(o):
                    pe.wait_ge(s["oT_copied"], o + 1)
                    nc.tensor.matmul(out_bank[:, 128:256], oT[:, :], w("Wo"), start=True, stop=True)\
                        .then_inc(s["out_mm"], 1)
                if has(p):
                    pe.wait_ge(s["v_copied"], p + 1)
                    wait(pe, s["on_ready"], p)
                    for j in range(H // 2):
                        if j % 4 == 0:
                            pe.wait_ge(s["pT_copied"], 2 * p + j // 4 + 1)
                        for a in range(2):
                            ins = nc.tensor.matmul(pv_bank[HALF * a:HALF * a + T, 2 * VW * j:2 * VW * (j + 1)],
                                                   pT[:, j, HALF * a:HALF * a + T],
                                                   vblk[:, b, a, j, :, :].rearrange("p o d -> p (o d)"),
                                                   start=True, stop=True)
                    ins.then_inc(s["pv_mm"], 1)

            def transposes(c):
                pe.wait_ge(s["y2_ready"], c + 1)
                if c >= 2:
                    pe.wait_ge(s["y2T_copied"], c - 1)
                for j in range(4):
                    ins = nc.tensor.transpose(tail_banks[c % 2][:, 128 * j:128 * j + 128], y2[:, 4 * c + j, :], ident)
                ins.then_inc(s["y2T_mm"], 1)

            def queries(c):
                pe.wait_ge(s["y2T_copied"], c + 1)
                if c >= 2:
                    pe.wait_ge(s["q_biased"], c - 1)
                else:
                    pe.wait_ge(s["v_copied"], NT)
                nc.tensor.matmul(tail_banks[2 + c % 2], w("xwq"),
                                 y2T[:, 4 * c:4 * c + 4, :].rearrange("p i t -> p (i t)"),
                                 start=True, stop=True).then_inc(s["q_mm"], 1)

            periods(pe, period)
            queries(0)
            transposes(2)
            queries(1)
            queries(2)
            transposes(3)
            queries(3)

        @block.vector
        def _(dve):
            nc.vector.memset(xres[:, 0:NT // 2, :], 0.0).then_inc(s["zeroed"], 1)
            nc.vector.memset(vblk[:, :, :, :, :, :], 0.0).then_inc(s["v_zeroed"], 1)
            dve.wait_ge(s["v_zeroed"], 1)
            for odd in range(2):
                nc.vector.memset(vblk[HALF * odd:HALF * odd + T, :, :, :, odd, DH:VW], 1.0)
            nc.vector.memset(s_bank[:, :, :], 0.0)
            pv = pv_bank[:, 0:H * VW].rearrange("p (j o d) -> p j o d", o=2, d=VW)
            nc.vector.memset(pv[:, :, :, 0:DH], 0.0)
            nc.vector.memset(pv[:, :, :, DH:VW], 1.0).then_inc(s["pads"], 1)

            def inverse_std(nth, added, tiles):
                dve.wait_ge(s["bn_done"], added)
                at = slice(tiles[0], tiles[-1] + 1)
                for i in tiles:
                    ins = nc.vector.bn_aggr(mv[:, i, :], bn[:, i, :])
                ins.then_inc(s["mv_done"], 1)
                dve.wait_ge(s["mv_done"], nth)
                nc.vector.tensor_scalar(std[:, 0, at], mv[:, at, 1], EPS, None, ALU.add).then_inc(s["var_ready"], 1)
                dve.wait_ge(s["std_ready"], nth)
                nc.vector.reciprocal(std[:, 2, at], std[:, 1, at]).then_inc(s["rstd_ready"], 1)
                dve.wait_ge(s["rstd_ready"], nth)

            def first_stats(nth, tiles):
                for i in tiles:
                    nc.vector.bn_stats(bn[:, i, :], xres[:, i, :]).then_inc(s["bn_done"], 1)
                inverse_std(nth, tiles[-1] + 1, tiles)

            dve.wait_ge(s["first_in"], 32)
            first_stats(1, range(FIRST))

            def normalise(out, i):
                flat = lambda ap: ap.rearrange("p i d -> p (i d)")
                return nc.vector.tensor_scalar(out, flat(xres[:, tile(i), :]), flat(mv[:, tile(i), 0:1]),
                                               std[:, 2, tile(i)], ALU.subtract, ALU.mult)

            def period(p, u):
                z, r, o = p + 3, p + 1, p - 1
                b, other = u % 2, (u + 1) % 2
                if has(o):
                    dve.wait_ge(s["pv_mm"], o + 1)
                    nc.vector.reciprocal(inv[:, :, :, :], pv[:, :, :, DH:VW]).then_inc(s["inv_ready"], 1)
                    dve.wait_ge(s["inv_ready"], o + 1)
                    wait(dve, s["oT_mm"], o)
                    nc.vector.tensor_tensor(on[:, :].rearrange("p (j o d) -> p j o d", o=2, d=DH),
                                            pv[:, :, :, 0:DH], inv[:, :, :, :].broadcast_to([128, H // 2, 2, DH]),
                                            ALU.mult).then_inc(s["on_ready"], 1)
                if isinstance(p, int) and p == NT:
                    inverse_std(3, NT + EARLY, range(EARLY))
                    second_norm(range(8))
                if has(z):
                    wait(dve, s["yT_mm"], z - 1)
                    normalise(ytile[:, other, :], z).then_inc(s["ytile_ready"], 1)
                    if isinstance(z, int) and z == 0:
                        dve.wait_ge(s["x_in"], 32)
                        first_stats(2, range(FIRST, NT))
                if has(r):
                    wait(dve, s["pT_mm"], 2 * (r - 1))
                    a = att[:, other, :, 0:T]
                    if isinstance(r, int) and r == 0:
                        dve.wait_ge(s["pads"], 2)
                    for hh in range(2):
                        dve.wait_ge(s["s_mm"], 2 * r + hh + 1)
                        ins = nc.vector.tensor_tensor(
                            a[:, 8 * hh:8 * hh + 8, :], s_bank[:, hh, 0:HT // 2].rearrange("p (h t) -> p h t", t=T),
                            mid(w("causal"), 8), ALU.add)
                    ins.then_inc(s["masked"], 1)
                    dve.wait_ge(s["masked"], r + 1)
                    nc.vector.tensor_reduce(top[:, :], a, AX.X, ALU.max).then_inc(s["max_ready"], 1)
                    dve.wait_ge(s["max_ready"], r + 1)
                    nc.vector.tensor_tensor(a, a, last(top[:, :], T), ALU.subtract).then_inc(s["shifted"], 1)
                if has(o):
                    dve.wait_ge(s["out_mm"], o + 1)
                    x = xres[:, tile(o), :]
                    nc.vector.tensor_tensor(x, x, out_bank[:, 128:256].unsqueeze(1), ALU.add)\
                        .then_inc(s["x_added"], 1)
                    dve.wait_ge(s["x_added"], o + 1)
                    nc.vector.bn_stats(bn[:, tile(o), :].rearrange("p i n -> p (i n)"),
                                       x.rearrange("p i d -> p (i d)")).then_inc(s["bn_done"], 1)

            sinq, lo, hi = w("sinq"), slice(0, 64), slice(64, 128)

            def low_part(c):
                rows = slice(8 * c, 8 * c + 8)
                dve.wait_ge(s["q_high"], c + 1)
                nc.vector.tensor_tensor(ql[:, rows, :], qb[:, rows, :], qh[:, rows, :], ALU.subtract)\
                    .then_inc(s["q_low"], 1)

            def rotate(c):
                rows = slice(8 * c, 8 * c + 8)
                dve.wait_ge(s["q_biased"], c + 1)
                nc.vector.tensor_tensor(ql[lo, rows, :], qa[hi, rows, :], mid(sinq[hi], 8), ALU.mult)
                nc.vector.tensor_tensor(ql[hi, rows, :], qa[lo, rows, :], mid(sinq[lo], 8), ALU.mult)\
                    .then_inc(s["q_sin"], 1)
                dve.wait_ge(s["q_sin"], c + 1)
                dve.wait_ge(s["q_cos"], c + 1)
                nc.vector.tensor_tensor(qb[:, rows, :], qb[:, rows, :], ql[:, rows, :], ALU.add)\
                    .then_inc(s["q_sum"], 1)

            def second_norm(tiles):
                for i in tiles:
                    ins = normalise(y2[:, i, :], i)
                    if i % 4 == 3:
                        ins.then_inc(s["y2_ready"], 1)

            periods(dve, period)
            second_norm(range(8, EARLY))
            inverse_std(4, NT + NT, range(EARLY, NT))
            second_norm(range(EARLY, NT))
            for c in range(4):
                rotate(c)
                if c > 0:
                    low_part(c - 1)
            low_part(3)


def build_cross_attention(nc, ctxT, pack, qh, q3, oall, cx, cosk, sink, kst, low, shared):
    with ExitStack() as ctx:
        sb = lambda name, shape, dt=F32: ctx.enter_context(nc.sbuf_tensor(name, shape, dt))
        sem = lambda name: ctx.enter_context(nc.semaphore("b_" + name))
        psum = lambda name, shape: ctx.enter_context(nc.psum_tensor("b_" + name, shape, F32))
        w = lambda name: pack[:, PACK_AT[name][0]:PACK_AT[name][1]]
        ident = w("ident")

        max_bank = psum("max_bank", [128, 2, 512])
        exp_bank = psum("exp_bank", [128, 3, 512])
        o_bank = psum("o_bank", [128, 2, 2 * T])
        v_bank = psum("v_bank", [128, 512])
        k_bank = psum("k_bank", [128, 512])

        kb = sb("b_kb", [128, S])
        kr = sb("b_kr", [128, S])
        ks = sb("b_ks", [128, S])
        kh = sb("b_kh", [128, 2, S], F32R)
        kl = low[:, 0:S].bitcast(F32R)
        ql = low[:, :].rearrange("p (b t) -> p b t", t=T)
        v = sb("b_v", [KT, 2, NK, H, VW])
        prob = sb("b_prob", [KT, 3, HT])
        qblk = sb("b_qblk", [128, 2, HT], F32R)
        qst = sb("b_qst", [128, 2, HT], F32R)
        part = sb("b_part", [128, NG, NKC])
        mx = sb("b_mx", [128, NG])
        osb = sb("b_osb", [128, 2, 2, HALF])
        inv = sb("b_inv", [128, 2, 4, 1])

        names = ("q3_in q3_low_in kl_in kst_in0 kst_in1 ones_ready k_mm k_copied v_mm v_copied cos_done sin_done k_sum "
                 "kh_done kl_done qblk_ready qst_ready maxs_mm chunk_max max_ready mT_mm row_ready s_mm exp_done pv_mm "
                 "o_copied oT_mm inv_ready o_ready").split()
        s = {name: sem(name) for name in names}
        s.update(shared)
        kst_in, ctx_in = [s["kst_in0"], s["kst_in1"]], [s["ctx_in0"], s["ctx_in1"]]
        HDMA, LDMA = 16 * 16, 16 * 8
        NS, NM = 2 * NK, NG * NKC
        block = ctx.enter_context(nc.Block())

        def periods(eng, period):
            for n in range(-2, 2):
                period(n, n % 2, n // 2)
            with eng.Fori(1, B // 2 - 1) as it:
                for u in range(2):
                    period(2 * it + u, u, it)
            for n in range(B - 2, B + 1):
                period(n, n % 2, n // 2)

        def has(n):
            return not isinstance(n, int) or 0 <= n < B

        def row(n):
            return bass.ds(n, 1) if not isinstance(n, int) else slice(n, n + 1)

        @block.sync
        def _(sp):
            for quad, src in ((2, ql), (0, qh), (1, qh)):
                stacked = s["q3_low_in"] if quad == 2 else s["q3_in"]
                for half in range(2):
                    for g in range(4):
                        at = slice(64 * half + 16 * g, 64 * half + 16 * g + 16)
                        dst = slice(32 * quad + 16 * half, 32 * quad + 16 * half + 16)
                        sp.dma_start(q3[dst, g, :, :], src[at, :, :]).then_inc(stacked, 16)

            def period(n, u, it):
                m, o = n + 1, 1 - u
                if has(n + 3):
                    nxt = ctxT[n + 3] if isinstance(n, int) else \
                        ctxT[bass.ds(sp.snap(n + 3), 1)].rearrange("o p s -> (o p) s")
                made, used = 4 * m + 1, 3 * (m + 1)
                if not isinstance(n, int):
                    made, used = sp.snap(made), sp.snap(used)
                if has(m):
                    if isinstance(m, int) and m == 0:
                        sp.wait_ge(s["kh_done"], NKC)
                    else:
                        sp.wait_ge(s["qst_ready"], made)
                    parts = [("l", (32,)), ("h", (0, 64))]
                    if isinstance(m, int) and m == 0:
                        parts.reverse()
                    for part_, dsts in parts:
                        src = kh[:, o, :] if part_ == "h" else kl
                        if part_ == "l" and isinstance(m, int) and m == 0:
                            sp.wait_ge(s["kl_done"], 1)
                        for half in range(2):
                            for g in range(4):
                                at = slice(64 * half + 16 * g, 64 * half + 16 * g + 16)
                                for d in dsts:
                                    sp.dma_start(kst[d + 16 * half:d + 16 * half + 16, o, g, :].bitcast(F32),
                                                 src[at, :].bitcast(F32))\
                                        .then_inc(kst_in[o] if part_ == "h" else s["kl_in"], 16)
                if has(n + 3) and (not isinstance(n, int) or n >= -1):
                    sp.wait_ge(s["v_mm"], used)
                    sp.wait_ge(s["k_mm"], used)
                    sp.dma_start(cx[:, o, :], nxt).then_inc(ctx_in[o], 16)

            for n in range(-2, 2):
                period(n, n % 2, n // 2)
            with sp.Fori(1, B // 2 - 2) as it:
                for u in range(2):
                    period(2 * it + u, u, it)
            for n in range(B - 4, B):
                period(n, n % 2, n // 2)

        @block.gpsimd
        def _(pool):
            pool.wait_ge(s["rot_in"], 32)

            def block_queries(n, b):
                wait(pool, s["maxs_mm"], NM * (n - 1))
                nc.gpsimd.tensor_tensor(qblk[:, b, :].rearrange("p (h t) -> p h t", t=T),
                                        qh[:, row(n), :].broadcast_to([128, H, T]),
                                        last(w("mask_split"), T), ALU.mult).then_inc(s["qblk_ready"], 1)

            def period(n, u, it):
                m, k, o = n + 1, n + 2, 1 - u
                if has(m):
                    if isinstance(m, int) and m == 0:
                        pool.wait_ge(s["q3_in"], 16 * 16)
                    wait(pool, s["s_mm"], NS * (m - 1))
                    for g in range(4):
                        nc.gpsimd.tensor_tensor(
                            qst[0:96, o, HG * T * g:HG * T * (g + 1)].rearrange("p (h t) -> p h t", t=T),
                            q3[:, g, row(m), :].broadcast_to([96, HG, T]),
                            last(w("mask_stack")[0:96], T), ALU.mult).then_inc(s["qst_ready"], 1)
                if has(k):
                    wait(pool, s["kl_done"], k)
                    wait(pool, s["kh_done"], NKC * k)
                    for q in range(NKC):
                        at = slice(KC * q, KC * (q + 1))
                        pool.wait_ge(s["k_copied"], NKC * k + q + 1)
                        nc.gpsimd.tensor_tensor(kr[:, at], kb[:, at], cosk[:, at], ALU.mult)\
                            .then_inc(s["cos_done"], 1)
                        pool.wait_ge(s["cos_done"], NKC * k + q + 1)
                        pool.wait_ge(s["sin_done"], NKC * k + q + 1)
                        nc.gpsimd.tensor_tensor(kr[:, at], kr[:, at], ks[:, at], ALU.add).then_inc(s["k_sum"], 1)
                    block_queries(k, u)
                    pool.wait_ge(s["kh_done"], NKC * (k + 1))
                    wait(pool, s["kl_in"], LDMA * k)
                    if isinstance(k, int) and k == 0:
                        pool.wait_ge(s["q3_low_in"], 16 * 8)
                    nc.gpsimd.tensor_tensor(kl[:, :], kr[:, :], kh[:, u, :].bitcast(F32), ALU.subtract)\
                        .then_inc(s["kl_done"], 1)

            periods(pool, period)

        V_SLOT = {1: 0, 3: 1, 5: 2}
        K_SLOT = {0: 0, 2: 1, 4: 2}
        M_COUNT = [3, 2, 3, 2, 3, 2, 2, 2, 2]
        M_SLOT = [range(sum(M_COUNT[:i]), sum(M_COUNT[:i + 1])) for i in range(len(M_COUNT))]
        SIN_SLOT = {1: 0, 3: 1, 5: 2}
        HIGH_SLOT = {3: 0, 5: 1, 7: 2}
        ROW_SLOT = 9

        @block.scalar
        def _(act):
            def period(n, u, it):
                m, k, o = n + 1, n + 2, 1 - u
                for kt in range(NK):
                    if has(n):
                        wait(act, s["pv_mm"], NK * n + kt - 2)
                        for hh in range(2):
                            c = NS * n + 2 * kt + hh
                            act.wait_ge(s["s_mm"], c + 1)
                            nc.scalar.activation(prob[:, kt % 3, HT // 2 * hh:HT // 2 * (hh + 1)],
                                                 exp_bank[0:KT, (2 * kt + hh) % 3, 0:HT // 2],
                                                 ACT.Exp).then_inc(s["exp_done"], 1)
                    if kt == 0 and has(n - 1):
                        act.wait_ge(s["pv_mm"], NK * n)
                        wait(act, s["oT_mm"], n - 1)
                        nc.scalar.activation(osb[:, :, :, 0:T].rearrange("p j a t -> p (j a) t"),
                                             o_bank[:, :, :].rearrange("p j (a t) -> p (j a) t", t=T),
                                             ACT.Copy).then_inc(s["o_copied"], 1)
                    if kt in V_SLOT and has(m):
                        q = V_SLOT[kt]
                        act.wait_ge(s["v_mm"], 3 * m + q + 1)
                        wait(act, s["pv_mm"], NK * n)
                        if q == 0 and isinstance(n, int) and n <= 0:
                            act.wait_ge(s["ones_ready"], 1)
                        nc.scalar.activation(
                            v[:, o, 4 * q:4 * q + 4, :, 0:DH].rearrange("p k h d -> p (k h) d"),
                            v_bank[0:KT, :].rearrange("p (kh d) -> p kh d", d=DH), ACT.Copy).then_inc(s["v_copied"], 1)
                    if kt in K_SLOT and has(k):
                        q = K_SLOT[kt]
                        act.wait_ge(s["k_mm"], 3 * k + q + 1)
                        wait(act, s["cos_done"], NKC * (k - 1) + q + 1)
                        wait(act, s["sin_done"], NKC * (k - 1) + q + 1)
                        nc.scalar.activation(kb[:, KC * q:KC * (q + 1)], k_bank[:, 0:KC], ACT.Identity,
                                             bias=w("bk")).then_inc(s["k_copied"], 1)
                    if kt in HIGH_SLOT and has(k):
                        q = HIGH_SLOT[kt]
                        act.wait_ge(s["k_sum"], NKC * k + q + 1)
                        wait(act, s["maxs_mm"], NM * (k - 1))
                        wait(act, kst_in[u], HDMA * (it + 1))
                        nc.scalar.activation(kh[:, u, KC * q:KC * (q + 1)], kr[:, KC * q:KC * (q + 1)],
                                             ACT.Copy).then_inc(s["kh_done"], 1)

            periods(act, period)

        @block.tensor
        def _(pe):
            def products(n, u, kt):
                pe.wait_ge(s["exp_done"], NS * n + 2 * kt + 2)
                if kt == 0:
                    if isinstance(n, int) and n == 0:
                        pe.wait_ge(s["ones_ready"], 1)
                    pe.wait_ge(s["v_copied"], 3 * (n + 1))
                    wait(pe, s["o_copied"], n)
                for j in range(H // 2):
                    ins = nc.tensor.matmul(
                        o_bank[32 * (j % 4):32 * (j % 4) + 2 * VW, j // 4, 0:2 * T],
                        v[:, u, kt, 2 * j:2 * j + 2, :].rearrange("p h d -> p (h d)"),
                        prob[:, kt % 3, 2 * T * j:2 * T * (j + 1)],
                        start=(kt == 0 and j < 4), stop=(kt == NK - 1), skip_group_check=True)
                ins.then_inc(s["pv_mm"], 1)

            def period(n, u, it):
                m, k, o = n + 1, n + 2, 1 - u

                def maxima(c):
                    q, g = divmod(c, NG)
                    if c == 0:
                        pe.wait_ge(s["qblk_ready"], m + 1)
                    if g == 0:
                        pe.wait_ge(s["kh_done"], NKC * m + q + 1)
                    wait(pe, s["chunk_max"], NM * m + c - 1)
                    nc.tensor.matmul(max_bank[:, (o + c) % 2, 0:KC], qblk[:, o, 128 * g:128 * g + 128],
                                     kh[:, o, KC * q:KC * (q + 1)], start=True, stop=True)\
                        .then_inc(s["maxs_mm"], 1)

                for kt in range(NK):
                    chunks = list(M_SLOT[kt]) if kt < len(M_SLOT) and has(m) else []
                    if has(n):
                        if kt == 0:
                            pe.wait_ge(s["qst_ready"], 4 * (n + 1))
                            pe.wait_ge(s["row_ready"], n + 1)
                            pe.wait_ge(kst_in[u], HDMA * (it + 1))
                            pe.wait_ge(s["kl_in"], LDMA * (n + 1))
                        for hh in range(2):
                            wait(pe, s["exp_done"], NS * n + 2 * kt + hh - 2)
                            for g in range(2 * hh, 2 * hh + 2):
                                ins = nc.tensor.matmul(
                                    exp_bank[0:KT, (2 * kt + hh) % 3, HG * T * (g % 2):HG * T * (g % 2 + 1)],
                                    kst[:, u, g, KT * kt:KT * (kt + 1)], qst[:, u, HG * T * g:HG * T * (g + 1)],
                                    start=True, stop=True)
                            ins.then_inc(s["s_mm"], 1)
                            if chunks:
                                maxima(chunks.pop(0))
                        if kt > 0:
                            products(n, u, kt - 1)
                    if kt == 0 and has(n - 1):
                        products(n - 1, o, NK - 1)
                    for c in chunks:
                        maxima(c)
                    if kt in V_SLOT and has(m):
                        q = V_SLOT[kt]
                        if q == 0:
                            pe.wait_ge(ctx_in[o], 16 * ((it + u) + 1))
                            wait(pe, s["row_ready"], m)
                        wait(pe, s["v_copied"], 3 * m + q)
                        for j in range(4):
                            ins = nc.tensor.matmul(v_bank[0:KT, 128 * j:128 * j + 128],
                                                   cx[:, o, KT * (4 * q + j):KT * (4 * q + j + 1)], w("xwv"),
                                                   start=True, stop=True)
                        ins.then_inc(s["v_mm"], 1)
                    if kt in K_SLOT and has(k):
                        q = K_SLOT[kt]
                        if q == 0:
                            pe.wait_ge(ctx_in[u], 16 * (it + 2))
                            wait(pe, s["o_ready"], n - 1)
                        wait(pe, s["k_copied"], 3 * k + q)
                        nc.tensor.matmul(k_bank[:, 0:KC], w("xwk"), cx[:, u, KC * q:KC * (q + 1)],
                                         start=True, stop=True).then_inc(s["k_mm"], 1)
                    if kt == 6 and has(n - 1):
                        pe.wait_ge(s["o_copied"], n)
                        wait(pe, s["k_copied"], min_rows(n))
                        wait(pe, s["o_ready"], n - 1)
                        for j in range(2):
                            ins = nc.tensor.transpose(k_bank[:, 128 * j:128 * j + 128],
                                                      osb[:, j, :, :].rearrange("p a t -> p (a t)"), ident)
                        ins.then_inc(s["oT_mm"], 1)
                    if kt == ROW_SLOT and has(m):
                        pe.wait_ge(s["max_ready"], m + 1)
                        pe.wait_ge(s["v_copied"], 3 * (m + 1))
                        nc.tensor.transpose(v_bank[0:NG, 0:128], mx[:, :], ident).then_inc(s["mT_mm"], 1)

            def min_rows(n):
                return min(3 * (n + 3), 3 * B) if isinstance(n, int) else 3 * (n + 3)

            periods(pe, period)

        @block.vector
        def _(dve):
            nc.vector.memset(v[:, :, :, :, DH:VW], 1.0)
            nc.vector.memset(qst[96:128, :, :].bitcast(F32), 0.0)
            nc.vector.memset(osb[:, :, :, :], 0.0)
            nc.vector.memset(o_bank[:, :, :], 0.0).then_inc(s["ones_ready"], 1)
            dve.wait_ge(s["rot_in"], 32)
            lo, hi = slice(0, 64), slice(64, 128)

            def period(n, u, it):
                m, k, o = n + 1, n + 2, 1 - u
                for kt in range(NK):
                    if kt < len(M_SLOT) and has(m):
                        if kt == 0:
                            wait(dve, s["max_ready"], m)
                        for c in M_SLOT[kt]:
                            dve.wait_ge(s["maxs_mm"], NM * m + c + 1)
                            nc.vector.tensor_reduce(part[:, c % NG, c // NG:c // NG + 1],
                                                    max_bank[:, (o + c) % 2, 0:KC], AX.X, ALU.max)\
                                .then_inc(s["chunk_max"], 1)
                    if kt in SIN_SLOT and has(k):
                        q = SIN_SLOT[kt]
                        at = slice(KC * q, KC * (q + 1))
                        dve.wait_ge(s["k_copied"], NKC * k + q + 1)
                        wait(dve, s["k_sum"], NKC * (k - 1) + q + 1)
                        nc.vector.tensor_tensor(ks[lo, at], kb[hi, at], sink[hi, at], ALU.mult)
                        nc.vector.tensor_tensor(ks[hi, at], kb[lo, at], sink[lo, at], ALU.mult)\
                            .then_inc(s["sin_done"], 1)
                    if kt == ROW_SLOT and has(m):
                        dve.wait_ge(s["chunk_max"], NM * (m + 1))
                        wait(dve, s["mT_mm"], m)
                        nc.vector.tensor_reduce(mx[:, :], part[:, :, :], AX.X, ALU.max, negate=True)\
                            .then_inc(s["max_ready"], 1)
                    if kt == ROW_SLOT and has(n - 1):
                        dve.wait_ge(s["oT_mm"], n)
                        for a in range(2):
                            ov = k_bank[HALF * a:HALF * a + T, 0:256].rearrange("p (j q r) -> p j q r", j=2, r=32)
                            nc.vector.reciprocal(inv[HALF * a:HALF * a + T, :, :, :],
                                                 ov[:, :, :, VW * a + DH:VW * a + VW]).then_inc(s["inv_ready"], 1)
                        dve.wait_ge(s["inv_ready"], 2 * n)
                        dst = oall[HALF * o:HALF * o + T, row_tile(n - 1, it, u), :]\
                            .rearrange("p i (j q a d) -> p (i j) q a d", j=2, a=2, d=DH)
                        for a in range(2):
                            ov = k_bank[HALF * a:HALF * a + T, 0:256].rearrange("p (j q r) -> p j q r", j=2, r=32)
                            ins = nc.vector.tensor_tensor(dst[:, :, :, a, :], ov[:, :, :, VW * a:VW * a + DH],
                                                          inv[HALF * a:HALF * a + T, :, :, :]
                                                          .broadcast_to([T, 2, 4, DH]), ALU.mult)
                        ins.then_inc(s["o_ready"], 1)
                    if kt == ROW_SLOT and has(m):
                        dve.wait_ge(s["mT_mm"], m + 1)
                        wait(dve, s["s_mm"], NS * (m - 1))
                        nc.vector.tensor_tensor(qst[96:96 + NG, o, :].rearrange("p (g r) -> p g r", r=128),
                                                mid(v_bank[0:NG, 0:128], NG), last(w("mask_m")[0:NG], 128),
                                                ALU.mult).then_inc(s["row_ready"], 1)

            def row_tile(n, it, u):
                t = it if u == 1 else it - 1
                return bass.ds(t, 1) if not isinstance(t, int) else slice(t, t + 1)

            periods(dve, period)


def build_experts(nc, pack, wd_dram, xres, oall, out_dram):
    with ExitStack() as ctx:
        sb = lambda name, shape, dt=F32: ctx.enter_context(nc.sbuf_tensor(name, shape, dt))
        sem = lambda name: ctx.enter_context(nc.semaphore("c_" + name))
        bank = [ctx.enter_context(nc.psum_tensor(f"c_bank{i}", [128, 512], F32)) for i in range(8)]
        w = lambda name: pack[:, PACK_AT[name][0]:PACK_AT[name][1]]
        ident = w("ident")
        NC, CT = 4, NT // 4
        O_BANK = [bank[4 + c % 3] for c in range(NC)]
        H_BANK = [bank[2 + k % 4] for k in range(2 * NC)]
        E_BANK = [[bank[6], bank[7]], [bank[2], bank[3]]]

        oT = sb("c_oT", [128, NT, 128])
        bias = sb("c_bias", [128, D])
        bn = sb("c_bn", [128, NT, 6])
        mv = sb("c_mv", [128, NT, 2])
        std = sb("c_std", [128, 3, NT])
        y = sb("c_y", [128, NT, D])
        yT = sb("c_yT", [128, NT, 128])
        brow = sb("c_brow", [1, D])
        ones = sb("c_ones", [128, 128])
        logit = sb("c_logit", [128, NT, NE])
        top = sb("c_top", [128, NT, 8])
        topi = sb("c_topi", [128, NT, 8], U32)
        topf = sb("c_topf", [128, NT, 8])
        hot = sb("c_hot", [128, 3, NT, NE])
        ex = sb("c_ex", [128, NT, NE])
        off = sb("c_off", [128, 2, NT, NE])
        cum = sb("c_cum", [128, NT, NE])
        kept = sb("c_kept", [128, 2, NT, NE])
        gate = sb("c_gate", [128, 2, NT])
        keep = sb("c_keep", [128, 2, NT])
        den = sb("c_den", [128, 3, NT])
        comb = sb("c_comb", [128, NT, NE])
        wd = sb("c_wd", [128, 2, NE * D])
        wdh = sb("c_wdh", [128, 2, NE * D], F32R)
        wdl = sb("c_wdl", [128, 2, NE * D], F32R)
        hid = sb("c_hid", [128, 2, NT, 128])
        hidh = sb("c_hidh", [128, 2, 2, 128], F32R)
        hidl = sb("c_hidl", [128, 2, 2, 128], F32R)
        acc = sb("c_acc", [128, NT, D])
        odd_acc = sb("c_odd_acc", [128, 2, D])

        names = ("ones_ready brow_mm brow_ready bias_mm bias_copied bias_added oT_mm oT_copied o_mm x_added bn_done "
                 "mv_done var_ready std_ready rstd_ready y_ready yT_mm yT_copied lg_mm logit_ready step gap_ready "
                 "ex_ready hots_ready cum_mm comb_ready wd_in wdh_ready wdl_ready h_mm h_done hidh_ready hidl_ready "
                 "e_mm acc_step sum_done out_in").split()
        s = {name: sem(name) for name in names}
        block = ctx.enter_context(nc.Block())

        def chunk(ap, c):
            return ap[:, CT * c:CT * (c + 1), :].rearrange("p i t -> p (i t)")

        def tile(i):
            return bass.ds(i, 1) if not isinstance(i, int) else slice(i, i + 1)

        @block.sync
        def _(sp):
            sp.dma_start(wd[:, :, :], wd_dram).then_inc(s["wd_in"], 16)
            ov = out_dram.rearrange("(i two) t d -> two t i d", two=2)
            for c in range(NC):
                sp.wait_ge(s["sum_done"], CT * (c + 1))
                at = slice(CT * c, CT * (c + 1))
                sp.dma_start(ov[0][:, at, :], acc[0:T, at, :]).then_inc(s["out_in"], 16)
                sp.dma_start(ov[1][:, at, :], acc[HALF:HALF + T, at, :]).then_inc(s["out_in"], 16)
            sp.wait_ge(s["out_in"], 16 * 2 * NC)

        @block.gpsimd
        def _(pool):
            for c in range(NC):
                pool.wait_ge(s["bias_copied"], 1)
                at = slice(CT * c, CT * (c + 1))
                nc.gpsimd.tensor_tensor(xres[:, at, :], xres[:, at, :], mid(bias[:, :], CT), ALU.add)\
                    .then_inc(s["bias_added"], 1)
            for f in range(2):
                pool.wait_ge(s["wdh_ready"], f + 1)
                nc.gpsimd.tensor_tensor(wdl[:, f, :], wd[:, f, :], wdh[:, f, :].bitcast(F32), ALU.subtract)\
                    .then_inc(s["wdl_ready"], 1)

            def low(i, u):
                pool.wait_ge(s["hidh_ready"], i + 1)
                wait(pool, s["e_mm"], 2 * (i - 1))
                nc.gpsimd.tensor_tensor(hidl[:, u, :, :], hid[:, :, tile(i), :].rearrange("p f i t -> p (f i) t"),
                                        hidh[:, u, :, :].bitcast(F32), ALU.subtract).then_inc(s["hidl_ready"], 1)

            def output(i, u):
                pool.wait_ge(s["acc_step"], NE * (i + 1))
                a = acc[:, tile(i), :].rearrange("p i d -> p (i d)")
                nc.gpsimd.tensor_tensor(a, a, odd_acc[:, u, :], ALU.add).then_inc(s["sum_done"], 1)

            for i in range(2):
                low(i, i)
            with pool.Fori(0, NT // 2 - 1) as it:
                for u in range(2):
                    low(2 * it + u + 2, u)
                    output(2 * it + u, u)
            for i in range(NT - 2, NT):
                output(i, i % 2)

        @block.scalar
        def _(act):
            for c in range(NC):
                act.wait_ge(s["oT_mm"], c + 1)
                nc.scalar.activation(chunk(oT, c), bank[c][:, :], ACT.Copy).then_inc(s["oT_copied"], 1)
                if c == 1:
                    act.wait_ge(s["bias_mm"], 1)
                    nc.scalar.activation(bias[:, :], bank[7][:, 128:256], ACT.Copy).then_inc(s["bias_copied"], 1)
            act.wait_ge(s["wd_in"], 16)
            for f in range(2):
                nc.scalar.activation(wdh[:, f, :], wd[:, f, :], ACT.Copy).then_inc(s["wdh_ready"], 1)
            act.wait_ge(s["var_ready"], 1)
            nc.scalar.activation(std[:, 1, :], std[:, 0, :], ACT.Sqrt).then_inc(s["std_ready"], 1)
            for c in range(NC):
                act.wait_ge(s["yT_mm"], c + 1)
                nc.scalar.activation(chunk(yT, c), bank[c][:, :], ACT.Copy).then_inc(s["yT_copied"], 1)
            act.wait_ge(s["gap_ready"], 1)
            nc.scalar.activation(ex[:, :, :], ex[:, :, :], ACT.Exp)
            nc.scalar.activation(gate[:, 1, :], gate[:, 0, :], ACT.Exp).then_inc(s["ex_ready"], 1)
            for k in range(2 * NC):
                c, f = k // 2, k % 2
                act.wait_ge(s["h_mm"], k + 1)
                nc.scalar.activation(chunk(hid[:, f, :, :], c), H_BANK[k][:, :], ACT.Silu).then_inc(s["h_done"], 1)

            def high(i, u):
                wait(act, s["e_mm"], 2 * (i - 1))
                nc.scalar.activation(hidh[:, u, :, :], hid[:, :, tile(i), :].rearrange("p f i t -> p (f i) t"),
                                     ACT.Copy).then_inc(s["hidh_ready"], 1)

            act.wait_ge(s["h_done"], 2 * NC)
            for i in range(2):
                high(i, i)
            with act.Fori(1, NT // 2) as it:
                for u in range(2):
                    high(2 * it + u, u)

        @block.tensor
        def _(pe):
            nc.tensor.matmul(bank[7][0:1, 0:D], w("bv"), w("xwo"), start=True, stop=True).then_inc(s["brow_mm"], 1)
            for c in range(NC):
                for j in range(CT):
                    ins = nc.tensor.transpose(bank[c][:, 128 * j:128 * j + 128], oall[:, CT * c + j, :], ident)
                ins.then_inc(s["oT_mm"], 1)
                if c == 1:
                    pe.wait_ge(s["ones_ready"], 1)
                    pe.wait_ge(s["brow_ready"], 1)
                    nc.tensor.matmul(bank[7][:, 128:256], ones[0:1, :], brow[0:1, :], start=True, stop=True)\
                        .then_inc(s["bias_mm"], 1)
            for c in range(NC):
                pe.wait_ge(s["oT_copied"], c + 1)
                if c == 3:
                    pe.wait_ge(s["x_added"], 1)
                for j in range(CT):
                    ins = nc.tensor.matmul(O_BANK[c][:, 128 * j:128 * j + 128], oT[:, CT * c + j, :], w("xwo"),
                                           start=True, stop=True)
                ins.then_inc(s["o_mm"], 1)

            def logits(c):
                pe.wait_ge(s["yT_copied"], c + 1)
                if c >= 2:
                    pe.wait_ge(s["logit_ready"], c - 1)
                for i in range(CT):
                    ins = nc.tensor.matmul(bank[6 + c % 2][:, NE * i:NE * i + NE], yT[:, CT * c + i, :], w("wr"),
                                           start=True, stop=True)
                ins.then_inc(s["lg_mm"], 1)

            for c in range(NC):
                pe.wait_ge(s["y_ready"], c + 1)
                for j in range(CT):
                    ins = nc.tensor.transpose(bank[c][:, 128 * j:128 * j + 128], y[:, CT * c + j, :], ident)
                ins.then_inc(s["yT_mm"], 1)
                if c > 0:
                    logits(c - 1)
            logits(NC - 1)

            def hidden(k):
                c, f = k // 2, k % 2
                wait(pe, s["h_done"], k - 3)
                nc.tensor.matmul(H_BANK[k][:, :], w("wg")[:, 128 * f:128 * f + 128], chunk(yT, c),
                                 start=True, stop=True).then_inc(s["h_mm"], 1)

            for k in range(2):
                hidden(k)
            pe.wait_ge(s["hots_ready"], 1)
            hots = hot[:, 2, :, :].rearrange("p i e -> p (i e)")
            nc.tensor.matmul(bank[0][:, 0:NT * NE], w("tri"), hots, start=True, stop=True)
            nc.tensor.matmul(bank[1][:, 0:NT * NE], ones[:, :], hots, start=True, stop=True).then_inc(s["cum_mm"], 1)
            for k in range(2, 2 * NC):
                hidden(k)
            pe.wait_ge(s["wdl_ready"], 2)

            def experts(i, u):
                pe.wait_ge(s["hidl_ready"], i + 1)
                wait(pe, s["acc_step"], NE * (i - 1))
                for c in range(2):
                    cols = slice(512 * c, 512 * c + 512)
                    for f in range(2):
                        high, lows = hidh[:, u, f, :], hidl[:, u, f, :]
                        nc.tensor.matmul(E_BANK[u][c][:, :], high, wdh[:, f, cols], start=(f == 0), stop=False)
                        nc.tensor.matmul(E_BANK[u][c][:, :], high, wdl[:, f, cols], start=False, stop=False)
                        ins = nc.tensor.matmul(E_BANK[u][c][:, :], lows, wdh[:, f, cols], start=False, stop=(f == 1))
                    ins.then_inc(s["e_mm"], 1)

            for i in range(2):
                experts(i, i)
            with pe.Fori(1, NT // 2) as it:
                for u in range(2):
                    experts(2 * it + u, u)

        @block.vector
        def _(dve):
            nc.vector.memset(ones[:, :], 1.0).then_inc(s["ones_ready"], 1)
            dve.wait_ge(s["brow_mm"], 1)
            nc.vector.tensor_tensor(brow[0:1, :], bank[7][0:1, 0:D], w("bo")[0:1, :], ALU.add)\
                .then_inc(s["brow_ready"], 1)
            for c in range(NC):
                dve.wait_ge(s["o_mm"], c + 1)
                dve.wait_ge(s["bias_added"], c + 1)
                nc.vector.tensor_tensor(chunk(xres, c), chunk(xres, c), O_BANK[c][:, :], ALU.add)\
                    .then_inc(s["x_added"], 1)
                dve.wait_ge(s["x_added"], c + 1)
                for i in range(CT * c, CT * (c + 1)):
                    ins = nc.vector.bn_stats(bn[:, i, :], xres[:, i, :])
                ins.then_inc(s["bn_done"], 1)
            dve.wait_ge(s["bn_done"], NC)
            for i in range(NT):
                ins = nc.vector.bn_aggr(mv[:, i, :], bn[:, i, :])
            ins.then_inc(s["mv_done"], 1)
            dve.wait_ge(s["mv_done"], 1)
            nc.vector.tensor_scalar(std[:, 0, :], mv[:, :, 1], EPS, None, ALU.add).then_inc(s["var_ready"], 1)
            dve.wait_ge(s["std_ready"], 1)
            nc.vector.reciprocal(std[:, 2, :], std[:, 1, :]).then_inc(s["rstd_ready"], 1)
            dve.wait_ge(s["rstd_ready"], 1)
            for i in range(NT):
                ins = nc.vector.tensor_scalar(y[:, i, :], xres[:, i, :], mv[:, i, 0:1], std[:, 2, i:i + 1],
                                              ALU.subtract, ALU.mult)
                if i % CT == CT - 1:
                    ins.then_inc(s["y_ready"], 1)

            n = [0]

            def step(ins):
                n[0] += 1
                ins.then_inc(s["step"], 1)
                dve.wait_ge(s["step"], n[0])

            for c in range(NC):
                dve.wait_ge(s["lg_mm"], c + 1)
                nc.vector.tensor_copy(chunk(logit, c), bank[6 + c % 2][:, 0:CT * NE])\
                    .then_inc(s["logit_ready"], 1)
                dve.wait_ge(s["logit_ready"], c + 1)
                for i in range(CT * c, CT * (c + 1)):
                    ins = nc.vector.max(top[:, i, :], logit[:, i, :])
            step(ins)
            nc.vector.tensor_tensor(ex[:, :, :], logit[:, :, :], top[:, :, 0:1].broadcast_to([128, NT, NE]),
                                    ALU.subtract)
            nc.vector.tensor_tensor(gate[:, 0, :].unsqueeze(2), top[:, :, 1:2], top[:, :, 0:1], ALU.subtract)\
                .then_inc(s["gap_ready"], 1)
            for i in range(NT):
                ins = nc.vector.max_index(topi[:, i, :], top[:, i, :], logit[:, i, :])
            step(ins)
            step(nc.vector.tensor_copy(topf[:, :, :], topi[:, :, :]))
            for c in range(2):
                ins = nc.vector.tensor_tensor(hot[:, c, :, :], mid(w("iota"), NT),
                                              topf[:, :, c:c + 1].broadcast_to([128, NT, NE]), ALU.is_equal)
            step(ins)
            step(nc.vector.tensor_tensor(hot[:, 2, :, :], hot[:, 0, :, :], hot[:, 1, :, :], ALU.add))
            nc.vector.tensor_scalar(hot[:, 2, :, :], hot[:, 2, :, :], w("valid"), None, ALU.mult)\
                .then_inc(s["hots_ready"], 1)
            nc.vector.memset(off[:, 0, 0:1, :], 0.0)
            dve.wait_ge(s["ex_ready"], 1)
            step(nc.vector.tensor_reduce(den[:, 0, :], ex[:, :, :], AX.X, ALU.add))
            step(nc.vector.reciprocal(gate[:, 0, :], den[:, 0, :]))
            step(nc.vector.tensor_tensor(gate[:, 1, :], gate[:, 1, :], gate[:, 0, :], ALU.mult))
            dve.wait_ge(s["cum_mm"], 1)
            tot = bank[1][:, 0:NT * NE].rearrange("p (i e) -> p i e", e=NE)
            step(nc.vector.tensor_copy(off[:, 0, 1:NT, :], tot[:, 0:NT - 1, :]))
            for k in range(4):
                src, dst, d = off[:, k % 2, :, :], off[:, (k + 1) % 2, :, :], 2 ** k
                nc.vector.tensor_copy(dst[:, 0:d, :], src[:, 0:d, :])
                step(nc.vector.tensor_tensor(dst[:, d:NT, :], src[:, d:NT, :], src[:, 0:NT - d, :], ALU.add))
            step(nc.vector.tensor_tensor(cum[:, :, :], bank[0][:, 0:NT * NE].rearrange("p (i e) -> p i e", e=NE),
                                         off[:, 0, :, :], ALU.add))
            for c in range(2):
                ins = nc.vector.scalar_tensor_tensor(out=kept[:, c, :, :], in0=cum[:, :, :], scalar=float(CAPACITY),
                                                     in1=hot[:, c, :, :], op0=ALU.is_le, op1=ALU.mult)
            step(ins)
            step(nc.vector.tensor_reduce(keep[:, :, :], kept[:, :, :, :], AX.X, ALU.add))
            step(nc.vector.tensor_tensor(gate[:, :, :], gate[:, :, :], keep[:, :, :], ALU.mult))
            step(nc.vector.tensor_tensor(den[:, 1, :], gate[:, 0, :], gate[:, 1, :], ALU.add))
            step(nc.vector.tensor_scalar(den[:, 1, :], den[:, 1, :], 1e-6, None, ALU.add))
            step(nc.vector.reciprocal(den[:, 2, :], den[:, 1, :]))
            step(nc.vector.tensor_tensor(gate[:, :, :], gate[:, :, :], mid(den[:, 2, :], 2), ALU.mult))
            step(nc.vector.tensor_tensor(kept[:, :, :, :], hot[:, 0:2, :, :], last(gate[:, :, :], NE), ALU.mult))
            nc.vector.tensor_tensor(comb[:, :, :], kept[:, 0, :, :], kept[:, 1, :, :], ALU.add)\
                .then_inc(s["comb_ready"], 1)
            dve.wait_ge(s["comb_ready"], 1)

            def accumulate(i, u):
                for e in range(NE):
                    if e % 4 == 0:
                        dve.wait_ge(s["e_mm"], 2 * i + e // 4 + 1)
                    product = E_BANK[u][e // 4][:, 128 * (e % 4):128 * (e % 4) + 128]
                    weight = comb[:, tile(i), e:e + 1].rearrange("p i e -> p (i e)")
                    total = acc[:, tile(i), :].rearrange("p i d -> p (i d)") if e % 2 == 0 else odd_acc[:, u, :]
                    if e == 1:
                        wait(dve, s["sum_done"], i - 1)
                        ins = nc.vector.tensor_scalar(total, product, weight, None, ALU.mult)
                    else:
                        if e >= 2:
                            dve.wait_ge(s["acc_step"], NE * i + e - 1)
                        start = xres[:, tile(i), :].rearrange("p i d -> p (i d)") if e == 0 else total
                        ins = nc.vector.scalar_tensor_tensor(out=total, in0=product, scalar=weight, in1=start,
                                                             op0=ALU.mult, op1=ALU.add)
                    ins.then_inc(s["acc_step"], 1)

            for i in range(2):
                accumulate(i, i)
            with dve.Fori(1, NT // 2) as it:
                for u in range(2):
                    accumulate(2 * it + u, u)


def build(nc, x, ctxT, rot, packed, wd, out):
    with ExitStack() as ctx:
        sb = lambda name, shape, dt=F32: ctx.enter_context(nc.sbuf_tensor(name, shape, dt))
        xres = sb("xres", [128, NT, D])
        oall = sb("oall", [128, NT, D])
        pack = sb("pack", [128, PACK_N])
        with ExitStack() as attention:
            sb = lambda name, shape, dt=F32: attention.enter_context(nc.sbuf_tensor(name, shape, dt))
            qh = sb("qh", [128, B, T])
            q3 = sb("q3", [96, 4, B, T])
            cosk = sb("cosk", [128, S])
            sink = sb("sink", [128, S])
            cx = sb("cx", [128, 2, S])
            kst = sb("kst", [128, 2, 4, S], F32R)
            low = sb("low", [128, B * T])
            shared = {name: attention.enter_context(nc.semaphore(name)) for name in ("rot_in", "ctx_in0", "ctx_in1")}
            build_self_attention(nc, x, packed, ctxT, rot, pack, xres, oall, qh, cx, cosk, sink, kst, low, shared)
            build_cross_attention(nc, ctxT, pack, qh, q3, oall, cx, cosk, sink, kst, low, shared)
        build_experts(nc, pack, wd, xres, oall, out)


def kernel(x, ctx_1024, L0_attn_Wq, L0_attn_Wk, L0_attn_Wv, L0_attn_Wo, L0_xattn_wq, L0_xattn_bq, L0_xattn_wk,
           L0_xattn_bk, L0_xattn_wv, L0_xattn_bv, L0_xattn_wo, L0_xattn_bo, L0_ffn_w_router, L0_ffn_w_gate,
           L0_ffn_w_down):
    import numpy as np
    import concourse.bacc as bacc
    from concourse.bass_utils import run_bass_kernel_spmd as run

    split = np.array([DH * h + 2 * f + odd for odd in range(2) for h in range(H) for f in range(DH // 2)])

    def tables(length, inverse, factor):
        f32 = np.float32
        base = (np.arange(0, DH, 2, dtype=f32) + f32(0.4 * DH)) / f32(1.4 * DH)
        low = -length // 2
        power = np.arange(low, length + low, dtype=f32) / f32(D)
        scale = base[None, :] ** power[:, None]
        freq = (1.0 / 10000.0 ** (np.arange(DH // 2, dtype=f32) / f32(DH // 2))).astype(f32)
        ang = np.arange(length, dtype=f32)[:, None] * freq[None, :]
        if inverse:
            scale = 1.0 / scale
        cos = (np.cos(ang) * scale * factor).T.astype(f32)
        sin = (np.sin(ang) * scale * factor).T.astype(f32)
        return np.tile(cos, (2 * H, 1)), np.concatenate([np.tile(sin, (H, 1)), -np.tile(sin, (H, 1))])

    cosk, sink = tables(S, True, np.float32(1.0))
    cosq, sinq = tables(T, False, np.float32(DH ** -0.5))
    p = np.arange(128)
    c = {
        "ident": np.eye(128),
        "causal": np.where((np.arange(T)[None, :] > (p % HALF)[:, None]) & ((p % HALF) < T)[:, None], -1e30, 0.0),
        "mask_nat": (p // DH)[:, None] == np.arange(H)[None, :],
        "mask_split": ((p % 64) // 4)[:, None] == np.arange(H)[None, :],
        "mask_stack": ((p % 16) // 4)[:, None] == np.arange(HG)[None, :],
        "mask_m": p[:, None] == np.arange(NG)[None, :],
        "tri": p[:, None] <= p[None, :],
        "valid": ((p % HALF) < T)[:, None],
        "iota": np.broadcast_to(np.arange(NE), (128, NE)),
        "cosq": cosq, "sinq": sinq,
    }
    c = {k: np.asarray(a).astype(np.float32) for k, a in c.items()}
    a = {k: np.asarray(v) for k, v in dict(
        Wq=L0_attn_Wq, Wk=L0_attn_Wk, Wv=L0_attn_Wv, Wo=L0_attn_Wo, xwv=L0_xattn_wv, xwo=L0_xattn_wo,
        wr=L0_ffn_w_router, wg=L0_ffn_w_gate).items()}
    c.update({k: v.T for k, v in a.items()})
    c["xwq"] = np.asarray(L0_xattn_wq).T[:, split]
    c["xwk"] = np.asarray(L0_xattn_wk).T[:, split]
    c["bq"] = np.asarray(L0_xattn_bq)[split][:, None]
    c["bk"] = np.asarray(L0_xattn_bk)[split][:, None]
    c["bv"] = np.asarray(L0_xattn_bv)[:, None]
    c["bo"] = np.broadcast_to(np.asarray(L0_xattn_bo)[None, :], (128, D))
    wd = np.asarray(L0_ffn_w_down).transpose(2, 0, 1).reshape(2, 128, NE * D).transpose(1, 0, 2)
    packed = np.ascontiguousarray(np.concatenate([c[name] for name, _ in PACK], axis=1))

    arrays = {
        "x": np.ascontiguousarray(np.asarray(x)),
        "ctxT": np.ascontiguousarray(np.asarray(ctx_1024).transpose(0, 2, 1)),
        "rot": np.ascontiguousarray(np.stack([cosk, sink])),
        "packed": packed,
        "wd": np.ascontiguousarray(wd),
    }
    nc = bacc.Bacc("TRN2", target_bir_lowering=False, num_devices=1)
    args = [nc.dram_tensor(k, v.shape, mybir.dt.from_np(v.dtype), kind="ExternalInput").ap()
            for k, v in arrays.items()]
    out = nc.dram_tensor("out", (B, T, D), F32, kind="ExternalOutput").ap()
    build(nc, *args, out)
    r = run(nc, [arrays], core_ids=[0])
    return r.results[0]["out"]
```
